# Optimizing a Trainium2 kernel written in Bass

```python
import numpy as np
import jax
import jax.numpy as jnp

def _softmax(x, axis=-1):
    return jax.nn.softmax(x, axis=axis)

def _gelu(x):
    return jax.nn.gelu(x, approximate=True)

def _silu(x):
    return jax.nn.silu(x)

def _sigmoid(x):
    return jax.nn.sigmoid(x)

def _layernorm(x, axis=-1, eps=1e-05):
    m = jnp.mean(x, axis=axis, keepdims=True)
    v = jnp.var(x, axis=axis, keepdims=True)
    return (x - m) / jnp.sqrt(v + eps)

def _scatter_add(tgt, idx, src, axis=0):
    return tgt.at[idx].add(src)

def _segment_sum(src, seg, n):
    return jax.ops.segment_sum(src, seg, n)
kernel_name = 'mk_adaln_d1_jaxref_r4_b4c9d0'

def setup_inputs(seed: int=0):
    np.random.seed(seed)
    _w = jnp.asarray

    def _L0_attn_setup():
        import jax, jax.numpy as jnp
        import numpy as np
        B, S, D = (2, 512, 256)
        H = 16
        HD = D // H
        WINDOW = 128
        key = jax.random.key(seed)
        ks = jax.random.split(key, 9)
        sd = 1.0 / np.sqrt(D)
        return {'x': jax.random.normal(ks[0], (B, S, D), dtype=jnp.float32), 'Wq': jax.random.normal(ks[1], (D, D), dtype=jnp.float32) * sd, 'bq': jnp.zeros((D,), dtype=jnp.float32), 'Wk': jax.random.normal(ks[2], (D, D), dtype=jnp.float32) * sd, 'bk': jnp.zeros((D,), dtype=jnp.float32), 'Wv': jax.random.normal(ks[3], (D, D), dtype=jnp.float32) * sd, 'bv': jnp.zeros((D,), dtype=jnp.float32), 'Wo': jax.random.normal(ks[4], (D, D), dtype=jnp.float32) * sd, 'bo': jnp.zeros((D,), dtype=jnp.float32)}
    _L0_attn_in = _L0_attn_setup()

    def _L0_ffn_setup():
        import jax, jax.numpy as jnp
        import numpy as np
        D_MODEL = 256
        D_FF = 1024
        NUM_EXPERTS = 8
        TOP_K = 2
        SEQ = 256
        BATCH = 2
        key = jax.random.key(seed)
        ks = jax.random.split(key, 7)
        s = 0.02
        x = jax.random.normal(ks[0], (SEQ, BATCH, D_MODEL), dtype=jnp.float32)
        gate_w = jax.random.normal(ks[1], (D_MODEL, NUM_EXPERTS), dtype=jnp.float32) * s
        gate_b = jnp.zeros((NUM_EXPERTS,), dtype=jnp.float32)
        W1 = jax.random.normal(ks[2], (NUM_EXPERTS, D_MODEL, D_FF), dtype=jnp.float32) * s
        b1 = jnp.zeros((NUM_EXPERTS, D_FF), dtype=jnp.float32)
        W2 = jax.random.normal(ks[3], (NUM_EXPERTS, D_FF, D_MODEL), dtype=jnp.float32) * s
        b2 = jnp.zeros((NUM_EXPERTS, D_MODEL), dtype=jnp.float32)
        return {'x': x, 'gate_w': gate_w, 'gate_b': gate_b, 'W1': W1, 'b1': b1, 'W2': W2, 'b2': b2}
    _L0_ffn_in = _L0_ffn_setup()
    _L0_c = _w((lambda *s: np.random.randn(*s).astype(np.float32) * 0.05)(1, 256))
    _L0_wmod = _w((lambda *s: np.random.randn(*s).astype(np.float32) * 0.05)(256, 6 * 256) * 256 ** (-0.5))
    _d = {'L0_attn_x': _L0_attn_in['x'], 'L0_attn_Wq': _L0_attn_in['Wq'], 'L0_attn_bq': _L0_attn_in['bq'], 'L0_attn_Wk': _L0_attn_in['Wk'], 'L0_attn_bk': _L0_attn_in['bk'], 'L0_attn_Wv': _L0_attn_in['Wv'], 'L0_attn_bv': _L0_attn_in['bv'], 'L0_attn_Wo': _L0_attn_in['Wo'], 'L0_attn_bo': _L0_attn_in['bo'], 'L0_ffn_gate_w': _L0_ffn_in['gate_w'], 'L0_ffn_gate_b': _L0_ffn_in['gate_b'], 'L0_ffn_W1': _L0_ffn_in['W1'], 'L0_ffn_b1': _L0_ffn_in['b1'], 'L0_ffn_W2': _L0_ffn_in['W2'], 'L0_ffn_b2': _L0_ffn_in['b2'], 'L0_c': _L0_c, 'L0_wmod': _L0_wmod}
    _x0 = _d['L0_attn_x']
    _d['L0_attn_x'] = jax.random.normal(jax.random.fold_in(jax.random.key(seed), 1), (1, 4096, 256), dtype=_x0.dtype)
    del _x0
    return _d

def reference(L0_attn_x, L0_attn_Wq, L0_attn_bq, L0_attn_Wk, L0_attn_bk, L0_attn_Wv, L0_attn_bv, L0_attn_Wo, L0_attn_bo, L0_ffn_gate_w, L0_ffn_gate_b, L0_ffn_W1, L0_ffn_b1, L0_ffn_W2, L0_ffn_b2, L0_c, L0_wmod):

    def _L0_attn_ref(x, Wq, bq, Wk, bk, Wv, bv, Wo, bo):
        import jax, jax.numpy as jnp
        import numpy as np
        B, S, D = (2, 512, 256)
        H = 16
        HD = D // H
        WINDOW = 128
        b, s, d = x.shape
        q = (x @ Wq + bq).reshape(b, s, H, HD).transpose(0, 2, 1, 3)
        k = (x @ Wk + bk).reshape(b, s, H, HD).transpose(0, 2, 1, 3)
        v = (x @ Wv + bv).reshape(b, s, H, HD).transpose(0, 2, 1, 3)
        rows = jnp.arange(s)[:, None]
        cols = jnp.arange(s)[None, :]
        mask = cols <= rows + WINDOW
        scores = jnp.einsum('bhqd,bhkd->bhqk', q, k) / jnp.sqrt(jnp.float32(HD))
        scores = jnp.where(mask[None, None], scores, -jnp.inf)
        attn = jax.nn.softmax(scores, axis=-1)
        out = jnp.einsum('bhqk,bhkd->bhqd', attn, v)
        out = out.transpose(0, 2, 1, 3).reshape(b, s, d)
        return out @ Wo + bo

    def _L0_ffn_ref(x, gate_w, gate_b, W1, b1, W2, b2):
        import jax, jax.numpy as jnp
        import numpy as np
        D_MODEL = 256
        D_FF = 1024
        NUM_EXPERTS = 8
        TOP_K = 2
        SEQ = 256
        BATCH = 2
        S, B, D = x.shape
        x_flat = x.reshape(-1, D)
        scores = x_flat @ gate_w + gate_b
        topk_vals, topk_idx = jax.lax.top_k(scores, TOP_K)
        topk_probs = jax.nn.softmax(topk_vals, axis=-1)
        one_hot = jax.nn.one_hot(topk_idx, NUM_EXPERTS, dtype=x.dtype)
        combine = jnp.einsum('tk,tke->te', topk_probs, one_hot)
        h = jax.nn.relu(jnp.einsum('td,edf->etf', x_flat, W1) + b1[:, None, :])
        y = jnp.einsum('etf,efd->etd', h, W2) + b2[:, None, :]
        out = jnp.einsum('te,etd->td', combine, y)
        return out.reshape(S, B, D)
    x = L0_attn_x
    mod = (_silu(L0_c) @ L0_wmod).reshape(L0_c.shape[0], 6, 1, -1)
    sa, ca, ga, sb, cb, gb = (mod[:, 0], mod[:, 1], mod[:, 2], mod[:, 3], mod[:, 4], mod[:, 5])
    ga = (2 * (ga >= 0) - 1) * jnp.maximum(jnp.abs(ga), 0.25)
    gb = (2 * (gb >= 0) - 1) * jnp.maximum(jnp.abs(gb), 0.25)
    h = _layernorm(x, axis=-1) * (1 + ca) + sa
    x = x + ga * _L0_attn_ref(h, L0_attn_Wq, L0_attn_bq, L0_attn_Wk, L0_attn_bk, L0_attn_Wv, L0_attn_bv, L0_attn_Wo, L0_attn_bo)
    h = _layernorm(x, axis=-1) * (1 + cb) + sb
    x = x + gb * _L0_ffn_ref(h, L0_ffn_gate_w, L0_ffn_gate_b, L0_ffn_W1, L0_ffn_b1, L0_ffn_W2, L0_ffn_b2)
    return x

_drawn_inputs = setup_inputs


def setup_inputs(seed=0):
    import zlib

    import numpy as np

    out = dict(_drawn_inputs(seed))
    spreads = {'L0_attn_bq': (0.0, 0.8),
     'L0_attn_bk': (0.0, 0.8),
     'L0_attn_bv': (0.0, 0.309),
     'L0_attn_bo': (0.0, 0.324),
     'L0_ffn_gate_b': (0.0, 0.419),
     'L0_ffn_b1': (0.0, 0.8),
     'L0_ffn_b2': (0.0, 0.45)}
    factors = {'L0_attn_Wq': 3.056, 'L0_attn_Wk': 3.018, 'L0_attn_Wv': 2.85}
    for name, (base, spread) in spreads.items():
        noise = np.random.default_rng([zlib.crc32(name.encode()), seed]).standard_normal(out[name].shape)
        drawn = base * np.exp(spread * noise) if base else spread * noise
        out[name] = jnp.asarray(drawn.astype(out[name].dtype))
    for name, factor in factors.items():
        out[name] = (out[name] * factor).astype(out[name].dtype)
    return out
```

```python
from contextlib import ExitStack

import concourse.bass as bass
from concourse import mybir

ALU = mybir.AluOpType
ACT = mybir.ActivationFunctionType
AX = mybir.AxisListType
F32 = mybir.dt.float32
BF16 = mybir.dt.bfloat16
U32 = mybir.dt.uint32
I32 = mybir.dt.int32

P = 128
S = 4096
D = 256
KD = D // P
H = 16
HD = D // H
GH = 4
G = H // GH
NT = S // P
C = 512
NC = S // C
CB = C // P
TERMS = 6
ROWS = TERMS * HD
STACK = ROWS + 3
E = 8
FF = 1024 // P
TILES = (2 * S + E * (P - 1)) // P
MASKED = -3.0e38
EPS = 1e-5
LOADS = 4
STORES = TERMS * KD
K_TERM = [0, 0, 0, 1, 1, 2]
Q_TERM = [0, 1, 2, 0, 1, 0]


class Tally:

    def __init__(self, sem, base=0):
        self.sem, self.base, self.n = sem, base, 0

    def inc(self, ins):
        self.n += 1
        return ins.then_inc(self.sem, 1)

    def wait(self, eng):
        eng.wait_ge(self.sem, self.base + self.n)


def attention_inputs(nc, dram, keep):
    with ExitStack() as ctx:
        def sb(name, shape, dt):
            return ctx.enter_context(nc.sbuf_tensor(name, shape, dt))

        def psum(name, shape, dt):
            return ctx.enter_context(nc.psum_tensor(name, shape, dt))

        def sem(name):
            return ctx.enter_context(nc.semaphore(name))

        ident, gates, v, mod_cols = keep["ident"], keep["gates"], keep["v"], keep["mod_cols"]
        x = sb("x_rows", [P, NT, D], F32)
        xn = sb("xn", [P, 2, CB, D], F32)
        ccol = sb("ccol", [P, KD], F32)
        silu = sb("silu", [P, 4, KD], F32)
        silu_rows = sb("silu_rows", [P, KD, P], F32)
        wmod = sb("wmod", [P, KD, 6 * D], F32)
        wq = sb("wq", [P, KD, D], F32)
        wk = sb("wk", [P, KD, D], F32)
        wv = sb("wv", [P, KD, D], F32)
        bk = sb("bk", [P, KD], F32)
        bq = sb("bq", [P, KD], F32)
        bq_scaled = sb("bq_scaled", [P, KD], F32)
        bv_rows = sb("bv_rows", [P, D], F32)
        mod_raw = sb("mod_raw", [P, 8], F32)
        gate_raw = sb("gate_raw", [P, 2, D], F32)
        gate_sign = sb("gate_sign", [P, 2, D], F32)
        gate_abs = sb("gate_abs", [P, 2, D], F32)
        gate_size = sb("gate_size", [P, 2, D], F32)
        stats = sb("stats", [P, NT, 6], F32)
        mean2 = sb("mean2", [P, NT], F32)
        dev = sb("dev", [P, NT], F32)
        dev2 = sb("dev2", [P, NT], F32)
        m2 = sb("m2", [P, NT], F32)
        m2d = sb("m2d", [P, NT], F32)
        var = sb("var", [P, NT], F32)
        shift = sb("shift", [P, NT], F32)
        eps = sb("eps", [P, 1], F32)
        std = sb("std", [P, NT], F32)
        rstd = sb("rstd", [P, NT], F32)
        hT = sb("hT", [P, 2, KD, C], F32)
        kf = sb("kf", [P, KD, C], F32)
        qf = sb("qf", [P, KD, C], F32)
        kparts = sb("kparts", [P, 2, 3, KD, C], BF16)
        qparts = sb("qparts", [P, 2, 3, KD, C], BF16)
        ones = sb("ones", [P, P], F32)
        ones_rows = sb("ones_rows", [3 * H, S], BF16)

        ps_turn = psum("ps_turn", [P, KD, C], F32)
        ps_k = psum("ps_k", [P, KD, C], F32)
        ps_q = psum("ps_q", [P, KD, C], F32)
        ps_v = psum("ps_v", [P, CB, D], F32)

        x_in = [sem(f"x_in_{n}") for n in range(LOADS)]
        mod_in = sem("mod_in")
        w_in = sem("w_in")
        dve_step = sem("dve_step")
        act_step = sem("act_step")
        pool_step = sem("pool_step")
        c_exp = sem("c_exp")
        silu_ready = sem("silu_ready")
        rows_ready = sem("rows_ready")
        mod_ready = sem("mod_ready")
        cols_ready = sem("cols_ready")
        var_ready = sem("var_ready")
        std_ready = sem("std_ready")
        xn_ready = sem("xn_ready")
        turned = sem("turned")
        h_ready = sem("h_ready")
        k_ready = sem("k_ready")
        v_ready = sem("v_ready")
        kq_kept = sem("kq_kept")
        parts_ready = sem("parts_ready")
        v_kept = sem("v_kept")
        stats_ready = sem("stats_ready")
        norm_ready = sem("norm_ready")
        ones_stored = sem("ones_stored")
        k_stored = [sem(f"k_stored_{u}") for u in range(2)]
        q_stored = [sem(f"q_stored_{u}") for u in range(2)]

        x_v = dram["x"].rearrange("a (t p) d -> p (a t) d", p=P)
        block = ctx.enter_context(nc.Block())

        @block.sync
        def _(sp):
            sp.dma_start(ccol[:], dram["c"].rearrange("a (k p) -> p (a k)", p=P),
                         allow_slow_non_contiguous=True).then_inc(mod_in, 16)
            for n in range(LOADS):
                part = slice(n * NT // LOADS, (n + 1) * NT // LOADS)
                sp.dma_start(x[:, part, :], x_v[:, part, :]).then_inc(x_in[n], 16)
            sp.wait_ge(pool_step, 2)
            sp.dma_start(dram["k_stack"][ROWS:STACK].rearrange("r h s -> (r h) s"), ones_rows[:]).then_inc(ones_stored, 16)
            with sp.Fori(0, NC // 2) as it:
                for u in range(2):
                    for n, (parts, order, stack, kept) in enumerate(
                            ((kparts, K_TERM, "k_stack", k_stored), (qparts, Q_TERM, "q_stack", q_stored))):
                        sp.wait_ge(parts_ready, it * 4 + (2 * u + n + 3))
                        for term, part in enumerate(order):
                            for m in range(KD):
                                to = dram[stack][term * HD:(term + 1) * HD, m * 8:(m + 1) * 8,
                                                 bass.ds(it * 2 * C + u * C, C)].rearrange("d h s -> h d s")
                                sp.dma_start(to, parts[:, u, part, m, :]).then_inc(kept[u], 16)
            sp.wait_ge(ones_stored, 16)
            for u in range(2):
                sp.wait_ge(k_stored[u], 16 * STORES * (NC // 2 + 1))
                sp.wait_ge(q_stored[u], 16 * STORES * (NC // 2 + 1))

        @block.gpsimd
        def _(pool):
            nc.gpsimd.memset(ones_rows[:], 1.0).then_inc(pool_step, 1)
            nc.gpsimd.memset(ones[:], 1.0).then_inc(pool_step, 1)
            pool.wait_ge(pool_step, 2)
            nc.gpsimd.affine_select(out=keep["ident"][:], in_=ones[:], compare_op=ALU.is_equal, fill=0.0,
                                    base=0, pattern=[[-1, P]], channel_multiplier=1).then_inc(pool_step, 1)
            nc.gpsimd.affine_select(out=keep["ident_bf"][:], in_=ones[:], compare_op=ALU.is_equal, fill=0.0,
                                    base=0, pattern=[[-1, P]], channel_multiplier=1).then_inc(pool_step, 1)
            nc.gpsimd.memset(keep["mask_kq"][:], 0.0).then_inc(pool_step, 1)
            nc.gpsimd.memset(keep["mask_qk"][:], 0.0).then_inc(pool_step, 1)
            pool.wait_ge(pool_step, 6)
            nc.gpsimd.affine_select(out=keep["mask_kq"][:], in_=keep["mask_kq"][:], compare_op=ALU.is_ge, fill=MASKED,
                                    base=0, pattern=[[1, P]], channel_multiplier=-1).then_inc(pool_step, 1)
            nc.gpsimd.affine_select(out=keep["mask_qk"][:], in_=keep["mask_qk"][:], compare_op=ALU.is_ge, fill=MASKED,
                                    base=0, pattern=[[-1, P]], channel_multiplier=1).then_inc(pool_step, 1)
            pool.wait_ge(pool_step, 8)

        @block.scalar
        def _(act):
            act.dma_start(wmod[:], dram["wmod"].rearrange("(k p) n -> p k n", p=P),
                         allow_slow_non_contiguous=True).then_inc(mod_in, 16)
            for to, name in ((wk, "Wk"), (wq, "Wq"), (wv, "Wv")):
                act.dma_start(to[:], dram[name].rearrange("(k p) n -> p k n", p=P)).then_inc(w_in, 16)
            for to, name in ((bk, "bk"), (bq, "bq")):
                act.dma_start(to[:], dram[name].rearrange("(k p) -> p k", p=P),
                              allow_slow_non_contiguous=True).then_inc(w_in, 16)
            act.dma_start(bv_rows[:], dram["bv"].rearrange("(a n) -> a n", a=1).partition_broadcast(P)).then_inc(w_in, 16)
            act.wait_ge(mod_in, 32)
            nc.scalar.activation(silu[:, 0, :], ccol[:], ACT.Exp, scale=-1.0).then_inc(c_exp, 1)
            act.wait_ge(w_in, 16 * 6)
            nc.scalar.mul(bq_scaled[:], bq[:], HD ** -0.5).then_inc(act_step, 1)
            act.wait_ge(mod_ready, 2)
            nc.scalar.copy(mod_raw[:], ps_turn[:, 0, 0:8]).then_inc(act_step, 1)
            nc.scalar.copy(gate_raw[:], ps_k[:, 0, :].rearrange("p (a d) -> p a d", a=2)).then_inc(act_step, 1)
            act.wait_ge(var_ready, 1)
            nc.scalar.activation(std[:], var[:], ACT.Sqrt, bias=eps[:, 0:1]).then_inc(std_ready, 1)
            act.wait_ge(norm_ready, 1)
            act.wait_ge(cols_ready, 1)
            act.wait_ge(act_step, 3)
            act.sem_inc(h_ready, KD)
            act.sem_inc(kq_kept, 2 * KD)
            with act.Fori(0, NC // 2) as it:
                for u in range(2):
                    c = it * 2 + u
                    act.wait_ge(turned, c + 1)
                    for j in range(CB):
                        t = it * (2 * CB) + u * CB + j
                        nc.scalar.activation(xn[:, u, j, :], x[:, bass.ds(t, 1), :].rearrange("p a d -> p (a d)"),
                                             ACT.Identity, scale=rstd[:, bass.ds(t, 1)],
                                             bias=shift[:, bass.ds(t, 1)]).then_inc(xn_ready, 1)
                    act.wait_ge(v_ready, c + 1)
                    act.wait_ge(turned, c + 3)
                    for k in range(KD):
                        nc.scalar.activation(hT[:, u, k, :], ps_turn[:, k, :], ACT.Identity,
                                             scale=mod_cols[:, 2 + k:3 + k],
                                             bias=mod_cols[:, k:k + 1]).then_inc(h_ready, 1)
                    act.wait_ge(k_ready, c * 2 + 1)
                    act.wait_ge(parts_ready, c * 2 + 1)
                    for m in range(KD):
                        nc.scalar.activation(kf[:, m, :], ps_k[:, m, :], ACT.Identity,
                                             bias=bk[:, m:m + 1]).then_inc(kq_kept, 1)
                    act.wait_ge(k_ready, c * 2 + 2)
                    act.wait_ge(parts_ready, c * 2 + 2)
                    for m in range(KD):
                        nc.scalar.activation(qf[:, m, :], ps_q[:, m, :], ACT.Identity, scale=HD ** -0.5,
                                             bias=bq_scaled[:, m:m + 1]).then_inc(kq_kept, 1)

        @block.tensor
        def _(pe):
            pe.wait_ge(mod_in, 32)
            pe.wait_ge(silu_ready, 1)
            for n, start in enumerate((0, P, D, D + P, 3 * D, 3 * D + P, 4 * D, 4 * D + P)):
                for k in range(KD):
                    last = nc.tensor.matmul(ps_turn[:, 0, n:n + 1], wmod[:, k, start:start + P],
                                            silu[:, 3, k:k + 1], start=k == 0, stop=k == KD - 1)
            last.then_inc(mod_ready, 1)
            pe.wait_ge(rows_ready, KD)
            for n, start in enumerate((2 * D, 5 * D)):
                for k in range(KD):
                    last = nc.tensor.matmul(ps_k[:, 0, n * D:(n + 1) * D], silu_rows[:, k, :],
                                            wmod[:, k, start:start + D], start=k == 0, stop=k == KD - 1)
            last.then_inc(mod_ready, 1)
            pe.wait_ge(act_step, 3)
            pe.wait_ge(pool_step, 8)
            pe.wait_ge(w_in, 16 * 6)
            pe.sem_inc(turned, 2)
            pe.sem_inc(v_ready, 2)
            with pe.Fori(0, NC // 2) as it:
                for u in range(2):
                    c = it * 2 + u
                    pe.wait_ge(xn_ready, c * CB + CB)
                    pe.wait_ge(h_ready, c * KD + KD)
                    for k in range(KD):
                        for j in range(CB):
                            last = nc.tensor.transpose(ps_turn[:, k, j * P:(j + 1) * P],
                                                       xn[:, u, j, k * P:(k + 1) * P], ident[:])
                    last.then_inc(turned, 1)
                    pe.wait_ge(h_ready, c * KD + 2 * KD)
                    for n, (w, ps) in enumerate(((wk, ps_k), (wq, ps_q))):
                        pe.wait_ge(kq_kept, c * (2 * KD) + (n + 1) * KD)
                        for m in range(KD):
                            for k in range(KD):
                                last = nc.tensor.matmul(ps[:, m, :], w[:, k, m * P:(m + 1) * P], hT[:, u, k, :],
                                                        start=k == 0, stop=k == KD - 1)
                        last.then_inc(k_ready, 1)
                    pe.wait_ge(v_kept, c + 1)
                    for j in range(CB):
                        for k in range(KD):
                            last = nc.tensor.matmul(ps_v[:, j, :], hT[:, u, k, j * P:(j + 1) * P], wv[:, k, :],
                                                    start=k == 0, stop=k == KD - 1)
                    last.then_inc(v_ready, 1)

        @block.vector
        def _(dve):
            step = Tally(dve_step)
            step.inc(nc.vector.memset(eps[:], EPS))
            dve.wait_ge(c_exp, 1)
            step.inc(nc.vector.tensor_scalar_add(silu[:, 1, :], silu[:, 0, :], 1.0))
            step.wait(dve)
            step.inc(nc.vector.reciprocal(silu[:, 2, :], silu[:, 1, :]))
            step.wait(dve)
            nc.vector.tensor_tensor(silu[:, 3, :], silu[:, 2, :], ccol[:], ALU.mult).then_inc(silu_ready, 1)
            dve.wait_ge(silu_ready, 1)
            dve.wait_ge(pool_step, 2)
            for k in range(KD):
                nc.vector.tensor_scalar(silu_rows[:, k, :], ones[:], silu[:, 3, k:k + 1], None,
                                        ALU.mult).then_inc(rows_ready, 1)
            for n in range(LOADS):
                dve.wait_ge(x_in[n], 16)
                with dve.Fori(n * NT // LOADS, (n + 1) * NT // LOADS) as t:
                    nc.vector.bn_stats(stats[:, bass.ds(t, 1), :].rearrange("p a s -> p (a s)"),
                                       x[:, bass.ds(t, 1), :].rearrange("p a d -> p (a d)")).then_inc(stats_ready, 1)
            dve.wait_ge(stats_ready, NT)
            step.inc(nc.vector.tensor_tensor(mean2[:], stats[:, :, 1], stats[:, :, 4], ALU.add))
            step.inc(nc.vector.tensor_tensor(dev[:], stats[:, :, 1], stats[:, :, 4], ALU.subtract))
            step.inc(nc.vector.tensor_tensor(m2[:], stats[:, :, 2], stats[:, :, 5], ALU.add))
            step.wait(dve)
            step.inc(nc.vector.tensor_tensor(dev2[:], dev[:], dev[:], ALU.mult))
            step.inc(nc.vector.tensor_scalar(m2d[:], m2[:], 1.0 / D, None, ALU.mult))
            step.wait(dve)
            nc.vector.scalar_tensor_tensor(out=var[:], in0=dev2[:], scalar=0.25, in1=m2d[:], op0=ALU.mult,
                                           op1=ALU.add).then_inc(var_ready, 1)
            dve.wait_ge(std_ready, 1)
            step.inc(nc.vector.reciprocal(rstd[:], std[:]))
            step.wait(dve)
            nc.vector.scalar_tensor_tensor(out=shift[:], in0=mean2[:], scalar=-0.5, in1=rstd[:], op0=ALU.mult,
                                           op1=ALU.mult).then_inc(norm_ready, 1)
            dve.wait_ge(act_step, 3)
            step.inc(nc.vector.tensor_copy(mod_cols[:], mod_raw[:]))
            step.wait(dve)
            for n in (2, 6):
                step.inc(nc.vector.tensor_scalar_add(mod_cols[:, n:n + 2], mod_raw[:, n:n + 2], 1.0))
            step.wait(dve)
            step.inc(nc.vector.tensor_scalar(gate_sign[:], gate_raw[:], 0.0, 2.0, ALU.is_ge, ALU.mult))
            step.inc(nc.vector.scalar_tensor_tensor(out=gate_abs[:], in0=gate_raw[:], scalar=-1.0, in1=gate_raw[:],
                                                    op0=ALU.mult, op1=ALU.max))
            step.wait(dve)
            step.inc(nc.vector.tensor_scalar(gate_size[:], gate_abs[:], 0.25, None, ALU.max))
            step.wait(dve)
            nc.vector.scalar_tensor_tensor(out=gates[:], in0=gate_sign[:], scalar=-1.0, in1=gate_size[:],
                                           op0=ALU.add, op1=ALU.mult).then_inc(cols_ready, 1)
            dve.wait_ge(w_in, 16 * 6)
            dve.sem_inc(parts_ready, 2)
            dve.sem_inc(v_kept, 1)
            for u in range(2):
                dve.sem_inc(k_stored[u], 16 * STORES)
                dve.sem_inc(q_stored[u], 16 * STORES)
            first = step.n
            per_chunk = 6
            with dve.Fori(0, NC // 2) as it:
                for u in range(2):
                    c = it * 2 + u
                    step = Tally(dve_step, c * per_chunk + first)
                    for n, (full, parts, kept) in enumerate(((kf, kparts, k_stored), (qf, qparts, q_stored))):
                        dve.wait_ge(kq_kept, c * (2 * KD) + (2 * KD + (n + 1) * KD))
                        dve.wait_ge(kept[u], it * (16 * STORES) + 16 * STORES)
                        step.inc(nc.vector.tensor_copy(parts[:, u, 0], full[:]))
                        step.wait(dve)
                        step.inc(nc.vector.tensor_tensor(full[:], full[:], parts[:, u, 0], ALU.subtract))
                        step.wait(dve)
                        step.inc(nc.vector.tensor_copy(parts[:, u, 1], full[:]))
                        step.wait(dve)
                        nc.vector.tensor_tensor(parts[:, u, 2], full[:], parts[:, u, 1],
                                                ALU.subtract).then_inc(parts_ready, 1)
                    assert step.n == per_chunk
                    dve.wait_ge(v_ready, c + 3)
                    nc.vector.tensor_tensor(v[:, bass.ds(it * (2 * CB) + u * CB, CB), :], ps_v[:],
                                            bv_rows[:].unsqueeze(1).to_broadcast([P, CB, D]),
                                            ALU.add).then_inc(v_kept, 1)
            dve.wait_ge(v_kept, NC + 1)

def over_tiles(eng, body):
    body(0, False)
    with eng.Fori(1, NC - 1) as tile:
        body(tile, False)
    body(NC - 1, True)


def row_maxima(nc, dram, keep):
    with ExitStack() as ctx:
        def sb(name, shape, dt):
            return ctx.enter_context(nc.sbuf_tensor(name, shape, dt))

        def psum(name, shape, dt):
            return ctx.enter_context(nc.psum_tensor(name, shape, dt))

        def sem(name):
            return ctx.enter_context(nc.semaphore(name))

        ident, ident_bf, mask = keep["ident"], keep["ident_bf"], keep["mask_qk"]
        U = GH * CB
        BANKS = 4
        CUT = 5
        k_rows = sb("mx_k_rows", [ROWS, GH, S], BF16)
        q_rows = sb("mx_q_rows", [ROWS, GH, C], BF16)
        best = sb("mx_best", [P, U], F32)
        edge = sb("mx_edge", [P, GH], F32)
        chunk = sb("mx_chunk", [P, U], F32)
        neg = sb("mx_neg", [U, P], F32)
        parts = sb("mx_parts", [U, 3, P], BF16)
        ps = psum("mx_ps", [P, BANKS, C], F32)
        ps_turn = psum("mx_turn", [U, C], F32)

        k_in = sem("mx_k_in")
        q_in = sem("mx_q_in")
        scored = sem("mx_scored")
        reduced = sem("mx_reduced")
        joined = sem("mx_joined")
        turned = sem("mx_turned")
        cut = sem("mx_cut")
        stored = sem("mx_stored")
        written = sem("mx_written")

        def units_before(tile):
            return tile * (U // 2 + GH) + tile * tile * (U // 2)

        GROUP_UNITS = units_before(NC) - GH

        def joins_before(tile):
            return (tile * tile + tile)

        GROUP_JOINS = joins_before(NC) - 2

        block = ctx.enter_context(nc.Block())

        @block.sync
        def _(sp):
            sp.sem_inc(stored, 16)
            with sp.Fori(0, G) as g:
                with sp.Fori(0, NC) as tile:
                    r = g * NC + tile
                    sp.wait_ge(turned, r + 1)
                    sp.dma_start(q_rows[:], dram["q_stack"][0:ROWS, bass.ds(g * GH, GH),
                                                            bass.ds(tile * C, C)]).then_inc(q_in, 16)
                    sp.dma_start(k_rows[:], dram["k_stack"][0:ROWS, bass.ds(g * GH, GH), :]).then_inc(k_in, 16)
                    sp.wait_ge(cut, r * CUT + CUT + 1)
                    for part in range(3):
                        to = dram["q_stack"][ROWS + part, bass.ds(g * GH, GH), bass.ds(tile * C, C)]
                        sp.dma_start(to.rearrange("h (j q) -> h j q", q=P), parts[:, part, :]).then_inc(stored, 16)
                    sp.wait_ge(stored, r * 48 + 64)
                    sp.sem_inc(written, 1)

        @block.tensor
        def _(pe):
            pe.sem_inc(turned, 1)
            with pe.Fori(0, G) as g:
                def tile_scores(tile, last):
                    base = pe.snap(g * GROUP_UNITS + units_before(tile))
                    r = g * NC + tile
                    pe.wait_ge(q_in, r * 16 + 16)
                    pe.wait_ge(k_in, r * 16 + 16)
                    unit = 0
                    for h in range(GH):
                        for j in range(CB):
                            pe.wait_ge(reduced, base + (unit + 1))
                            out = ps[:, unit % BANKS, :]
                            width = min(j + 2, CB) * P
                            masked = j + 1 < CB
                            ins = nc.tensor.matmul(out[:, 0:width], q_rows[:, h, j * P:(j + 1) * P],
                                                   k_rows[:, h, bass.ds(tile * C, width)],
                                                   start=True, stop=not masked)
                            if masked:
                                ins = nc.tensor.matmul(out[:, width - P:width], ident_bf[:], mask[:],
                                                       start=False, stop=True)
                            ins.then_inc(scored, 1)
                            unit += 1
                    if not last:
                        for h in range(GH):
                            pe.wait_ge(reduced, base + (unit + 1))
                            out = ps[:, unit % BANKS, 0:P]
                            nc.tensor.matmul(out, q_rows[:, h, C - P:C],
                                             k_rows[:, h, bass.ds(tile * C + C, P)], start=True, stop=False)
                            nc.tensor.matmul(out, ident_bf[:], mask[:], start=False, stop=True).then_inc(scored, 1)
                            unit += 1
                    if not isinstance(tile, int) or tile > 0:
                        with pe.Fori(0, tile) as kc:
                            for u in range(U):
                                pe.wait_ge(reduced, base + kc * U + (unit + u + 1))
                                h, j = u // CB, u % CB
                                nc.tensor.matmul(ps[:, (unit + u) % BANKS, :], q_rows[:, h, j * P:(j + 1) * P],
                                                 k_rows[:, h, bass.ds(kc * C, C)], start=True,
                                                 stop=True).then_inc(scored, 1)
                    pe.wait_ge(joined, g * GROUP_JOINS + joins_before(tile) + tile * 2 + (0 if last else 2))
                    pe.wait_ge(cut, r * CUT + 1)
                    nc.tensor.transpose(ps_turn[:, 0:P], best[:], ident[:]).then_inc(turned, 1)

                over_tiles(pe, tile_scores)

        @block.vector
        def _(dve):
            dve.sem_inc(reduced, BANKS)
            dve.sem_inc(cut, 1)
            with dve.Fori(0, G) as g:
                def tile_maxima(tile, last):
                    base = dve.snap(g * GROUP_UNITS + units_before(tile))
                    joins = dve.snap(g * GROUP_JOINS + joins_before(tile))
                    r = g * NC + tile
                    dve.wait_ge(turned, r + 1)
                    unit = 0
                    for h in range(GH):
                        for j in range(CB):
                            dve.wait_ge(scored, base + (unit + 1))
                            width = min(j + 2, CB) * P
                            nc.vector.tensor_reduce(best[:, unit:unit + 1], ps[:, unit % BANKS, 0:width], AX.X,
                                                    ALU.max).then_inc(reduced, 1)
                            unit += 1
                    if not last:
                        for h in range(GH):
                            dve.wait_ge(scored, base + (unit + 1))
                            nc.vector.tensor_reduce(edge[:, h:h + 1], ps[:, unit % BANKS, 0:P], AX.X,
                                                    ALU.max).then_inc(reduced, 1)
                            unit += 1
                        dve.wait_ge(reduced, base + (unit + BANKS))
                        bottom = best[:].rearrange("p (h j) -> p h j", h=GH)[:, :, CB - 1]
                        nc.vector.tensor_tensor(bottom, bottom, edge[:], ALU.max).then_inc(joined, 2)
                    if not isinstance(tile, int) or tile > 0:
                        with dve.Fori(0, tile) as kc:
                            dve.wait_ge(joined, joins + kc * 2 + (0 if last else 2))
                            for u in range(U):
                                dve.wait_ge(scored, base + kc * U + (unit + u + 1))
                                nc.vector.tensor_reduce(chunk[:, u:u + 1], ps[:, (unit + u) % BANKS, :], AX.X,
                                                        ALU.max).then_inc(reduced, 1)
                            dve.wait_ge(reduced, base + kc * U + (unit + U + BANKS))
                            nc.vector.tensor_tensor(best[:], best[:], chunk[:], ALU.max).then_inc(joined, 2)
                    dve.wait_ge(turned, r + 2)
                    dve.wait_ge(stored, r * 48 + 16)
                    step = Tally(cut, r * CUT + 1)
                    step.inc(nc.vector.tensor_scalar(neg[:], ps_turn[:, 0:P], -1.0, None, ALU.mult))
                    step.wait(dve)
                    step.inc(nc.vector.tensor_copy(parts[:, 0], neg[:]))
                    step.wait(dve)
                    step.inc(nc.vector.tensor_tensor(neg[:], neg[:], parts[:, 0], ALU.subtract))
                    step.wait(dve)
                    step.inc(nc.vector.tensor_copy(parts[:, 1], neg[:]))
                    step.wait(dve)
                    step.inc(nc.vector.tensor_tensor(parts[:, 2], neg[:], parts[:, 1], ALU.subtract))
                    assert step.n == CUT

                over_tiles(dve, tile_maxima)


def attention(nc, dram, keep):
    with ExitStack() as ctx:
        def sb(name, shape, dt):
            return ctx.enter_context(nc.sbuf_tensor(name, shape, dt))

        def psum(name, shape, dt):
            return ctx.enter_context(nc.psum_tensor(name, shape, dt))

        def sem(name):
            return ctx.enter_context(nc.semaphore(name))

        ident, ident_bf, mask, v, mixed = (keep[n] for n in ("ident", "ident_bf", "mask_kq", "v", "mixed"))
        CT = 32
        RING = CB
        FAR = RING
        HALF = GH // 2
        LAG = 2

        k_rows = sb("at_k_rows", [STACK, 2 * GH * S], BF16)
        q_rows = sb("at_q_rows", [STACK, 2 * GH * C], BF16)
        probs = sb("at_probs", [P, RING + 1, GH, C], F32)
        v_now = sb("at_v_now", [P, RING + 1, GH, CT], F32)
        out_T = sb("at_out_T", [P, C], F32)
        inv = sb("at_inv", [P, CB, GH], F32)
        warm = sb("at_warm", [P, 1], F32)
        zeros = sb("at_zeros", [P, 8 * D], F32)

        ps_s = psum("at_scores", [P, 2, HALF, C], F32)
        ps_o = psum("at_out", [P, C], F32)
        ps_t = psum("at_turn", [P, CB, P], F32)

        k_in = sem("at_k_in")
        q_in = sem("at_q_in")
        ready = sem("at_ready")
        scored = sem("at_scored")
        exped = sem("at_exped")
        slot_free = sem("at_slot_free")
        q_there = sem("at_q_there")
        v_copied = sem("at_v_copied")
        pv_done = sem("at_pv_done")
        out_read = sem("at_out_read")
        turned = sem("at_turned")
        inverted = sem("at_inverted")
        normed = sem("at_normed")
        zeroed = sem("at_zeroed")
        queue_clear = sem("at_queue_clear")

        def steps_before(tile):
            return tile * tile * (CB // 2) + tile * (CB // 2 + 1)

        GROUP_STEPS = steps_before(NC) - 1

        def first_steps(last):
            steps = [(j, (j - 1) * P, (CB - j) if j < CB else FAR) for j in range(CB, 0, -1)]
            return steps[1 if last else 0:] + [(0, 0, 0)]

        block = ctx.enter_context(nc.Block())

        @block.sync
        def _(sp):
            def load_keys(g, half):
                sp.dma_start(k_rows[:, bass.ds(half * (GH * S), GH * S)],
                             dram["k_stack"][:, bass.ds(g * GH, GH), :]).then_inc(k_in, 16)

            def load_queries(g, tile, half):
                sp.wait_ge(turned, g * NC + tile + 1)
                sp.dma_start(q_rows[:, bass.ds(half * (GH * C), GH * C)],
                             dram["q_stack"][:, bass.ds(g * GH, GH), bass.ds(tile * C, C)]).then_inc(q_in, 16)
                sp.wait_ge(q_in, g * (NC * 16) + tile * 16 + 16)
                sp.sem_inc(q_there, 1)

            def group(g, last):
                for tile in range(2):
                    load_queries(g, tile, tile)
                if not last:
                    sp.wait_ge(k_in, g * 16 + 16)
                    load_keys(g + 1, (g + 1) % 2)
                with sp.Fori(1, NC // 2) as pair:
                    for u in range(2):
                        load_queries(g, pair * 2 + u, u)

            load_keys(0, 0)
            sp.wait_ge(zeroed, 1)
            rows = (TILES + 1) // 9 * P
            for n in range(9):
                sp.dma_start(dram["queue"][n * rows:(n + 1) * rows, :].rearrange("(p r) d -> p (r d)", p=P),
                             zeros[:]).then_inc(queue_clear, 16)
            with sp.Fori(0, G - 1) as g:
                group(g, False)
            group(G - 1, True)
            sp.wait_ge(k_in, G * 16)
            sp.wait_ge(queue_clear, 16 * 9)

        @block.gpsimd
        def _(pool):
            nc.gpsimd.memset(v_now[:], 0.0).then_inc(ready, 1)
            nc.gpsimd.memset(zeros[:], 0.0).then_inc(zeroed, 1)
            nc.gpsimd.memset(probs[:, 0], 0.0).then_inc(ready, 1)
            nc.gpsimd.memset(probs[:, RING - 1], 0.0).then_inc(ready, 1)
            pool.wait_ge(ready, 3)
            nc.gpsimd.memset(v_now[:, :, :, HD:HD + 1], 1.0).then_inc(ready, 1)
            pool.wait_ge(ready, 4)
            pool.sem_inc(v_copied, LAG)
            with pool.Fori(0, G) as g:
                def copy(n, kb, slot):
                    pool.wait_ge(pv_done, n + 1)
                    pool.sem_inc(slot_free, 1)
                    nc.gpsimd.tensor_copy(v_now[:, slot, :, 0:HD],
                                          v[:, bass.ds(kb, 1), bass.ds(g * (GH * HD), GH * HD)].rearrange(
                                              "p a (h d) -> p (a h) d", h=GH)).then_inc(v_copied, 1)

                def tile_values(tile, last):
                    n = pool.snap(g * GROUP_STEPS + steps_before(tile))
                    steps = first_steps(last)
                    for i, (j, _, slot) in enumerate(steps):
                        copy(n + i, tile * CB + j if j else 0, slot)
                    if not isinstance(tile, int) or tile > 0:
                        with pool.Fori(0, tile) as it:
                            for u in range(CB):
                                copy(n + it * CB + (len(steps) + u), it * CB + (u + 1), (u + 1) % RING)

                over_tiles(pool, tile_values)

        @block.tensor
        def _(pe):
            def scores(n, half, kb, first, place, edge):
                k_at, q_at = place
                pe.wait_ge(exped, n * 2 + (half + 3))
                for i in range(HALF):
                    h = half * HALF + i
                    ins = nc.tensor.matmul(ps_s[:, half, i, first:C],
                                           k_rows[:, bass.ds(k_at + kb * P + h * S, P)],
                                           q_rows[:, bass.ds(q_at + (h * C + first), C - first)],
                                           start=True, stop=not edge)
                    if edge:
                        ins = nc.tensor.matmul(ps_s[:, half, i, first:first + P], ident_bf[:], mask[:],
                                               start=False, stop=True)
                ins.then_inc(scored, 1)

            def product(n, first, slot, start):
                pe.wait_ge(v_copied, n + 1)
                pe.wait_ge(exped, n * 2 + 2)
                for h in range(GH):
                    ins = nc.tensor.matmul(ps_o[h * CT:(h + 1) * CT, first:C], v_now[:, slot, h, :],
                                           probs[:, slot, h, first:C], start=start, stop=False,
                                           skip_group_check=True)
                ins.then_inc(pv_done, 1)

            def transposes(r):
                pe.wait_ge(out_read, r + 1)
                pe.wait_ge(normed, r + 1)
                for j in range(CB):
                    ins = nc.tensor.transpose(ps_t[:, j, :], out_T[:, j * P:(j + 1) * P], ident[:])
                ins.then_inc(turned, 1)

            pe.wait_ge(ready, 4)
            pe.sem_inc(turned, 1)
            pe.sem_inc(pv_done, LAG)
            for h in range(GH):
                nc.tensor.matmul(ps_o[h * CT:(h + 1) * CT, :], v_now[:, 0, h, :], probs[:, 0, h, :], start=True,
                                 stop=False, skip_group_check=True)
            with pe.Fori(0, G) as g:
                def tile_steps(tile, last):
                    n = pe.snap(g * GROUP_STEPS + steps_before(tile))
                    r = g * NC + tile
                    place = (pe.snap((g % 2) * (GH * S)),
                             (tile % 2) * (GH * C) if isinstance(tile, int) else pe.snap((tile % 2) * (GH * C)))
                    pe.wait_ge(k_in, g * 16 + 16)
                    pe.wait_ge(q_in, r * 16 + 16)
                    steps = first_steps(last)
                    waiting = [(0, RING - 1, False), (0, 0, False)]
                    for i, (j, first, slot) in enumerate(steps):
                        kb = tile * CB + j if j else 0
                        scores(n + i, 0, kb, first, place, j > 0)
                        if i == LAG:
                            pe.wait_ge(out_read, r + 1)
                        product(n + i, *waiting.pop(0))
                        scores(n + i, 1, kb, first, place, j > 0)
                        if i == LAG + 1:
                            transposes(r)
                        waiting.append((first, slot, i == 0))
                    if not isinstance(tile, int) or tile > 0:
                        with pe.Fori(0, tile) as it:
                            for u in range(CB):
                                m = n + it * CB + (len(steps) + u)
                                scores(m, 0, it * CB + (u + 1), 0, place, False)
                                product(m, 0, (u + 1 - LAG) % RING, False)
                                scores(m, 1, it * CB + (u + 1), 0, place, False)

                over_tiles(pe, tile_steps)
            product(G * GROUP_STEPS, 0, RING - 1, False)
            product(G * GROUP_STEPS + 1, 0, 0, False)
            transposes(G * NC)

        @block.scalar
        def _(act):
            nc.scalar.activation(warm[:], ident[:, 0:1], ACT.Exp).then_inc(exped, 1)
            act.sem_inc(exped, 3)
            with act.Fori(0, G) as g:
                def exponentials(n, first, slot):
                    for half in range(2):
                        act.wait_ge(scored, n * 2 + (half + 1))
                        if half == 0:
                            act.wait_ge(pv_done, n + 1)
                        heads = slice(half * HALF, (half + 1) * HALF)
                        nc.scalar.activation(probs[:, slot, heads, first:C], ps_s[:, half, :, first:C],
                                             ACT.Exp).then_inc(exped, 1)

                def tile_exponentials(tile, last):
                    n = act.snap(g * GROUP_STEPS + steps_before(tile))
                    steps = first_steps(last)
                    for i, (_, first, slot) in enumerate(steps):
                        exponentials(n + i, first, slot)
                    if not isinstance(tile, int) or tile > 0:
                        with act.Fori(0, tile) as it:
                            for u in range(CB):
                                exponentials(n + it * CB + (len(steps) + u), 0, (u + 1) % RING)

                over_tiles(act, tile_exponentials)

        @block.vector
        def _(dve):
            nc.vector.memset(out_T[:], 0.0).then_inc(out_read, 1)
            dve.sem_inc(normed, 2)
            with dve.Fori(0, G) as g:
                def tile_out(tile, last):
                    n = dve.snap(g * GROUP_STEPS + steps_before(tile))
                    r = g * NC + tile
                    dve.wait_ge(pv_done, n + tile * CB + (len(first_steps(last)) + 2 * LAG))
                    dve.wait_ge(turned, r + 2)
                    nc.vector.tensor_copy(out_T[:], ps_o[:]).then_inc(out_read, 1)
                    dve.wait_ge(turned, r + 3)
                    heads = ps_t[:].rearrange("p j (h c) -> p j h c", h=GH)
                    nc.vector.reciprocal(inv[:], heads[:, :, :, HD]).then_inc(inverted, 1)
                    dve.wait_ge(inverted, r + 1)
                    to = mixed[:, bass.ds(tile * CB, CB), bass.ds(g * (GH * HD), GH * HD)]
                    nc.vector.tensor_tensor(to.rearrange("p j (h d) -> p j h d", h=GH), heads[:, :, :, 0:HD],
                                            inv[:].unsqueeze(3).to_broadcast([P, CB, GH, HD]),
                                            ALU.mult).then_inc(normed, 1)

                over_tiles(dve, tile_out)


def route(nc, dram, keep):
    with ExitStack() as ctx:
        def sb(name, shape, dt):
            return ctx.enter_context(nc.sbuf_tensor(name, shape, dt))

        def psum(name, shape, dt):
            return ctx.enter_context(nc.psum_tensor(name, shape, dt))

        def sem(name):
            return ctx.enter_context(nc.semaphore(name))

        ident, gates, mod_cols, mixed = (keep[n] for n in ("ident", "gates", "mod_cols", "mixed"))
        rows = keep["w2"][:, E // 2:].rearrange("p e f d -> p (e f) d")
        m_now = keep["w2"][:, E // 2 - 2].rearrange("p (u j) d -> p u j d", u=2)
        spare = keep["w2"][:, E // 2 - 1]
        wo = sb("rt_wo", [P, KD, D], F32)
        gate_w = sb("rt_gate_w", [P, KD, E], F32)
        gate_b = sb("rt_gate_b", [P, E], F32)
        bo_gated = sb("rt_bo_gated", [P, D], F32)
        b1_rows = sb("rt_b1_rows", [E * FF, P], F32)
        x_now = sb("rt_x_now", [P, 2, CB, D], F32)
        xs = sb("rt_xs", [P, CB, D], F32)
        aT = sb("rt_aT", [P, KD, C], F32)
        hT = sb("rt_hT", [P, KD, C], F32)
        gated = sb("rt_gated", [P, CB, D], F32)
        stats = sb("rt_stats", [P, CB, 6], F32)
        mean_var = sb("rt_mean_var", [P, CB, 2], F32)
        eps = sb("rt_eps", [P, 1], F32)
        std = sb("rt_std", [P, CB], F32)
        rstd = sb("rt_rstd", [P, CB], F32)
        shift = sb("rt_shift", [P, CB], F32)
        score = sb("rt_score", [P, NT, E], F32)
        masked, equal, *pick = (spare[:, i].rearrange("p (t e) -> p t e", e=E) for i in range(4))
        top = [sb(f"rt_top_{i}", [P, NT], F32) for i in range(2)]
        least = sb("rt_least", [P, NT], F32)
        order = sb("rt_order", [P, E], F32)
        both = sb("rt_both", [P, NT, E], BF16)
        before_bf = sb("rt_before", [P, P], BF16)
        ones_bf = sb("rt_ones", [P, P], BF16)
        ex = sb("rt_ex", [P, NT], F32)
        den = sb("rt_den", [P, NT], F32)
        *scan, total = (spare[:, i].rearrange("p (t e) -> p t e", e=E) for i in range(4, 7))
        filled = spare[:, 7].rearrange("p (e t) -> p e t", e=E)
        starts_at = sb("rt_starts_at", [P, NT], F32)
        tiles = sb("rt_tiles", [P, E], F32)
        run = [sb(f"rt_run_{i}", [P, E], F32) for i in range(2)]
        start = sb("rt_start", [P, E], F32)
        slot = sb("rt_slot", [P, NT, E], F32)
        slot_of = sb("rt_slot_of", [P, NT, 2], F32)
        tile_no = sb("rt_tile_no", [1, TILES], F32)
        begun = sb("rt_begun", [1, TILES, E], F32)
        owner = sb("rt_owner", [1, TILES], F32)

        ps_a = psum("rt_ps_a", [P, KD, C], F32)
        ps_o = psum("rt_ps_o", [P, CB, D], F32)
        ps_t = psum("rt_ps_t", [P, KD, C], F32)
        ps_g = psum("rt_ps_g", [P, C], F32)
        ps_r = psum("rt_ps_r", [P, 2, NT * E], F32)

        w_in = sem("rt_w_in")
        x_in = [sem(f"rt_x_in_{u}") for u in range(2)]
        pool_step = sem("rt_pool_step")
        dve_step = sem("rt_dve_step")
        m_free = sem("rt_m_free")
        m_copied = sem("rt_m_copied")
        sum_seen = sem("rt_sum_seen")
        stats_seen = sem("rt_stats_seen")
        x_biased = sem("rt_x_biased")
        m_turned = sem("rt_m_turned")
        a_kept = sem("rt_a_kept")
        projected = sem("rt_projected")
        o_read = sem("rt_o_read")
        sum_ready = sem("rt_sum_ready")
        var_ready = sem("rt_var_ready")
        std_ready = sem("rt_std_ready")
        norm_ready = sem("rt_norm_ready")
        xs_ready = sem("rt_xs_ready")
        xs_kept = sem("rt_xs_kept")
        x_turned = sem("rt_x_turned")
        h_kept = sem("rt_h_kept")
        scored = sem("rt_scored")
        score_kept = sem("rt_score_kept")
        b1_turned = sem("rt_b1_turned")
        tops_ready = sem("rt_tops_ready")
        ex_ready = sem("rt_ex_ready")
        both_ready = sem("rt_both_ready")
        counted = sem("rt_counted")
        slots_ready = sem("rt_slots_ready")
        scattered = sem("rt_scattered")
        bias_ready = sem("rt_bias_ready")

        x_v = dram["x"].rearrange("a (t p) d -> p (a t) d", p=P)
        block = ctx.enter_context(nc.Block())

        @block.sync
        def _(sp):
            with sp.Fori(0, NC // 2) as it:
                for u in range(2):
                    c = it * 2 + u
                    sp.wait_ge(sum_ready, c + 1)
                    sp.dma_start(x_now[:, u], x_v[:, bass.ds(c * CB, CB), :]).then_inc(x_in[u], 16)

        @block.gpsimd
        def _(pool):
            nc.gpsimd.iota(order[:], pattern=[[1, E]], base=-E, channel_multiplier=0,
                           allow_small_or_imprecise_dtypes=True).then_inc(pool_step, 1)
            nc.gpsimd.iota(starts_at[:], pattern=[[P, NT]], base=0, channel_multiplier=0,
                           allow_small_or_imprecise_dtypes=True).then_inc(pool_step, 1)
            nc.gpsimd.iota(tile_no[:], pattern=[[1, TILES]], base=0, channel_multiplier=0,
                           allow_small_or_imprecise_dtypes=True).then_inc(pool_step, 1)
            nc.gpsimd.memset(ones_bf[:], 1.0).then_inc(pool_step, 1)
            pool.wait_ge(pool_step, 4)
            nc.gpsimd.affine_select(out=before_bf[:], in_=ones_bf[:], compare_op=ALU.is_gt, fill=0.0, base=0,
                                    pattern=[[1, P]], channel_multiplier=-1).then_inc(pool_step, 1)
            pool.wait_ge(w_in, 16 * 5)
            nc.gpsimd.tensor_tensor(bo_gated[:], bo_gated[:], gates[:, 0, :], ALU.mult).then_inc(pool_step, 1)
            pool.wait_ge(pool_step, 6)
            pool.sem_inc(xs_kept, 1)
            with pool.Fori(0, NC // 2) as it:
                for u in range(2):
                    c = it * 2 + u
                    pool.wait_ge(m_turned, c + 1)
                    pool.sem_inc(m_free, 1)
                    nc.gpsimd.tensor_copy(m_now[:, u], mixed[:, bass.ds(c * CB, CB), :]).then_inc(m_copied, 1)
                    pool.wait_ge(x_in[u], it * 16 + 16)
                    nc.gpsimd.tensor_tensor(x_now[:, u], x_now[:, u],
                                            bo_gated[:].unsqueeze(1).to_broadcast([P, CB, D]),
                                            ALU.add).then_inc(x_biased, 1)
                    pool.wait_ge(xs_ready, c * CB + 2 * CB)
                    nc.gpsimd.tensor_copy(rows[:, bass.ds(c * CB, CB), :], xs[:]).then_inc(xs_kept, 1)
            pool.wait_ge(xs_kept, NC + 1)
            pool.wait_ge(slots_ready, 1)
            for t in range(NT):
                for i in range(2):
                    pool.indirect_dma_start(dram["queue"], bass.IndirectOffsetOnAxis(
                        ap=keep["slots"][:, 2 * t + i:2 * t + i + 1], axis=0), rows[:, t, :], None
                                            ).then_inc(scattered, 16)
            pool.wait_ge(scattered, 16 * 2 * NT)

        @block.tensor
        def _(pe):
            pe.wait_ge(w_in, 16 * 5)
            nc.tensor.transpose(ps_t[:, 0, 0:E * FF], b1_rows[:], ident[0:E * FF, 0:E * FF]).then_inc(b1_turned, 1)
            pe.wait_ge(bias_ready, 1)
            pe.sem_inc(m_turned, 2)
            pe.sem_inc(projected, 1)
            pe.sem_inc(scored, 1)
            with pe.Fori(0, NC // 2) as it:
                for u in range(2):
                    c = it * 2 + u
                    pe.wait_ge(m_copied, c + 1)
                    pe.wait_ge(a_kept, c + 1)
                    for k in range(KD):
                        for j in range(CB):
                            ins = nc.tensor.transpose(ps_a[:, k, j * P:(j + 1) * P],
                                                      m_now[:, u, j, k * P:(k + 1) * P], ident[:])
                    ins.then_inc(m_turned, 1)
                    pe.wait_ge(a_kept, c + 2)
                    pe.wait_ge(o_read, c + 1)
                    for j in range(CB):
                        for k in range(KD):
                            ins = nc.tensor.matmul(ps_o[:, j, :], aT[:, k, j * P:(j + 1) * P], wo[:, k, :],
                                                   start=k == 0, stop=k == KD - 1)
                    ins.then_inc(projected, 1)
                    pe.wait_ge(xs_ready, c * CB + 2 * CB)
                    pe.wait_ge(h_kept, c + 1)
                    for k in range(KD):
                        for j in range(CB):
                            ins = nc.tensor.transpose(ps_t[:, k, j * P:(j + 1) * P],
                                                      xs[:, j, k * P:(k + 1) * P], ident[:])
                    ins.then_inc(x_turned, 1)
                    pe.wait_ge(h_kept, c + 2)
                    pe.wait_ge(score_kept, c + 1)
                    for j in range(CB):
                        for k in range(KD):
                            ins = nc.tensor.matmul(ps_g[:, j * E:(j + 1) * E], hT[:, k, j * P:(j + 1) * P],
                                                   gate_w[:, k, :], start=k == 0, stop=k == KD - 1)
                    ins.then_inc(scored, 1)
            pe.wait_ge(both_ready, 1)
            flat = both[:].rearrange("p t e -> p (t e)")
            nc.tensor.matmul(ps_r[:, 0, :], before_bf[:], flat, start=True, stop=True)
            nc.tensor.matmul(ps_r[:, 1, :], ones_bf[:], flat, start=True, stop=True).then_inc(counted, 1)

        @block.scalar
        def _(act):
            act.dma_start(wo[:], dram["Wo"].rearrange("(k p) n -> p k n", p=P)).then_inc(w_in, 16)
            act.dma_start(gate_w[:], dram["gate_w"].rearrange("(k p) n -> p k n", p=P)).then_inc(w_in, 16)
            act.dma_start(gate_b[:], dram["gate_b"].rearrange("(a n) -> a n", a=1).partition_broadcast(P)
                          ).then_inc(w_in, 16)
            act.dma_start(bo_gated[:], dram["bo"].rearrange("(a n) -> a n", a=1).partition_broadcast(P)
                          ).then_inc(w_in, 16)
            act.dma_start(b1_rows[:], dram["b1"].rearrange("e (f p) -> (e f) p", p=P)).then_inc(w_in, 16)
            act.dma_start(keep["b2"][:], dram["b2"].rearrange("(a e) d -> a e d", a=1).partition_broadcast(P)
                          ).then_inc(keep["weights_in"], 16)
            for e in range(E):
                act.dma_start(keep["w1"][:, e], dram["W1"][e].rearrange("(k p) f -> p k f", p=P)
                              ).then_inc(keep["weights_in"], 16)
            for e in range(E // 2 - 2):
                act.dma_start(keep["w2"][:, e], dram["W2"][e].rearrange("(f p) d -> p f d", p=P)
                              ).then_inc(keep["weights_in"], 16)
            act.wait_ge(b1_turned, 1)
            nc.scalar.copy(keep["b1"][:], ps_t[:, 0, 0:E * FF]).then_inc(bias_ready, 1)
            act.wait_ge(pool_step, 6)
            act.sem_inc(a_kept, 1)
            act.wait_ge(bias_ready, 1)
            act.sem_inc(h_kept, 1)
            act.sem_inc(xs_ready, CB)
            act.wait_ge(dve_step, 1)
            nc.scalar.activation(std[:, 0:1], eps[:], ACT.Sqrt).then_inc(std_ready, 1)
            with act.Fori(0, NC) as c:
                act.wait_ge(m_turned, c + 3)
                act.wait_ge(projected, c + 1)
                nc.scalar.copy(aT[:], ps_a[:]).then_inc(a_kept, 1)
                act.wait_ge(var_ready, c + 1)
                nc.scalar.activation(std[:], mean_var[:, :, 1], ACT.Sqrt, bias=eps[:, 0:1]).then_inc(std_ready, 1)
                act.wait_ge(norm_ready, c + 1)
                act.wait_ge(xs_kept, c + 1)
                for j in range(CB):
                    nc.scalar.activation(xs[:, j, :], mixed[:, bass.ds(c * CB + j, 1), :].rearrange("p a d -> p (a d)"),
                                         ACT.Identity, scale=rstd[:, j:j + 1],
                                         bias=shift[:, j:j + 1]).then_inc(xs_ready, 1)
                act.wait_ge(x_turned, c + 1)
                act.wait_ge(scored, c + 1)
                for k in range(KD):
                    ins = nc.scalar.activation(hT[:, k, :], ps_t[:, k, :], ACT.Identity,
                                               scale=mod_cols[:, 6 + k:7 + k], bias=mod_cols[:, 4 + k:5 + k])
                ins.then_inc(h_kept, 1)
            act.wait_ge(tops_ready, 1)
            nc.scalar.activation(ex[:], least[:], ACT.Exp).then_inc(ex_ready, 1)
            act.wait_ge(h_kept, NC + 1)

        @block.vector
        def _(dve):
            step = Tally(dve_step)
            step.inc(nc.vector.memset(eps[:], EPS))
            dve.sem_inc(sum_ready, 2)
            dve.sem_inc(o_read, 1)
            dve.sem_inc(score_kept, 1)
            dve.wait_ge(w_in, 16 * 5)
            STEPS = 2
            first = step.n
            with dve.Fori(0, NC // 2) as it:
                for u in range(2):
                    c = it * 2 + u
                    step = Tally(dve_step, c * STEPS + first)
                    dve.wait_ge(projected, c + 2)
                    nc.vector.tensor_tensor(gated[:], ps_o[:], gates[:, 0, :].unsqueeze(1).to_broadcast([P, CB, D]),
                                            ALU.mult).then_inc(o_read, 1)
                    dve.wait_ge(o_read, c + 2)
                    dve.wait_ge(x_biased, c + 1)
                    chunk = mixed[:, bass.ds(c * CB, CB), :]
                    nc.vector.tensor_tensor(chunk, gated[:], x_now[:, u], ALU.add).then_inc(sum_ready, 1)
                    dve.wait_ge(sum_ready, c + 3)
                    dve.sem_inc(sum_seen, 1)
                    for j in range(CB):
                        ins = nc.vector.bn_stats(stats[:, j, :],
                                                 mixed[:, bass.ds(c * CB + j, 1), :].rearrange("p a d -> p (a d)"))
                    step.inc(ins)
                    step.wait(dve)
                    dve.wait_ge(xs_ready, c * CB + CB)
                    dve.sem_inc(stats_seen, 1)
                    for j in range(CB):
                        ins = nc.vector.bn_aggr(mean_var[:, j, :], stats[:, j, :])
                    ins.then_inc(var_ready, 1)
                    dve.wait_ge(std_ready, c + 2)
                    step.inc(nc.vector.reciprocal(rstd[:], std[:]))
                    step.wait(dve)
                    nc.vector.scalar_tensor_tensor(out=shift[:], in0=mean_var[:, :, 0], scalar=-1.0, in1=rstd[:],
                                                   op0=ALU.mult, op1=ALU.mult).then_inc(norm_ready, 1)
                    dve.wait_ge(scored, c + 2)
                    nc.vector.tensor_tensor(score[:, bass.ds(c * CB, CB), :],
                                            ps_g[:, 0:CB * E].rearrange("p (j e) -> p j e", e=E),
                                            gate_b[:].unsqueeze(1).to_broadcast([P, CB, E]),
                                            ALU.add).then_inc(score_kept, 1)
                    assert step.n == STEPS
            dve.wait_ge(score_kept, NC + 1)
            dve.wait_ge(pool_step, 6)
            step = Tally(dve_step, first + NC * STEPS)

            def wide(ap):
                return ap.unsqueeze(2).to_broadcast([P, NT, E])

            experts = order[:].unsqueeze(1).to_broadcast([P, NT, E])
            values = score
            for i in range(2):
                step.inc(nc.vector.tensor_reduce(top[i][:], values[:], AX.X, ALU.max))
                step.wait(dve)
                step.inc(nc.vector.tensor_tensor(equal, values[:], wide(top[i][:]), ALU.is_equal))
                step.wait(dve)
                step.inc(nc.vector.tensor_tensor(equal, equal, experts, ALU.mult))
                step.wait(dve)
                step.inc(nc.vector.tensor_reduce(least[:], equal, AX.X, ALU.min))
                step.wait(dve)
                step.inc(nc.vector.tensor_tensor(pick[i][:], experts, wide(least[:]), ALU.is_equal))
                step.wait(dve)
                if i == 0:
                    step.inc(nc.vector.scalar_tensor_tensor(out=masked, in0=pick[0][:], scalar=MASKED,
                                                            in1=score[:], op0=ALU.mult, op1=ALU.add))
                    step.wait(dve)
                    values = masked
            nc.vector.tensor_tensor(both[:], pick[0][:], pick[1][:], ALU.add).then_inc(both_ready, 1)
            nc.vector.tensor_tensor(least[:], top[1][:], top[0][:], ALU.subtract).then_inc(tops_ready, 1)
            dve.wait_ge(ex_ready, 1)
            step.inc(nc.vector.tensor_scalar_add(den[:], ex[:], 1.0))
            step.wait(dve)
            step.inc(nc.vector.reciprocal(keep["share"][:, 0, :], den[:]))
            step.wait(dve)
            step.inc(nc.vector.tensor_tensor(keep["share"][:, 1, :], ex[:], keep["share"][:, 0, :], ALU.mult))
            dve.wait_ge(counted, 1)
            step.inc(nc.vector.tensor_copy(total[:], ps_r[:, 1, :].rearrange("p (t e) -> p t e", e=E)))
            step.wait(dve)
            have, n, reach = total, 0, 1
            while reach < NT:
                to = scan[n % 2]
                step.inc(nc.vector.tensor_copy(to[:, 0:reach], have[:, 0:reach]))
                step.inc(nc.vector.tensor_tensor(to[:, reach:], have[:, reach:], have[:, 0:NT - reach], ALU.add))
                step.wait(dve)
                have, n, reach = to, n + 1, reach * 2
            count = have[:, NT - 1, :]
            step.inc(nc.vector.tensor_tensor(filled[:], count.unsqueeze(2).to_broadcast([P, E, NT]),
                                             starts_at[:].unsqueeze(1).to_broadcast([P, E, NT]), ALU.is_gt))
            step.wait(dve)
            step.inc(nc.vector.tensor_reduce(tiles[:], filled[:], AX.X, ALU.add))
            step.wait(dve)
            sums, n, reach = tiles, 0, 1
            while reach < E:
                to = run[n % 2]
                step.inc(nc.vector.tensor_copy(to[:, 0:reach], sums[:, 0:reach]))
                step.inc(nc.vector.tensor_tensor(to[:, reach:], sums[:, reach:], sums[:, 0:E - reach], ALU.add))
                step.wait(dve)
                sums, n, reach = to, n + 1, reach * 2
            step.inc(nc.vector.tensor_tensor(start[:], sums[:], tiles[:], ALU.subtract))
            step.inc(nc.vector.tensor_tensor(slot[:], have[:], total[:], ALU.subtract))
            step.wait(dve)
            step.inc(nc.vector.tensor_tensor(slot[:], slot[:], ps_r[:, 0, :].rearrange("p (t e) -> p t e", e=E),
                                             ALU.add))
            step.wait(dve)
            step.inc(nc.vector.scalar_tensor_tensor(out=slot[:], in0=start[:].unsqueeze(1).to_broadcast([P, NT, E]),
                                                    scalar=float(P), in1=slot[:], op0=ALU.mult, op1=ALU.add))
            step.wait(dve)
            for i in range(2):
                step.inc(nc.vector.tensor_tensor(pick[i][:], pick[i][:], slot[:], ALU.mult))
                step.wait(dve)
                step.inc(nc.vector.tensor_reduce(slot_of[:, :, i], pick[i][:], AX.X, ALU.add))
            step.wait(dve)
            nc.vector.tensor_copy(keep["slots"][:], slot_of[:].rearrange("p t i -> p (t i)")).then_inc(slots_ready, 1)
            step.inc(nc.vector.tensor_tensor(begun[:], tile_no[:].unsqueeze(2).to_broadcast([1, TILES, E]),
                                             start[0:1, :].unsqueeze(1).to_broadcast([1, TILES, E]), ALU.is_ge))
            step.wait(dve)
            step.inc(nc.vector.tensor_reduce(owner[:], begun[:], AX.X, ALU.add))
            step.wait(dve)
            step.inc(nc.vector.tensor_scalar_add(owner[:], owner[:], -1.0))
            step.wait(dve)
            step.inc(nc.vector.tensor_copy(keep["owner"][:], owner[:]))
            step.wait(dve)


def experts(nc, dram, keep):
    with ExitStack() as ctx:
        def sb(name, shape, dt):
            return ctx.enter_context(nc.sbuf_tensor(name, shape, dt))

        def psum(name, shape, dt):
            return ctx.enter_context(nc.psum_tensor(name, shape, dt))

        def sem(name):
            return ctx.enter_context(nc.semaphore(name))

        ident, mod_cols, w1, w2, b1, b2, owner = (
            keep[n] for n in ("ident", "mod_cols", "w1", "w2", "b1", "b2", "owner"))
        HALVES = FF * P // C
        x_tile = sb("ex_x_tile", [P, 2, D], F32)
        xT = sb("ex_xT", [P, KD, P], F32)
        h = sb("ex_h", [P, FF * P], F32)
        hT = sb("ex_hT", [P, FF, P], F32)
        y = sb("ex_y", [P, 2, D], F32)

        ps_x = psum("ex_ps_x", [P, C], F32)
        ps_h = [psum(f"ex_ps_h_{i}", [P, C], F32) for i in range(HALVES)]
        ps_hT = psum("ex_ps_hT", [P, FF, P], F32)
        ps_y = [psum(f"ex_ps_y_{u}", [P, C], F32) for u in range(2)]

        x_in = [sem(f"ex_x_in_{u}") for u in range(2)]
        w2_in = sem("ex_w2_in")
        x_turned = sem("ex_x_turned")
        xT_ready = sem("ex_xT_ready")
        hidden = [sem(f"ex_hidden_{i}") for i in range(HALVES)]
        h_copied = [sem(f"ex_h_copied_{i}") for i in range(HALVES)]
        h_turned = sem("ex_h_turned")
        rectified = sem("ex_rectified")
        out_done = sem("ex_out_done")
        y_ready = sem("ex_y_ready")
        y_stored = [sem(f"ex_y_stored_{u}") for u in range(2)]
        block = ctx.enter_context(nc.Block())

        def over_queue(eng, body, done=0):
            with eng.Fori(done, (TILES - 1) // 2) as it:
                for u in range(2):
                    body(it * 2 + (u + 1), (u + 1) % 2, it)

        @block.sync
        def _(sp):
            for e in range(E // 2 - 2, E):
                sp.dma_start(w2[:, e], dram["W2"][e].rearrange("(f p) d -> p f d", p=P)).then_inc(w2_in, 16)
            sp.sem_inc(x_turned, 2)

            def load(tile, u):
                sp.wait_ge(x_turned, tile + 1)
                sp.dma_start(x_tile[:, u, :], dram["queue"][bass.ds(tile * P, P), :]).then_inc(x_in[u], 16)

            load(0, 0)
            over_queue(sp, lambda tile, u, it: load(tile, u))
            load(TILES, TILES % 2)
            sp.wait_ge(x_in[TILES % 2], 16 * ((TILES + 1) // 2))

        @block.gpsimd
        def _(pool):
            def store(tile, u):
                pool.wait_ge(y_ready, tile + 3)
                pool.dma_start(dram["answers"][bass.ds(tile * P, P), :], y[:, u, :]).then_inc(y_stored[u], 16)

            store(0, 0)
            over_queue(pool, lambda tile, u, it: store(tile, u))
            for u in range(2):
                pool.wait_ge(y_stored[u], 16 * ((TILES + 1 - u) // 2))

        @block.tensor
        def _(pe):
            def turn_rows(tile, u, loads):
                pe.wait_ge(x_in[u], loads * 16)
                pe.wait_ge(xT_ready, tile + 1)
                for k in range(KD):
                    ins = nc.tensor.transpose(ps_x[:, k * P:(k + 1) * P], x_tile[:, u, k * P:(k + 1) * P], ident[:])
                ins.then_inc(x_turned, 1)

            def first_layer(tile):
                e = pe.value_load(owner[0:1, bass.ds(tile, 1)], min_val=0, max_val=E - 1)
                pe.wait_ge(xT_ready, tile + 2)
                for i in range(HALVES):
                    pe.wait_ge(h_copied[i], tile + 1)
                    for k in range(KD):
                        ins = nc.tensor.matmul(ps_h[i][:], xT[:, k, :],
                                               w1[:, bass.ds(e, 1), k, i * C:(i + 1) * C].rearrange(
                                                   "p a f -> p (a f)"), start=k == 0, stop=k == KD - 1)
                    ins.then_inc(hidden[i], 1)
                return e

            def turn_hidden(tile):
                for i in range(HALVES):
                    pe.wait_ge(h_copied[i], tile + 2)
                pe.wait_ge(rectified, tile * FF + FF)
                for f in range(FF):
                    ins = nc.tensor.transpose(ps_hT[:, f, :], h[:, f * P:(f + 1) * P], ident[:])
                ins.then_inc(h_turned, 1)

            def second_layer(tile, u):
                e = pe.value_load(owner[0:1, bass.ds(tile, 1)], min_val=0, max_val=E - 1)
                pe.wait_ge(rectified, tile * FF + 2 * FF)
                pe.wait_ge(y_ready, tile + 1)
                for f in range(FF):
                    ins = nc.tensor.matmul(ps_y[u][:, 0:D], hT[:, f, :],
                                           w2[:, bass.ds(e, 1), f, :].rearrange("p a d -> p (a d)"),
                                           start=f == 0, stop=f == FF - 1)
                ins.then_inc(out_done, 1)

            pe.wait_ge(keep["weights_in"], 16 * (1 + E + E // 2 - 2))
            turn_rows(0, 0, 1)
            first_layer(0)
            pe.wait_ge(w2_in, 16 * (E // 2 + 2))
            turn_rows(1, 1, 1)
            turn_hidden(0)

            def tile_steps(tile, u, it):
                first_layer(tile)
                second_layer(tile - 1, 1 - u)
                turn_rows(tile + 1, 1 - u, it + (2 if u == 1 else 2))
                turn_hidden(tile)

            over_queue(pe, tile_steps)
            second_layer(TILES - 1, (TILES - 1) % 2)

        @block.scalar
        def _(act):
            act.sem_inc(h_copied[0], 1)
            act.sem_inc(rectified, FF)

            def tile_steps(tile):
                e = act.value_load(owner[0:1, bass.ds(tile, 1)], min_val=0, max_val=E - 1)
                act.wait_ge(hidden[0], tile + 1)
                nc.scalar.copy(h[:, 0:C], ps_h[0][:]).then_inc(h_copied[0], 1)
                act.wait_ge(h_turned, tile + 1)
                for f in range(FF):
                    nc.scalar.activation(hT[:, f, :], ps_hT[:, f, :], ACT.Relu,
                                         bias=b1[:, bass.ds(e * FF + f, 1)]).then_inc(rectified, 1)

            tile_steps(0)
            over_queue(act, lambda tile, u, it: tile_steps(tile))

        @block.vector
        def _(dve):
            dve.sem_inc(h_copied[1], 1)
            dve.sem_inc(xT_ready, 1)
            dve.sem_inc(y_ready, 2)

            def modulate(tile):
                dve.wait_ge(x_turned, tile + 3)
                for k in range(KD):
                    ins = nc.vector.tensor_scalar(xT[:, k, :], ps_x[:, k * P:(k + 1) * P], mod_cols[:, 6 + k:7 + k],
                                                  mod_cols[:, 4 + k:5 + k], ALU.mult, ALU.add)
                ins.then_inc(xT_ready, 1)

            def copy_hidden(tile):
                dve.wait_ge(hidden[1], tile + 1)
                nc.vector.tensor_copy(h[:, C:2 * C], ps_h[1][:]).then_inc(h_copied[1], 1)

            def answer(tile, u, stores):
                e = dve.value_load(owner[0:1, bass.ds(tile, 1)], min_val=0, max_val=E - 1)
                dve.wait_ge(out_done, tile + 1)
                if not isinstance(stores, int) or stores > 0:
                    dve.wait_ge(y_stored[u], stores * 16)
                nc.vector.tensor_tensor(y[:, u, :], ps_y[u][:, 0:D],
                                        b2[:, bass.ds(e, 1), :].rearrange("p a d -> p (a d)"),
                                        ALU.add).then_inc(y_ready, 1)

            modulate(0)
            copy_hidden(0)
            modulate(1)

            def tile_steps(tile, u, it):
                copy_hidden(tile)
                answer(tile - 1, 1 - u, it)
                modulate(tile + 1)

            for tile in (1, 2):
                tile_steps(tile, tile % 2, 0)
            over_queue(dve, tile_steps, done=1)
            answer(TILES - 1, (TILES - 1) % 2, (TILES - 1) // 2)


def combine(nc, dram, keep):
    with ExitStack() as ctx:
        def sb(name, shape, dt):
            return ctx.enter_context(nc.sbuf_tensor(name, shape, dt))

        def sem(name):
            return ctx.enter_context(nc.semaphore(name))

        RING = 4
        share, gates, mixed = keep["share"], keep["gates"], keep["mixed"]
        answer = [sb(f"co_answer_{i}", [P, RING, D], F32) for i in range(2)]
        fetched = [sem(f"co_fetched_{r}") for r in range(RING)]
        stored = [sem(f"co_stored_{r}") for r in range(RING)]
        dve_step = sem("co_dve_step")
        summed = sem("co_summed")
        out_v = dram["out"].rearrange("a (t p) d -> p (a t) d", p=P)
        block = ctx.enter_context(nc.Block())

        @block.gpsimd
        def _(pool):
            for t in range(NT):
                if t >= RING:
                    pool.wait_ge(stored[t % RING], 16 * (t // RING))
                for i in range(2):
                    pool.indirect_dma_start(answer[i][:, t % RING, :], None, dram["answers"],
                                            bass.IndirectOffsetOnAxis(ap=keep["slots"][:, 2 * t + i:2 * t + i + 1],
                                                                      axis=0)).then_inc(fetched[t % RING], 16)

        @block.sync
        def _(sp):
            with sp.Fori(0, NT // RING) as it:
                for r in range(RING):
                    sp.wait_ge(summed, it * RING + (r + 1))
                    sp.dma_start(out_v[:, bass.ds(it * RING + r, 1), :], answer[1][:, r:r + 1, :]
                                 ).then_inc(stored[r], 16)
            for r in range(RING):
                sp.wait_ge(stored[r], 16 * (NT // RING))

        @block.vector
        def _(dve):
            STEPS = 3
            with dve.Fori(0, NT // RING) as it:
                for r in range(RING):
                    t = it * RING + r
                    step = Tally(dve_step, t * STEPS)
                    dve.wait_ge(fetched[r], it * 32 + 32)
                    first, second = answer[0][:, r, :], answer[1][:, r, :]
                    step.inc(nc.vector.tensor_scalar(first, first, share[:, 0, bass.ds(t, 1)], None, ALU.mult))
                    step.wait(dve)
                    step.inc(nc.vector.scalar_tensor_tensor(out=second, in0=second,
                                                            scalar=share[:, 1, bass.ds(t, 1)], in1=first,
                                                            op0=ALU.mult, op1=ALU.add))
                    step.wait(dve)
                    step.inc(nc.vector.tensor_tensor(second, second, gates[:, 1, :], ALU.mult))
                    step.wait(dve)
                    nc.vector.tensor_tensor(second, second,
                                            mixed[:, bass.ds(t, 1), :].rearrange("p a d -> p (a d)"),
                                            ALU.add).then_inc(summed, 1)
                    assert step.n == STEPS


def adaln_attention_experts(nc, dram):
    for name in ("k_stack", "q_stack"):
        dram[name] = nc.dram_tensor(name, (STACK, H, S), BF16).ap()
    for name, tiles in (("queue", TILES + 1), ("answers", TILES)):
        dram[name] = nc.dram_tensor(name, (tiles * P, D), F32).ap()
    with ExitStack() as outer:
        def kept(ctx, name, shape, dt):
            keep[name] = ctx.enter_context(nc.sbuf_tensor("kept_" + name, shape, dt))

        keep = {"weights_in": outer.enter_context(nc.semaphore("weights_in"))}
        kept(outer, "ident", [P, P], F32)
        kept(outer, "gates", [P, 2, D], F32)
        kept(outer, "mod_cols", [P, 8], F32)
        kept(outer, "mixed", [P, NT, D], F32)
        with ExitStack() as inner:
            kept(inner, "ident_bf", [P, P], BF16)
            kept(inner, "mask_kq", [P, P], BF16)
            kept(inner, "mask_qk", [P, P], BF16)
            kept(inner, "v", [P, NT, D], F32)
            attention_inputs(nc, dram, keep)
            row_maxima(nc, dram, keep)
            attention(nc, dram, keep)
        kept(outer, "w1", [P, E, KD, FF * P], F32)
        kept(outer, "w2", [P, E, FF, D], F32)
        kept(outer, "b1", [P, E * FF], F32)
        kept(outer, "b2", [P, E, D], F32)
        kept(outer, "slots", [P, 2 * NT], U32)
        kept(outer, "share", [P, 2, NT], F32)
        kept(outer, "owner", [1, TILES], I32)
        route(nc, dram, keep)
        experts(nc, dram, keep)
        combine(nc, dram, keep)


INPUTS = {
    "x": "L0_attn_x", "Wq": "L0_attn_Wq", "bq": "L0_attn_bq", "Wk": "L0_attn_Wk", "bk": "L0_attn_bk",
    "Wv": "L0_attn_Wv", "bv": "L0_attn_bv", "Wo": "L0_attn_Wo", "bo": "L0_attn_bo",
    "gate_w": "L0_ffn_gate_w", "gate_b": "L0_ffn_gate_b", "W1": "L0_ffn_W1", "b1": "L0_ffn_b1",
    "W2": "L0_ffn_W2", "b2": "L0_ffn_b2", "c": "L0_c", "wmod": "L0_wmod",
}


def kernel(**inputs):
    import numpy as _np
    import concourse.bacc as _bacc
    from concourse.bass_utils import run_bass_kernel_spmd as _run

    nc = _bacc.Bacc("TRN2", target_bir_lowering=False, num_devices=1)
    arrays, dram = {}, {}
    for name, given in INPUTS.items():
        a = _np.ascontiguousarray(inputs[given])
        arrays[f"in_{name}"] = a
        dram[name] = nc.dram_tensor(f"in_{name}", a.shape, mybir.dt.from_np(a.dtype), kind="ExternalInput").ap()
    dram["out"] = nc.dram_tensor("out", (1, S, D), F32, kind="ExternalOutput").ap()
    adaln_attention_experts(nc, dram)
    return _run(nc, [arrays], core_ids=[0]).results[0]["out"]
```

```python
from contextlib import ExitStack

import concourse.bass as bass
from concourse import mybir

ALU = mybir.AluOpType
ACT = mybir.ActivationFunctionType
AX = mybir.AxisListType
F32 = mybir.dt.float32
BF16 = mybir.dt.bfloat16
U32 = mybir.dt.uint32
I32 = mybir.dt.int32

P = 128
S = 4096
D = 256
KD = D // P
H = 16
HD = D // H
GH = 4
G = H // GH
NT = S // P
C = 512
NC = S // C
CB = C // P
TERMS = 6
ROWS = TERMS * HD
STACK = ROWS + 3
E = 8
FF = 1024 // P
TILES = (2 * S + E * (P - 1)) // P
MASKED = -3.0e38
EPS = 1e-5
FIRST_KEYS = 32
ROOM_UP = 70.0
ROOM_DOWN = 60.0
SLACK = 1.0 + 2.0 ** -6
LOADS = 4
STORES = TERMS
K_TERM = [0, 0, 0, 1, 1, 2]
Q_TERM = [0, 1, 2, 0, 1, 0]


class Tally:

    def __init__(self, sem, base=0):
        self.sem, self.base, self.n = sem, base, 0

    def inc(self, ins):
        self.n += 1
        return ins.then_inc(self.sem, 1)

    def wait(self, eng):
        eng.wait_ge(self.sem, self.base + self.n)


def attention_inputs(nc, dram, keep):
    with ExitStack() as ctx:
        def sb(name, shape, dt):
            return ctx.enter_context(nc.sbuf_tensor(name, shape, dt))

        def psum(name, shape, dt):
            return ctx.enter_context(nc.psum_tensor(name, shape, dt))

        def sem(name):
            return ctx.enter_context(nc.semaphore(name))

        ident, gates, v, mod_cols = keep["ident"], keep["gates"], keep["v"], keep["mod_cols"]
        x = sb("x_rows", [P, NT, D], F32)
        xn = sb("xn", [P, 2, CB, D], F32)
        ccol = sb("ccol", [P, KD], F32)
        silu = sb("silu", [P, 4, KD], F32)
        silu_rows = sb("silu_rows", [P, KD, P], F32)
        wmod = sb("wmod", [P, KD, 6 * D], F32)
        wq = sb("wq", [P, KD, D], F32)
        wk = sb("wk", [P, KD, D], F32)
        wv = sb("wv", [P, KD, D], F32)
        wk_turned = sb("wk_turned", [P, KD, D], F32)
        wq_turned = sb("wq_turned", [P, KD, D], F32)
        bk = sb("bk", [P, KD], F32)
        bq = sb("bq", [P, KD], F32)
        bq_scaled = sb("bq_scaled", [P, KD], F32)
        bv_rows = sb("bv_rows", [P, D], F32)
        mod_raw = sb("mod_raw", [P, 8], F32)
        gate_raw = sb("gate_raw", [P, 2, D], F32)
        gate_sign = sb("gate_sign", [P, 2, D], F32)
        gate_abs = sb("gate_abs", [P, 2, D], F32)
        gate_size = sb("gate_size", [P, 2, D], F32)
        stats = sb("stats", [P, NT, 6], F32)
        mean2 = sb("mean2", [P, NT], F32)
        dev = sb("dev", [P, NT], F32)
        dev2 = sb("dev2", [P, NT], F32)
        m2 = sb("m2", [P, NT], F32)
        m2d = sb("m2d", [P, NT], F32)
        var = sb("var", [P, NT], F32)
        shift = sb("shift", [P, NT], F32)
        eps = sb("eps", [P, 1], F32)
        std = sb("std", [P, NT], F32)
        rstd = sb("rstd", [P, NT], F32)
        hT = sb("hT", [P, 2, KD, C], F32)
        kf = sb("kf", [P, KD, C], F32)
        qf = sb("qf", [P, KD, C], F32)
        kparts = sb("kparts", [P, 2, 3, KD, C], BF16)
        qparts = sb("qparts", [P, 2, 3, KD, C], BF16)
        ones = sb("ones", [P, P], F32)
        ones_rows = sb("ones_rows", [3 * H, S], BF16)

        ps_turn = psum("ps_turn", [P, KD, C], F32)
        ps_k = psum("ps_k", [P, KD, C], F32)
        ps_q = psum("ps_q", [P, KD, C], F32)
        ps_v = psum("ps_v", [P, CB, D], F32)

        x_in = [sem(f"x_in_{n}") for n in range(LOADS)]
        mod_in = sem("mod_in")
        w_in = sem("w_in")
        dve_step = sem("dve_step")
        act_step = sem("act_step")
        pool_step = sem("pool_step")
        c_exp = sem("c_exp")
        silu_ready = sem("silu_ready")
        rows_ready = sem("rows_ready")
        mod_ready = sem("mod_ready")
        cols_ready = sem("cols_ready")
        var_ready = sem("var_ready")
        std_ready = sem("std_ready")
        xn_ready = sem("xn_ready")
        turned = sem("turned")
        h_ready = sem("h_ready")
        k_ready = sem("k_ready")
        v_ready = sem("v_ready")
        kq_kept = sem("kq_kept")
        parts_ready = sem("parts_ready")
        v_kept = sem("v_kept")
        stats_ready = sem("stats_ready")
        norm_ready = sem("norm_ready")
        ones_stored = sem("ones_stored")
        k_stored = [sem(f"k_stored_{u}") for u in range(2)]
        q_stored = [sem(f"q_stored_{u}") for u in range(2)]

        x_v = dram["x"].rearrange("a (t p) d -> p (a t) d", p=P)
        block = ctx.enter_context(nc.Block())

        @block.sync
        def _(sp):
            sp.dma_start(ccol[:], dram["c"].rearrange("a (k p) -> p (a k)", p=P),
                         allow_slow_non_contiguous=True).then_inc(mod_in, 16)
            for n in range(LOADS):
                part = slice(n * NT // LOADS, (n + 1) * NT // LOADS)
                sp.dma_start(x[:, part, :], x_v[:, part, :]).then_inc(x_in[n], 16)
            sp.wait_ge(pool_step, 2)
            sp.dma_start(dram["k_stack"][ROWS:STACK].rearrange("r h s -> (r h) s"), ones_rows[:]).then_inc(ones_stored, 16)
            with sp.Fori(0, NC // 2) as it:
                for u in range(2):
                    for n, (parts, order, stack, kept) in enumerate(
                            ((kparts, K_TERM, "k_stack", k_stored), (qparts, Q_TERM, "q_stack", q_stored))):
                        sp.wait_ge(parts_ready, it * 4 + (2 * u + n + 3))
                        for term, part in enumerate(order):
                            to = dram[stack][term * HD:(term + 1) * HD, :, bass.ds(it * 2 * C + u * C, C)]
                            sp.dma_start(to.rearrange("(m d) h s -> (d h) m s", m=KD), parts[:, u, part]
                                         ).then_inc(kept[u], 16)
            sp.wait_ge(ones_stored, 16)
            for u in range(2):
                sp.wait_ge(k_stored[u], 16 * STORES * (NC // 2 + 1))
                sp.wait_ge(q_stored[u], 16 * STORES * (NC // 2 + 1))

        @block.gpsimd
        def _(pool):
            nc.gpsimd.memset(ones_rows[:], 1.0).then_inc(pool_step, 1)
            nc.gpsimd.memset(ones[:], 1.0).then_inc(pool_step, 1)
            pool.wait_ge(pool_step, 2)
            nc.gpsimd.affine_select(out=keep["ident"][:], in_=ones[:], compare_op=ALU.is_equal, fill=0.0,
                                    base=0, pattern=[[-1, P]], channel_multiplier=1).then_inc(pool_step, 1)
            nc.gpsimd.affine_select(out=keep["ident_bf"][:], in_=ones[:], compare_op=ALU.is_equal, fill=0.0,
                                    base=0, pattern=[[-1, P]], channel_multiplier=1).then_inc(pool_step, 1)
            nc.gpsimd.memset(keep["mask_kq"][:], 0.0).then_inc(pool_step, 1)
            nc.gpsimd.memset(keep["mask_qk"][:], 0.0).then_inc(pool_step, 1)
            pool.wait_ge(pool_step, 6)
            nc.gpsimd.affine_select(out=keep["mask_kq"][:], in_=keep["mask_kq"][:], compare_op=ALU.is_ge, fill=MASKED,
                                    base=0, pattern=[[1, P]], channel_multiplier=-1).then_inc(pool_step, 1)
            nc.gpsimd.affine_select(out=keep["mask_qk"][:], in_=keep["mask_qk"][:], compare_op=ALU.is_ge, fill=MASKED,
                                    base=0, pattern=[[-1, P]], channel_multiplier=1).then_inc(pool_step, 1)
            pool.wait_ge(w_in, 16 * 6)
            for w, turned_w in ((wk, wk_turned), (wq, wq_turned)):
                for k in range(KD):
                    nc.gpsimd.tensor_copy(turned_w[:, k].rearrange("p (d h) -> p d h", h=H),
                                          w[:, k].rearrange("p (h d) -> p d h", h=H)).then_inc(pool_step, 1)
            pool.wait_ge(pool_step, 8 + 2 * KD)

        @block.scalar
        def _(act):
            act.dma_start(wmod[:], dram["wmod"].rearrange("(k p) n -> p k n", p=P),
                         allow_slow_non_contiguous=True).then_inc(mod_in, 16)
            for to, name in ((wk, "Wk"), (wq, "Wq"), (wv, "Wv")):
                act.dma_start(to[:], dram[name].rearrange("(k p) n -> p k n", p=P)).then_inc(w_in, 16)
            for to, name in ((bk, "bk"), (bq, "bq")):
                of = dram[name].rearrange("(h m d) -> d h m", h=H, m=KD)
                act.dma_start(to[:], of, allow_slow_non_contiguous=True).then_inc(w_in, 16)
            act.dma_start(bv_rows[:], dram["bv"].rearrange("(a n) -> a n", a=1).partition_broadcast(P)).then_inc(w_in, 16)
            act.wait_ge(mod_in, 32)
            nc.scalar.activation(silu[:, 0, :], ccol[:], ACT.Exp, scale=-1.0).then_inc(c_exp, 1)
            act.wait_ge(w_in, 16 * 6)
            nc.scalar.mul(bq_scaled[:], bq[:], HD ** -0.5).then_inc(act_step, 1)
            act.wait_ge(mod_ready, 2)
            nc.scalar.copy(mod_raw[:], ps_turn[:, 0, 0:8]).then_inc(act_step, 1)
            nc.scalar.copy(gate_raw[:], ps_k[:, 0, :].rearrange("p (a d) -> p a d", a=2)).then_inc(act_step, 1)
            act.wait_ge(var_ready, 1)
            nc.scalar.activation(std[:], var[:], ACT.Sqrt, bias=eps[:, 0:1]).then_inc(std_ready, 1)
            act.wait_ge(norm_ready, 1)
            act.wait_ge(cols_ready, 1)
            act.wait_ge(act_step, 3)
            act.sem_inc(h_ready, KD)
            act.sem_inc(kq_kept, 2 * KD)
            with act.Fori(0, NC // 2) as it:
                for u in range(2):
                    c = it * 2 + u
                    act.wait_ge(turned, c + 1)
                    for j in range(CB):
                        t = it * (2 * CB) + u * CB + j
                        nc.scalar.activation(xn[:, u, j, :], x[:, bass.ds(t, 1), :].rearrange("p a d -> p (a d)"),
                                             ACT.Identity, scale=rstd[:, bass.ds(t, 1)],
                                             bias=shift[:, bass.ds(t, 1)]).then_inc(xn_ready, 1)
                    act.wait_ge(v_ready, c + 1)
                    act.wait_ge(turned, c + 3)
                    for k in range(KD):
                        nc.scalar.activation(hT[:, u, k, :], ps_turn[:, k, :], ACT.Identity,
                                             scale=mod_cols[:, 2 + k:3 + k],
                                             bias=mod_cols[:, k:k + 1]).then_inc(h_ready, 1)
                    act.wait_ge(k_ready, c * 2 + 1)
                    act.wait_ge(parts_ready, c * 2 + 1)
                    for m in range(KD):
                        nc.scalar.activation(kf[:, m, :], ps_k[:, m, :], ACT.Identity,
                                             bias=bk[:, m:m + 1]).then_inc(kq_kept, 1)
                    act.wait_ge(k_ready, c * 2 + 2)
                    act.wait_ge(parts_ready, c * 2 + 2)
                    for m in range(KD):
                        nc.scalar.activation(qf[:, m, :], ps_q[:, m, :], ACT.Identity, scale=HD ** -0.5,
                                             bias=bq_scaled[:, m:m + 1]).then_inc(kq_kept, 1)

        @block.tensor
        def _(pe):
            pe.wait_ge(mod_in, 32)
            pe.wait_ge(silu_ready, 1)
            for n, start in enumerate((0, P, D, D + P, 3 * D, 3 * D + P, 4 * D, 4 * D + P)):
                for k in range(KD):
                    last = nc.tensor.matmul(ps_turn[:, 0, n:n + 1], wmod[:, k, start:start + P],
                                            silu[:, 3, k:k + 1], start=k == 0, stop=k == KD - 1)
            last.then_inc(mod_ready, 1)
            pe.wait_ge(rows_ready, KD)
            for n, start in enumerate((2 * D, 5 * D)):
                for k in range(KD):
                    last = nc.tensor.matmul(ps_k[:, 0, n * D:(n + 1) * D], silu_rows[:, k, :],
                                            wmod[:, k, start:start + D], start=k == 0, stop=k == KD - 1)
            last.then_inc(mod_ready, 1)
            pe.wait_ge(act_step, 3)
            pe.wait_ge(pool_step, 8 + 2 * KD)
            pe.wait_ge(w_in, 16 * 6)
            pe.sem_inc(turned, 2)
            pe.sem_inc(v_ready, 2)
            with pe.Fori(0, NC // 2) as it:
                for u in range(2):
                    c = it * 2 + u
                    pe.wait_ge(xn_ready, c * CB + CB)
                    pe.wait_ge(h_ready, c * KD + KD)
                    for k in range(KD):
                        for j in range(CB):
                            last = nc.tensor.transpose(ps_turn[:, k, j * P:(j + 1) * P],
                                                       xn[:, u, j, k * P:(k + 1) * P], ident[:])
                    last.then_inc(turned, 1)
                    pe.wait_ge(h_ready, c * KD + 2 * KD)
                    for n, (w, ps) in enumerate(((wk_turned, ps_k), (wq_turned, ps_q))):
                        pe.wait_ge(kq_kept, c * (2 * KD) + (n + 1) * KD)
                        for m in range(KD):
                            for k in range(KD):
                                last = nc.tensor.matmul(ps[:, m, :], w[:, k, m * P:(m + 1) * P], hT[:, u, k, :],
                                                        start=k == 0, stop=k == KD - 1)
                        last.then_inc(k_ready, 1)
                    pe.wait_ge(v_kept, c + 1)
                    for j in range(CB):
                        for k in range(KD):
                            last = nc.tensor.matmul(ps_v[:, j, :], hT[:, u, k, j * P:(j + 1) * P], wv[:, k, :],
                                                    start=k == 0, stop=k == KD - 1)
                    last.then_inc(v_ready, 1)

        @block.vector
        def _(dve):
            step = Tally(dve_step)
            step.inc(nc.vector.memset(eps[:], EPS))
            dve.wait_ge(c_exp, 1)
            step.inc(nc.vector.tensor_scalar_add(silu[:, 1, :], silu[:, 0, :], 1.0))
            step.wait(dve)
            step.inc(nc.vector.reciprocal(silu[:, 2, :], silu[:, 1, :]))
            step.wait(dve)
            nc.vector.tensor_tensor(silu[:, 3, :], silu[:, 2, :], ccol[:], ALU.mult).then_inc(silu_ready, 1)
            dve.wait_ge(silu_ready, 1)
            dve.wait_ge(pool_step, 2)
            for k in range(KD):
                nc.vector.tensor_scalar(silu_rows[:, k, :], ones[:], silu[:, 3, k:k + 1], None,
                                        ALU.mult).then_inc(rows_ready, 1)
            for n in range(LOADS):
                dve.wait_ge(x_in[n], 16)
                with dve.Fori(n * NT // LOADS, (n + 1) * NT // LOADS) as t:
                    nc.vector.bn_stats(stats[:, bass.ds(t, 1), :].rearrange("p a s -> p (a s)"),
                                       x[:, bass.ds(t, 1), :].rearrange("p a d -> p (a d)")).then_inc(stats_ready, 1)
            dve.wait_ge(stats_ready, NT)
            step.inc(nc.vector.tensor_tensor(mean2[:], stats[:, :, 1], stats[:, :, 4], ALU.add))
            step.inc(nc.vector.tensor_tensor(dev[:], stats[:, :, 1], stats[:, :, 4], ALU.subtract))
            step.inc(nc.vector.tensor_tensor(m2[:], stats[:, :, 2], stats[:, :, 5], ALU.add))
            step.wait(dve)
            step.inc(nc.vector.tensor_tensor(dev2[:], dev[:], dev[:], ALU.mult))
            step.inc(nc.vector.tensor_scalar(m2d[:], m2[:], 1.0 / D, None, ALU.mult))
            step.wait(dve)
            nc.vector.scalar_tensor_tensor(out=var[:], in0=dev2[:], scalar=0.25, in1=m2d[:], op0=ALU.mult,
                                           op1=ALU.add).then_inc(var_ready, 1)
            dve.wait_ge(std_ready, 1)
            step.inc(nc.vector.reciprocal(rstd[:], std[:]))
            step.wait(dve)
            nc.vector.scalar_tensor_tensor(out=shift[:], in0=mean2[:], scalar=-0.5, in1=rstd[:], op0=ALU.mult,
                                           op1=ALU.mult).then_inc(norm_ready, 1)
            dve.wait_ge(act_step, 3)
            step.inc(nc.vector.tensor_copy(mod_cols[:], mod_raw[:]))
            step.wait(dve)
            for n in (2, 6):
                step.inc(nc.vector.tensor_scalar_add(mod_cols[:, n:n + 2], mod_raw[:, n:n + 2], 1.0))
            step.wait(dve)
            step.inc(nc.vector.tensor_scalar(gate_sign[:], gate_raw[:], 0.0, 2.0, ALU.is_ge, ALU.mult))
            step.inc(nc.vector.scalar_tensor_tensor(out=gate_abs[:], in0=gate_raw[:], scalar=-1.0, in1=gate_raw[:],
                                                    op0=ALU.mult, op1=ALU.max))
            step.wait(dve)
            step.inc(nc.vector.tensor_scalar(gate_size[:], gate_abs[:], 0.25, None, ALU.max))
            step.wait(dve)
            nc.vector.scalar_tensor_tensor(out=gates[:], in0=gate_sign[:], scalar=-1.0, in1=gate_size[:],
                                           op0=ALU.add, op1=ALU.mult).then_inc(cols_ready, 1)
            dve.wait_ge(w_in, 16 * 6)
            dve.sem_inc(parts_ready, 2)
            dve.sem_inc(v_kept, 1)
            for u in range(2):
                dve.sem_inc(k_stored[u], 16 * STORES)
                dve.sem_inc(q_stored[u], 16 * STORES)
            first = step.n
            per_chunk = 6
            with dve.Fori(0, NC // 2) as it:
                for u in range(2):
                    c = it * 2 + u
                    step = Tally(dve_step, c * per_chunk + first)
                    for n, (full, parts, kept) in enumerate(((kf, kparts, k_stored), (qf, qparts, q_stored))):
                        dve.wait_ge(kq_kept, c * (2 * KD) + (2 * KD + (n + 1) * KD))
                        dve.wait_ge(kept[u], it * (16 * STORES) + 16 * STORES)
                        step.inc(nc.vector.tensor_copy(parts[:, u, 0], full[:]))
                        step.wait(dve)
                        step.inc(nc.vector.tensor_tensor(full[:], full[:], parts[:, u, 0], ALU.subtract))
                        step.wait(dve)
                        step.inc(nc.vector.tensor_copy(parts[:, u, 1], full[:]))
                        step.wait(dve)
                        nc.vector.tensor_tensor(parts[:, u, 2], full[:], parts[:, u, 1],
                                                ALU.subtract).then_inc(parts_ready, 1)
                    assert step.n == per_chunk
                    dve.wait_ge(v_ready, c + 3)
                    nc.vector.tensor_tensor(v[:, bass.ds(it * (2 * CB) + u * CB, CB), :], ps_v[:],
                                            bv_rows[:].unsqueeze(1).to_broadcast([P, CB, D]),
                                            ALU.add).then_inc(v_kept, 1)
            dve.wait_ge(v_kept, NC + 1)

def over_tiles(eng, body):
    body(0, False)
    with eng.Fori(1, NC - 1) as tile:
        body(tile, False)
    body(NC - 1, True)


def score_shifts(nc, dram, keep):
    with ExitStack() as ctx:
        def sb(name, shape, dt):
            return ctx.enter_context(nc.sbuf_tensor(name, shape, dt))

        def psum(name, shape, dt):
            return ctx.enter_context(nc.psum_tensor(name, shape, dt))

        def sem(name):
            return ctx.enter_context(nc.semaphore(name))

        ident = keep["ident"]
        BLOCKS = 8
        PARTS = NT // BLOCKS
        W = BLOCKS * P
        HH = H // KD
        RING = 4
        SETS = H * NT // P
        high = [sb(f"sh_high_{n}", [P, KD, S], BF16) for n in "kq"]
        square = [sb(f"sh_square_{n}", [P, 2, KD, W], BF16) for n in "kq"]
        ones = sb("sh_ones", [P, P], F32)
        own = sb("sh_own", [P, HH], BF16)
        first_keys = sb("sh_first_keys", [P, KD, HH, FIRST_KEYS], BF16)
        low = sb("sh_low", [P, H, NT], F32)
        bound2 = sb("sh_bound2", [P, H, NT], F32)
        bound = sb("sh_bound", [P, H, NT], F32)
        width = sb("sh_width", [P, H, NT], F32)
        shift = sb("sh_shift", [P, H, NT], F32)
        longest = sb("sh_longest", [P, H], F32)
        longest_all = sb("sh_longest_all", [H, 1], F32)
        longest_diag = sb("sh_longest_diag", [H, H], F32)
        widest = sb("sh_widest", [P, 1], F32)
        widest_all = sb("sh_widest_all", [1, 1], F32)
        too_wide = sb("sh_too_wide", [1, 1], F32)
        rest = sb("sh_rest", [P, SETS, P], F32)
        parts = sb("sh_parts", [P, 3, SETS, P], BF16)

        ps_low = psum("sh_ps_low", [P, RING, H, FIRST_KEYS], F32)
        ps_norm = [psum(f"sh_ps_norm_{n}", [P, H, NT], F32) for n in "kq"]
        ps_small = psum("sh_ps_small", [P, C], F32)
        ps_turn = psum("sh_ps_turn", [P, SETS, P], F32)

        high_in = [[sem(f"sh_{n}_in_{m}") for m in range(PARTS)] for n in "kq"]
        pool_step = sem("sh_pool_step")
        keys_ready = sem("sh_keys_ready")
        squared = sem("sh_squared")
        low_scored = sem("sh_low_scored")
        low_kept = sem("sh_low_kept")
        norms_ready = sem("sh_norms_ready")
        dve_step = sem("sh_dve_step")
        small_ready = sem("sh_small_ready")
        bound2_ready = sem("sh_bound2_ready")
        bound_ready = sem("sh_bound_ready")
        shift_ready = sem("sh_shift_ready")
        turned = sem("sh_turned")
        parts_ready = sem("sh_parts_ready")
        stored = sem("sh_stored")
        block = ctx.enter_context(nc.Block())

        def load(eng, n, stack):
            term = (K_TERM, Q_TERM)[n].index(0)
            for part in range(PARTS):
                for m in range(KD):
                    of = dram[stack][term * HD:(term + 1) * HD, m * HH:(m + 1) * HH, part * W:(part + 1) * W]
                    eng.dma_start(high[n][:, m, part * W:(part + 1) * W], of.rearrange("d h s -> h d s")
                                  ).then_inc(high_in[n][part], 16)

        @block.sync
        def _(sp):
            load(sp, 1, "q_stack")
            for part in range(3):
                sp.wait_ge(parts_ready, part + 1)
                to = dram["q_stack"][ROWS + part].rearrange("h (t s) -> (h t) s", s=P)
                sp.dma_start(to.rearrange("(n p) s -> p n s", p=P), parts[:, part]).then_inc(stored, 16)
            sp.wait_ge(stored, 16 * 3)

        @block.gpsimd
        def _(pool):
            nc.gpsimd.memset(own[:], 1.0).then_inc(pool_step, 1)
            nc.gpsimd.memset(ones[:], 1.0).then_inc(pool_step, 1)
            pool.wait_ge(pool_step, 1)
            nc.gpsimd.affine_select(out=own[:], in_=own[:], compare_op=ALU.is_ge, fill=0.0, base=0,
                                    pattern=[[-HD, HH]], channel_multiplier=1).then_inc(pool_step, 1)
            pool.wait_ge(pool_step, 3)
            nc.gpsimd.affine_select(out=own[:], in_=own[:], compare_op=ALU.is_ge, fill=0.0, base=HD - 1,
                                    pattern=[[HD, HH]], channel_multiplier=-1).then_inc(pool_step, 1)

        @block.scalar
        def _(act):
            load(act, 0, "k_stack")
            act.dma_start(keep["k_rows"][:, 0:GH * S], dram["k_stack"][:, 0:GH, :]).then_inc(keep["k_in"], 16)
            for part in range(PARTS):
                for n in range(2):
                    act.wait_ge(high_in[n][part], 16 * KD)
                    if part >= 2:
                        act.wait_ge(norms_ready, part - 1)
                    nc.scalar.activation(square[n][:, part % 2], high[n][:, :, part * W:(part + 1) * W],
                                         ACT.Square).then_inc(squared, 1)
            act.wait_ge(bound2_ready, 1)
            nc.scalar.activation(bound[:], bound2[:], ACT.Sqrt).then_inc(bound_ready, 1)

        @block.tensor
        def _(pe):
            pe.wait_ge(keys_ready, KD)
            for t in range(NT):
                part = t // BLOCKS
                if t % BLOCKS == 0:
                    pe.wait_ge(high_in[1][part], 16 * KD)
                if t >= RING:
                    pe.wait_ge(low_kept, t - RING + 1)
                for m in range(KD):
                    ins = nc.tensor.matmul(ps_low[:, t % RING, m * HH:(m + 1) * HH, :], high[1][:, m, t * P:(t + 1) * P],
                                           first_keys[:, m], start=True, stop=True)
                ins.then_inc(low_scored, 1)
                if t % BLOCKS == 0:
                    pe.wait_ge(squared, 2 * part + 2)
                for n in range(2):
                    for m in range(KD):
                        ins = nc.tensor.matmul(ps_norm[n][:, m * HH:(m + 1) * HH, t],
                                               square[n][:, part % 2, m, t % BLOCKS * P:(t % BLOCKS + 1) * P],
                                               own[:], start=True, stop=True)
                if t % BLOCKS == BLOCKS - 1:
                    ins.then_inc(norms_ready, 1)
            pe.wait_ge(dve_step, 1)
            nc.tensor.transpose(ps_small[0:H, 0:P], longest[:], ident[:]).then_inc(small_ready, 1)
            pe.wait_ge(dve_step, 3)
            nc.tensor.matmul(ps_small[:, P:P + H], ones[0:H, :], longest_diag[:], start=True,
                             stop=True).then_inc(small_ready, 1)
            pe.wait_ge(shift_ready, 1)
            flat = shift[:].rearrange("p h t -> p (h t)")
            for n in range(SETS):
                ins = nc.tensor.transpose(ps_turn[:, n, :], flat[:, n * P:(n + 1) * P], ident[:])
            ins.then_inc(turned, 1)
            pe.wait_ge(shift_ready, 2)
            nc.tensor.transpose(ps_small[0:1, 2 * P:3 * P], widest[:], ident[:]).then_inc(small_ready, 1)

        @block.vector
        def _(dve):
            dve.wait_ge(high_in[0][0], 16 * KD)
            dve.wait_ge(pool_step, 4)
            for m in range(KD):
                nc.vector.tensor_tensor(first_keys[:, m],
                                        high[0][:, m, 0:FIRST_KEYS].unsqueeze(1).to_broadcast([P, HH, FIRST_KEYS]),
                                        own[:].unsqueeze(2).to_broadcast([P, HH, FIRST_KEYS]),
                                        ALU.mult).then_inc(keys_ready, 1)
            for t in range(NT):
                dve.wait_ge(low_scored, t + 1)
                nc.vector.tensor_reduce(low[:, :, t], ps_low[:, t % RING], AX.X, ALU.max).then_inc(low_kept, 1)
            dve.wait_ge(norms_ready, PARTS)
            step = Tally(dve_step)
            step.inc(nc.vector.tensor_reduce(longest[:], ps_norm[0][:], AX.X, ALU.max))
            dve.wait_ge(small_ready, 1)
            step.inc(nc.vector.tensor_reduce(longest_all[:], ps_small[0:H, 0:P], AX.X, ALU.max))
            step.wait(dve)
            step.inc(nc.vector.tensor_scalar(longest_diag[:], ident[0:H, 0:H], longest_all[:, 0:1], None, ALU.mult))
            dve.wait_ge(small_ready, 2)
            step.inc(nc.vector.tensor_copy(longest[:], ps_small[:, P:P + H]))
            step.wait(dve)
            nc.vector.scalar_tensor_tensor(out=bound2[:], in0=ps_norm[1][:], scalar=SLACK * SLACK,
                                           in1=longest[:].unsqueeze(2).to_broadcast([P, H, NT]),
                                           op0=ALU.mult, op1=ALU.mult).then_inc(bound2_ready, 1)
            dve.wait_ge(low_kept, NT)
            dve.wait_ge(bound_ready, 1)
            step.inc(nc.vector.scalar_tensor_tensor(out=width[:], in0=bound[:], scalar=-ROOM_UP, in1=low[:],
                                                    op0=ALU.add, op1=ALU.max))
            step.wait(dve)
            nc.vector.tensor_scalar(shift[:], width[:], -1.0, None, ALU.mult).then_inc(shift_ready, 1)
            dve.wait_ge(shift_ready, 1)
            step.inc(nc.vector.tensor_tensor(width[:], bound[:], low[:], ALU.subtract))
            step.wait(dve)
            nc.vector.tensor_reduce(widest[:], width[:].rearrange("p h t -> p (h t)"), AX.X,
                                    ALU.max).then_inc(shift_ready, 1)
            dve.wait_ge(turned, 1)
            nc.vector.tensor_copy(parts[:, 0], ps_turn[:]).then_inc(parts_ready, 1)
            dve.wait_ge(parts_ready, 1)
            step.inc(nc.vector.tensor_tensor(rest[:], ps_turn[:], parts[:, 0], ALU.subtract))
            step.wait(dve)
            nc.vector.tensor_copy(parts[:, 1], rest[:]).then_inc(parts_ready, 1)
            dve.wait_ge(parts_ready, 2)
            nc.vector.tensor_tensor(parts[:, 2], rest[:], parts[:, 1], ALU.subtract).then_inc(parts_ready, 1)
            dve.wait_ge(small_ready, 3)
            step.inc(nc.vector.tensor_reduce(widest_all[:], ps_small[0:1, 2 * P:3 * P], AX.X, ALU.max))
            step.wait(dve)
            step.inc(nc.vector.tensor_scalar(too_wide[:], widest_all[:], ROOM_UP + ROOM_DOWN, None,
                                             ALU.is_gt))
            step.wait(dve)
            step.inc(nc.vector.tensor_copy(keep["too_wide"][:], too_wide[:]))
            step.wait(dve)


def row_maxima(nc, dram, keep):
    with ExitStack() as ctx:
        def sb(name, shape, dt):
            return ctx.enter_context(nc.sbuf_tensor(name, shape, dt))

        def psum(name, shape, dt):
            return ctx.enter_context(nc.psum_tensor(name, shape, dt))

        def sem(name):
            return ctx.enter_context(nc.semaphore(name))

        ident, ident_bf, mask = keep["ident"], keep["ident_bf"], keep["mask_qk"]
        U = GH * CB
        BANKS = 4
        CUT = 5
        k_rows = sb("mx_k_rows", [ROWS, GH, S], BF16)
        q_rows = sb("mx_q_rows", [ROWS, GH, C], BF16)
        best = sb("mx_best", [P, U], F32)
        edge = sb("mx_edge", [P, GH], F32)
        chunk = sb("mx_chunk", [P, U], F32)
        neg = sb("mx_neg", [U, P], F32)
        parts = sb("mx_parts", [U, 3, P], BF16)
        ps = psum("mx_ps", [P, BANKS, C], F32)
        ps_turn = psum("mx_turn", [U, C], F32)

        k_in = sem("mx_k_in")
        q_in = sem("mx_q_in")
        scored = sem("mx_scored")
        reduced = sem("mx_reduced")
        joined = sem("mx_joined")
        turned = sem("mx_turned")
        cut = sem("mx_cut")
        stored = sem("mx_stored")
        written = sem("mx_written")

        def units_before(tile):
            return tile * (U // 2 + GH) + tile * tile * (U // 2)

        GROUP_UNITS = units_before(NC) - GH

        def joins_before(tile):
            return (tile * tile + tile)

        GROUP_JOINS = joins_before(NC) - 2

        block = ctx.enter_context(nc.Block())

        @block.sync
        def _(sp):
            sp.sem_inc(stored, 16)
            needed = sp.value_load(keep["too_wide"][0:1, 0:1], min_val=0, max_val=1)
            with sp.If(needed > 0):
                with sp.Fori(0, G) as g:
                    with sp.Fori(0, NC) as tile:
                        r = g * NC + tile
                        sp.wait_ge(turned, r + 1)
                        sp.dma_start(q_rows[:], dram["q_stack"][0:ROWS, bass.ds(g * GH, GH),
                                                                bass.ds(tile * C, C)]).then_inc(q_in, 16)
                        sp.dma_start(k_rows[:], dram["k_stack"][0:ROWS, bass.ds(g * GH, GH), :]).then_inc(k_in, 16)
                        sp.wait_ge(cut, r * CUT + CUT + 1)
                        for part in range(3):
                            to = dram["q_stack"][ROWS + part, bass.ds(g * GH, GH), bass.ds(tile * C, C)]
                            sp.dma_start(to.rearrange("h (j q) -> h j q", q=P), parts[:, part, :]).then_inc(stored, 16)
                        sp.wait_ge(stored, r * 48 + 64)
                        sp.sem_inc(written, 1)

        @block.tensor
        def _(pe):
            pe.sem_inc(turned, 1)
            needed = pe.value_load(keep["too_wide"][0:1, 0:1], min_val=0, max_val=1)
            with pe.If(needed > 0):
                with pe.Fori(0, G) as g:
                    def tile_scores(tile, last):
                        base = pe.snap(g * GROUP_UNITS + units_before(tile))
                        r = g * NC + tile
                        pe.wait_ge(q_in, r * 16 + 16)
                        pe.wait_ge(k_in, r * 16 + 16)
                        unit = 0
                        for h in range(GH):
                            for j in range(CB):
                                pe.wait_ge(reduced, base + (unit + 1))
                                out = ps[:, unit % BANKS, :]
                                width = min(j + 2, CB) * P
                                masked = j + 1 < CB
                                ins = nc.tensor.matmul(out[:, 0:width], q_rows[:, h, j * P:(j + 1) * P],
                                                       k_rows[:, h, bass.ds(tile * C, width)],
                                                       start=True, stop=not masked)
                                if masked:
                                    ins = nc.tensor.matmul(out[:, width - P:width], ident_bf[:], mask[:],
                                                           start=False, stop=True)
                                ins.then_inc(scored, 1)
                                unit += 1
                        if not last:
                            for h in range(GH):
                                pe.wait_ge(reduced, base + (unit + 1))
                                out = ps[:, unit % BANKS, 0:P]
                                nc.tensor.matmul(out, q_rows[:, h, C - P:C],
                                                 k_rows[:, h, bass.ds(tile * C + C, P)], start=True, stop=False)
                                nc.tensor.matmul(out, ident_bf[:], mask[:], start=False, stop=True).then_inc(scored, 1)
                                unit += 1
                        if not isinstance(tile, int) or tile > 0:
                            with pe.Fori(0, tile) as kc:
                                for u in range(U):
                                    pe.wait_ge(reduced, base + kc * U + (unit + u + 1))
                                    h, j = u // CB, u % CB
                                    nc.tensor.matmul(ps[:, (unit + u) % BANKS, :], q_rows[:, h, j * P:(j + 1) * P],
                                                     k_rows[:, h, bass.ds(kc * C, C)], start=True,
                                                     stop=True).then_inc(scored, 1)
                        pe.wait_ge(joined, g * GROUP_JOINS + joins_before(tile) + tile * 2 + (0 if last else 2))
                        pe.wait_ge(cut, r * CUT + 1)
                        nc.tensor.transpose(ps_turn[:, 0:P], best[:], ident[:]).then_inc(turned, 1)

                    over_tiles(pe, tile_scores)

        @block.vector
        def _(dve):
            dve.sem_inc(reduced, BANKS)
            dve.sem_inc(cut, 1)
            needed = dve.value_load(keep["too_wide"][0:1, 0:1], min_val=0, max_val=1)
            with dve.If(needed > 0):
                with dve.Fori(0, G) as g:
                    def tile_maxima(tile, last):
                        base = dve.snap(g * GROUP_UNITS + units_before(tile))
                        joins = dve.snap(g * GROUP_JOINS + joins_before(tile))
                        r = g * NC + tile
                        dve.wait_ge(turned, r + 1)
                        unit = 0
                        for h in range(GH):
                            for j in range(CB):
                                dve.wait_ge(scored, base + (unit + 1))
                                width = min(j + 2, CB) * P
                                nc.vector.tensor_reduce(best[:, unit:unit + 1], ps[:, unit % BANKS, 0:width], AX.X,
                                                        ALU.max).then_inc(reduced, 1)
                                unit += 1
                        if not last:
                            for h in range(GH):
                                dve.wait_ge(scored, base + (unit + 1))
                                nc.vector.tensor_reduce(edge[:, h:h + 1], ps[:, unit % BANKS, 0:P], AX.X,
                                                        ALU.max).then_inc(reduced, 1)
                                unit += 1
                            dve.wait_ge(reduced, base + (unit + BANKS))
                            bottom = best[:].rearrange("p (h j) -> p h j", h=GH)[:, :, CB - 1]
                            nc.vector.tensor_tensor(bottom, bottom, edge[:], ALU.max).then_inc(joined, 2)
                        if not isinstance(tile, int) or tile > 0:
                            with dve.Fori(0, tile) as kc:
                                dve.wait_ge(joined, joins + kc * 2 + (0 if last else 2))
                                for u in range(U):
                                    dve.wait_ge(scored, base + kc * U + (unit + u + 1))
                                    nc.vector.tensor_reduce(chunk[:, u:u + 1], ps[:, (unit + u) % BANKS, :], AX.X,
                                                            ALU.max).then_inc(reduced, 1)
                                dve.wait_ge(reduced, base + kc * U + (unit + U + BANKS))
                                nc.vector.tensor_tensor(best[:], best[:], chunk[:], ALU.max).then_inc(joined, 2)
                        dve.wait_ge(turned, r + 2)
                        dve.wait_ge(stored, r * 48 + 16)
                        step = Tally(cut, r * CUT + 1)
                        step.inc(nc.vector.tensor_scalar(neg[:], ps_turn[:, 0:P], -1.0, None, ALU.mult))
                        step.wait(dve)
                        step.inc(nc.vector.tensor_copy(parts[:, 0], neg[:]))
                        step.wait(dve)
                        step.inc(nc.vector.tensor_tensor(neg[:], neg[:], parts[:, 0], ALU.subtract))
                        step.wait(dve)
                        step.inc(nc.vector.tensor_copy(parts[:, 1], neg[:]))
                        step.wait(dve)
                        step.inc(nc.vector.tensor_tensor(parts[:, 2], neg[:], parts[:, 1], ALU.subtract))
                        assert step.n == CUT

                    over_tiles(dve, tile_maxima)


def attention(nc, dram, keep):
    with ExitStack() as ctx:
        def sb(name, shape, dt):
            return ctx.enter_context(nc.sbuf_tensor(name, shape, dt))

        def psum(name, shape, dt):
            return ctx.enter_context(nc.psum_tensor(name, shape, dt))

        def sem(name):
            return ctx.enter_context(nc.semaphore(name))

        ident, ident_bf, mask, v, mixed = (keep[n] for n in ("ident", "ident_bf", "mask_kq", "v", "mixed"))
        CT = 32
        RING = CB
        FAR = RING
        HALF = GH // 2
        LAG = 2

        k_rows = keep["k_rows"]
        q_rows = sb("at_q_rows", [STACK, 2 * GH * C], BF16)
        probs = sb("at_probs", [P, RING + 1, GH, C], F32)
        v_now = sb("at_v_now", [P, RING + 1, GH, CT], F32)
        out_T = sb("at_out_T", [P, C], F32)
        inv = sb("at_inv", [P, CB, GH], F32)
        warm = sb("at_warm", [P, 1], F32)
        CLEARED = (TILES + 1) * P // NC
        zeros = sb("at_zeros", [P, CLEARED // P * D], F32)

        ps_s = psum("at_scores", [P, 2, HALF, C], F32)
        ps_o = psum("at_out", [P, C], F32)
        ps_t = psum("at_turn", [P, CB, P], F32)

        k_in = keep["k_in"]
        q_in = sem("at_q_in")
        v_zeroed = sem("at_v_zeroed")
        ready = sem("at_ready")
        scored = sem("at_scored")
        exped = sem("at_exped")
        slot_free = sem("at_slot_free")
        q_there = sem("at_q_there")
        v_copied = sem("at_v_copied")
        pv_done = sem("at_pv_done")
        out_read = sem("at_out_read")
        turned = sem("at_turned")
        inverted = sem("at_inverted")
        normed = sem("at_normed")
        zeroed = sem("at_zeroed")
        queue_clear = sem("at_queue_clear")

        def steps_before(tile):
            return tile * tile * (CB // 2) + tile * (CB // 2 + 1)

        GROUP_STEPS = steps_before(NC) - 1

        def first_steps(last):
            steps = [(j, (j - 1) * P, (CB - j) if j < CB else FAR) for j in range(CB, 0, -1)]
            return steps[1 if last else 0:] + [(0, 0, 0)]

        block = ctx.enter_context(nc.Block())

        @block.sync
        def _(sp):
            def load_keys(g, half):
                sp.dma_start(k_rows[:, bass.ds(half * (GH * S), GH * S)],
                             dram["k_stack"][:, bass.ds(g * GH, GH), :]).then_inc(k_in, 16)

            def load_queries(g, tile, half):
                sp.wait_ge(turned, g * NC + tile + 1)
                sp.dma_start(q_rows[:, bass.ds(half * (GH * C), GH * C)],
                             dram["q_stack"][:, bass.ds(g * GH, GH), bass.ds(tile * C, C)]).then_inc(q_in, 16)
                sp.wait_ge(q_in, g * (NC * 16) + tile * 16 + 16)
                sp.sem_inc(q_there, 1)

            def clear_rows(tile):
                to = dram["queue"][bass.ds(tile * CLEARED, CLEARED), :]
                sp.dma_start(to.rearrange("(p r) d -> p (r d)", p=P), zeros[:]).then_inc(queue_clear, 16)

            def group(g, last, first=False):
                for tile in range(2):
                    load_queries(g, tile, tile)
                    if first:
                        sp.wait_ge(zeroed, 1)
                        clear_rows(tile)
                if not last:
                    sp.wait_ge(k_in, g * 16 + 16)
                    load_keys(g + 1, (g + 1) % 2)
                with sp.Fori(1, NC // 2) as pair:
                    for u in range(2):
                        load_queries(g, pair * 2 + u, u)
                        if first:
                            clear_rows(pair * 2 + u)

            group(0, False, first=True)
            with sp.Fori(1, G - 1) as g:
                group(g, False)
            group(G - 1, True)
            sp.wait_ge(k_in, G * 16)
            sp.wait_ge(queue_clear, 16 * NC)

        @block.gpsimd
        def _(pool):
            nc.gpsimd.memset(v_now[:], 0.0).then_inc(v_zeroed, 1)
            pool.wait_ge(v_zeroed, 1)
            nc.gpsimd.memset(v_now[:, :, :, HD:HD + 1], 1.0).then_inc(ready, 1)
            pool.wait_ge(ready, 3)
            pool.sem_inc(v_copied, LAG)
            with pool.Fori(0, G) as g:
                def copy(n, kb, slot):
                    pool.wait_ge(pv_done, n + 1)
                    pool.sem_inc(slot_free, 1)
                    nc.gpsimd.tensor_copy(v_now[:, slot, :, 0:HD],
                                          v[:, bass.ds(kb, 1), bass.ds(g * (GH * HD), GH * HD)].rearrange(
                                              "p a (h d) -> p (a h) d", h=GH)).then_inc(v_copied, 1)

                def tile_values(tile, last):
                    n = pool.snap(g * GROUP_STEPS + steps_before(tile))
                    steps = first_steps(last)
                    for i, (j, _, slot) in enumerate(steps):
                        copy(n + i, tile * CB + j if j else 0, slot)
                    if not isinstance(tile, int) or tile > 0:
                        with pool.Fori(0, tile) as it:
                            for u in range(CB):
                                copy(n + it * CB + (len(steps) + u), it * CB + (u + 1), (u + 1) % RING)

                over_tiles(pool, tile_values)

        @block.tensor
        def _(pe):
            def scores(n, half, kb, first, place, edge):
                k_at, q_at = place
                pe.wait_ge(exped, n * 2 + (half + 3))
                for i in range(HALF):
                    h = half * HALF + i
                    ins = nc.tensor.matmul(ps_s[:, half, i, first:C],
                                           k_rows[:, bass.ds(k_at + kb * P + h * S, P)],
                                           q_rows[:, bass.ds(q_at + (h * C + first), C - first)],
                                           start=True, stop=not edge)
                    if edge:
                        ins = nc.tensor.matmul(ps_s[:, half, i, first:first + P], ident_bf[:], mask[:],
                                               start=False, stop=True)
                ins.then_inc(scored, 1)

            def product(n, first, slot, start):
                pe.wait_ge(v_copied, n + 1)
                pe.wait_ge(exped, n * 2 + 2)
                for h in range(GH):
                    ins = nc.tensor.matmul(ps_o[h * CT:(h + 1) * CT, first:C], v_now[:, slot, h, :],
                                           probs[:, slot, h, first:C], start=start, stop=False,
                                           skip_group_check=True)
                ins.then_inc(pv_done, 1)

            def transposes(r):
                pe.wait_ge(out_read, r + 1)
                pe.wait_ge(normed, r + 1)
                for j in range(CB):
                    ins = nc.tensor.transpose(ps_t[:, j, :], out_T[:, j * P:(j + 1) * P], ident[:])
                ins.then_inc(turned, 1)

            pe.wait_ge(ready, 3)
            pe.sem_inc(turned, 1)
            pe.sem_inc(pv_done, LAG)
            for h in range(GH):
                nc.tensor.matmul(ps_o[h * CT:(h + 1) * CT, :], v_now[:, 0, h, :], probs[:, 0, h, :], start=True,
                                 stop=False, skip_group_check=True)
            with pe.Fori(0, G) as g:
                def tile_steps(tile, last):
                    n = pe.snap(g * GROUP_STEPS + steps_before(tile))
                    r = g * NC + tile
                    place = (pe.snap((g % 2) * (GH * S)),
                             (tile % 2) * (GH * C) if isinstance(tile, int) else pe.snap((tile % 2) * (GH * C)))
                    pe.wait_ge(k_in, g * 16 + 16)
                    pe.wait_ge(q_in, r * 16 + 16)
                    steps = first_steps(last)
                    waiting = [(0, RING - 1, False), (0, 0, False)]
                    for i, (j, first, slot) in enumerate(steps):
                        kb = tile * CB + j if j else 0
                        scores(n + i, 0, kb, first, place, j > 0)
                        if i == LAG:
                            pe.wait_ge(out_read, r + 1)
                        product(n + i, *waiting.pop(0))
                        scores(n + i, 1, kb, first, place, j > 0)
                        if i == LAG + 1:
                            transposes(r)
                        waiting.append((first, slot, i == 0))
                    if not isinstance(tile, int) or tile > 0:
                        with pe.Fori(0, tile) as it:
                            for u in range(CB):
                                m = n + it * CB + (len(steps) + u)
                                scores(m, 0, it * CB + (u + 1), 0, place, False)
                                product(m, 0, (u + 1 - LAG) % RING, False)
                                scores(m, 1, it * CB + (u + 1), 0, place, False)

                over_tiles(pe, tile_steps)
            product(G * GROUP_STEPS, 0, RING - 1, False)
            product(G * GROUP_STEPS + 1, 0, 0, False)
            transposes(G * NC)

        @block.scalar
        def _(act):
            nc.scalar.activation(warm[:], ident[:, 0:1], ACT.Exp).then_inc(exped, 1)
            act.sem_inc(exped, 3)
            with act.Fori(0, G) as g:
                def exponentials(n, first, slot):
                    for half in range(2):
                        act.wait_ge(scored, n * 2 + (half + 1))
                        if half == 0:
                            act.wait_ge(pv_done, n + 1)
                        heads = slice(half * HALF, (half + 1) * HALF)
                        nc.scalar.activation(probs[:, slot, heads, first:C], ps_s[:, half, :, first:C],
                                             ACT.Exp).then_inc(exped, 1)

                def tile_exponentials(tile, last):
                    n = act.snap(g * GROUP_STEPS + steps_before(tile))
                    steps = first_steps(last)
                    for i, (_, first, slot) in enumerate(steps):
                        exponentials(n + i, first, slot)
                    if not isinstance(tile, int) or tile > 0:
                        with act.Fori(0, tile) as it:
                            for u in range(CB):
                                exponentials(n + it * CB + (len(steps) + u), 0, (u + 1) % RING)

                over_tiles(act, tile_exponentials)

        @block.vector
        def _(dve):
            nc.vector.memset(probs[:, 0], 0.0).then_inc(ready, 1)
            nc.vector.memset(probs[:, RING - 1], 0.0).then_inc(ready, 1)
            nc.vector.memset(out_T[:], 0.0).then_inc(out_read, 1)
            nc.vector.memset(zeros[:], 0.0).then_inc(zeroed, 1)
            dve.sem_inc(normed, 2)
            with dve.Fori(0, G) as g:
                def tile_out(tile, last):
                    n = dve.snap(g * GROUP_STEPS + steps_before(tile))
                    r = g * NC + tile
                    dve.wait_ge(pv_done, n + tile * CB + (len(first_steps(last)) + 2 * LAG))
                    dve.wait_ge(turned, r + 2)
                    nc.vector.tensor_copy(out_T[:], ps_o[:]).then_inc(out_read, 1)
                    dve.wait_ge(turned, r + 3)
                    heads = ps_t[:].rearrange("p j (h c) -> p j h c", h=GH)
                    nc.vector.reciprocal(inv[:], heads[:, :, :, HD]).then_inc(inverted, 1)
                    dve.wait_ge(inverted, r + 1)
                    to = mixed[:, bass.ds(tile * CB, CB), bass.ds(g * (GH * HD), GH * HD)]
                    nc.vector.tensor_tensor(to.rearrange("p j (h d) -> p j h d", h=GH), heads[:, :, :, 0:HD],
                                            inv[:].unsqueeze(3).to_broadcast([P, CB, GH, HD]),
                                            ALU.mult).then_inc(normed, 1)

                over_tiles(dve, tile_out)


def route(nc, dram, keep):
    with ExitStack() as ctx:
        def sb(name, shape, dt):
            return ctx.enter_context(nc.sbuf_tensor(name, shape, dt))

        def psum(name, shape, dt):
            return ctx.enter_context(nc.psum_tensor(name, shape, dt))

        def sem(name):
            return ctx.enter_context(nc.semaphore(name))

        ident, gates, mod_cols, mixed = (keep[n] for n in ("ident", "gates", "mod_cols", "mixed"))
        rows = keep["w2"][:, E // 2:].rearrange("p e f d -> p (e f) d")
        m_now = keep["w2"][:, E // 2 - 2].rearrange("p (u j) d -> p u j d", u=2)
        spare = keep["w2"][:, E // 2 - 1]
        wo = sb("rt_wo", [P, KD, D], F32)
        gate_w = sb("rt_gate_w", [P, KD, E], F32)
        gate_b = sb("rt_gate_b", [P, E], F32)
        bo_gated = sb("rt_bo_gated", [P, D], F32)
        b1_rows = sb("rt_b1_rows", [E * FF, P], F32)
        x_now = sb("rt_x_now", [P, 2, CB, D], F32)
        xs = sb("rt_xs", [P, CB, D], F32)
        aT = sb("rt_aT", [P, KD, C], F32)
        hT = sb("rt_hT", [P, KD, C], F32)
        gated = sb("rt_gated", [P, CB, D], F32)
        stats = sb("rt_stats", [P, CB, 6], F32)
        mean_var = sb("rt_mean_var", [P, CB, 2], F32)
        eps = sb("rt_eps", [P, 1], F32)
        std = sb("rt_std", [P, CB], F32)
        rstd = sb("rt_rstd", [P, CB], F32)
        shift = sb("rt_shift", [P, CB], F32)
        score = sb("rt_score", [P, NT, E], F32)
        masked, equal, *pick = (spare[:, i].rearrange("p (t e) -> p t e", e=E) for i in range(4))
        top = [sb(f"rt_top_{i}", [P, NT], F32) for i in range(2)]
        least = sb("rt_least", [P, NT], F32)
        order = sb("rt_order", [P, E], F32)
        both = sb("rt_both", [P, NT, E], BF16)
        before_bf = sb("rt_before", [P, P], BF16)
        ones_bf = sb("rt_ones", [P, P], BF16)
        ex = sb("rt_ex", [P, NT], F32)
        den = sb("rt_den", [P, NT], F32)
        *scan, total = (spare[:, i].rearrange("p (t e) -> p t e", e=E) for i in range(4, 7))
        filled = spare[:, 7].rearrange("p (e t) -> p e t", e=E)
        starts_at = sb("rt_starts_at", [P, NT], F32)
        tiles = sb("rt_tiles", [P, E], F32)
        run = [sb(f"rt_run_{i}", [P, E], F32) for i in range(2)]
        start = sb("rt_start", [P, E], F32)
        slot = sb("rt_slot", [P, NT, E], F32)
        slot_of = sb("rt_slot_of", [P, NT, 2], F32)
        tile_no = sb("rt_tile_no", [1, TILES], F32)
        begun = sb("rt_begun", [1, TILES, E], F32)
        owner = sb("rt_owner", [1, TILES], F32)

        ps_a = psum("rt_ps_a", [P, KD, C], F32)
        ps_o = psum("rt_ps_o", [P, CB, D], F32)
        ps_t = psum("rt_ps_t", [P, KD, C], F32)
        ps_g = psum("rt_ps_g", [P, C], F32)
        ps_r = psum("rt_ps_r", [P, 2, NT * E], F32)

        w_in = sem("rt_w_in")
        x_in = [sem(f"rt_x_in_{u}") for u in range(2)]
        pool_step = sem("rt_pool_step")
        dve_step = sem("rt_dve_step")
        m_in = [sem(f"rt_m_in_{u}") for u in range(2)]
        sum_seen = sem("rt_sum_seen")
        stats_seen = sem("rt_stats_seen")
        x_biased = sem("rt_x_biased")
        m_turned = sem("rt_m_turned")
        a_kept = sem("rt_a_kept")
        projected = sem("rt_projected")
        o_read = sem("rt_o_read")
        sum_ready = sem("rt_sum_ready")
        var_ready = sem("rt_var_ready")
        std_ready = sem("rt_std_ready")
        norm_ready = sem("rt_norm_ready")
        xs_ready = sem("rt_xs_ready")
        xs_kept = sem("rt_xs_kept")
        x_turned = sem("rt_x_turned")
        h_kept = sem("rt_h_kept")
        scored = sem("rt_scored")
        score_kept = sem("rt_score_kept")
        b1_turned = sem("rt_b1_turned")
        tops_ready = sem("rt_tops_ready")
        ex_ready = sem("rt_ex_ready")
        both_ready = sem("rt_both_ready")
        counted = sem("rt_counted")
        slots_ready = sem("rt_slots_ready")
        scattered = sem("rt_scattered")
        bias_ready = sem("rt_bias_ready")

        x_v = dram["x"].rearrange("a (t p) d -> p (a t) d", p=P)
        block = ctx.enter_context(nc.Block())

        def pairs(eng, body, begin, end):
            with eng.Fori(begin, end) as it:
                for u in range(2):
                    body(it * 2 + u, u, it)

        PAIRS = NC // 2

        @block.sync
        def _(sp):
            def load(c, u, it):
                chunk = bass.ds(c * CB, CB)
                sp.wait_ge(m_turned, c + 1)
                sp.dma_start(m_now[:, u], mixed[:, chunk, :]).then_inc(m_in[u], 16)
                sp.wait_ge(sum_ready, c + 1)
                sp.dma_start(x_now[:, u], x_v[:, chunk, :]).then_inc(x_in[u], 16)

            pairs(sp, load, 0, PAIRS)
            sp.dma_start(keep["b2"][:], dram["b2"].rearrange("(a e) d -> a e d", a=1).partition_broadcast(P)
                          ).then_inc(keep["weights_in"], 16)
            for e in range(E):
                sp.dma_start(keep["w1"][:, e], dram["W1"][e].rearrange("(k p) f -> p k f", p=P)
                              ).then_inc(keep["weights_in"], 16)
            for e in range(E // 2 - 2):
                sp.dma_start(keep["w2"][:, e], dram["W2"][e].rearrange("(f p) d -> p f d", p=P)
                              ).then_inc(keep["weights_in"], 16)

        @block.gpsimd
        def _(pool):
            nc.gpsimd.iota(order[:], pattern=[[1, E]], base=-E, channel_multiplier=0,
                           allow_small_or_imprecise_dtypes=True).then_inc(pool_step, 1)
            nc.gpsimd.iota(starts_at[:], pattern=[[P, NT]], base=0, channel_multiplier=0,
                           allow_small_or_imprecise_dtypes=True).then_inc(pool_step, 1)
            nc.gpsimd.iota(tile_no[:], pattern=[[1, TILES]], base=0, channel_multiplier=0,
                           allow_small_or_imprecise_dtypes=True).then_inc(pool_step, 1)
            nc.gpsimd.memset(ones_bf[:], 1.0).then_inc(pool_step, 1)
            pool.wait_ge(pool_step, 4)
            nc.gpsimd.affine_select(out=before_bf[:], in_=ones_bf[:], compare_op=ALU.is_gt, fill=0.0, base=0,
                                    pattern=[[1, P]], channel_multiplier=-1).then_inc(pool_step, 1)
            pool.wait_ge(w_in, 16 * 5)
            nc.gpsimd.tensor_tensor(bo_gated[:], bo_gated[:], gates[:, 0, :], ALU.mult).then_inc(pool_step, 1)
            pool.wait_ge(pool_step, 6)

            def add_bias(c, u, it):
                pool.wait_ge(x_in[u], it * 16 + 16)
                nc.gpsimd.tensor_tensor(x_now[:, u], x_now[:, u],
                                        bo_gated[:].unsqueeze(1).to_broadcast([P, CB, D]),
                                        ALU.add).then_inc(x_biased, 1)

            pairs(pool, add_bias, 0, PAIRS)
            pool.wait_ge(xs_kept, NC * 16 + 16)
            pool.wait_ge(slots_ready, 1)
            for t in range(NT):
                for i in range(2):
                    pool.indirect_dma_start(dram["queue"], bass.IndirectOffsetOnAxis(
                        ap=keep["slots"][:, 2 * t + i:2 * t + i + 1], axis=0), rows[:, t, :], None
                                            ).then_inc(scattered, 16)
            pool.wait_ge(scattered, 16 * 2 * NT)

        @block.tensor
        def _(pe):
            pe.wait_ge(w_in, 16 * 5)
            nc.tensor.transpose(ps_t[:, 0, 0:E * FF], b1_rows[:], ident[0:E * FF, 0:E * FF]).then_inc(b1_turned, 1)
            pe.wait_ge(bias_ready, 1)
            pe.sem_inc(m_turned, 2)
            pe.sem_inc(projected, 1)
            pe.sem_inc(scored, 1)

            def project(c, u, it):
                pe.wait_ge(m_in[u], it * 16 + 16)
                pe.wait_ge(a_kept, c + 1)
                for k in range(KD):
                    for j in range(CB):
                        ins = nc.tensor.transpose(ps_a[:, k, j * P:(j + 1) * P],
                                                  m_now[:, u, j, k * P:(k + 1) * P], ident[:])
                ins.then_inc(m_turned, 1)
                pe.wait_ge(a_kept, c + 2)
                pe.wait_ge(o_read, c + 1)
                for j in range(CB):
                    for k in range(KD):
                        ins = nc.tensor.matmul(ps_o[:, j, :], aT[:, k, j * P:(j + 1) * P], wo[:, k, :],
                                               start=k == 0, stop=k == KD - 1)
                ins.then_inc(projected, 1)

            def score_chunk(c):
                pe.wait_ge(xs_ready, c * CB + 2 * CB)
                pe.wait_ge(h_kept, c + 1)
                for k in range(KD):
                    for j in range(CB):
                        ins = nc.tensor.transpose(ps_t[:, k, j * P:(j + 1) * P],
                                                  xs[:, j, k * P:(k + 1) * P], ident[:])
                ins.then_inc(x_turned, 1)
                pe.wait_ge(h_kept, c + 2)
                pe.wait_ge(score_kept, c + 1)
                for j in range(CB):
                    for k in range(KD):
                        ins = nc.tensor.matmul(ps_g[:, j * E:(j + 1) * E], hT[:, k, j * P:(j + 1) * P],
                                               gate_w[:, k, :], start=k == 0, stop=k == KD - 1)
                ins.then_inc(scored, 1)

            def chunk_steps(c, u, it):
                project(c + 1, 1 - u, it + u)
                score_chunk(c)

            project(0, 0, 0)
            pairs(pe, chunk_steps, 0, PAIRS - 1)
            chunk_steps(NC - 2, 0, PAIRS - 1)
            score_chunk(NC - 1)
            pe.wait_ge(both_ready, 1)
            flat = both[:].rearrange("p t e -> p (t e)")
            nc.tensor.matmul(ps_r[:, 0, :], before_bf[:], flat, start=True, stop=True)
            nc.tensor.matmul(ps_r[:, 1, :], ones_bf[:], flat, start=True, stop=True).then_inc(counted, 1)

        @block.scalar
        def _(act):
            act.dma_start(wo[:], dram["Wo"].rearrange("(k p) n -> p k n", p=P)).then_inc(w_in, 16)
            act.dma_start(gate_w[:], dram["gate_w"].rearrange("(k p) n -> p k n", p=P)).then_inc(w_in, 16)
            act.dma_start(gate_b[:], dram["gate_b"].rearrange("(a n) -> a n", a=1).partition_broadcast(P)
                          ).then_inc(w_in, 16)
            act.dma_start(bo_gated[:], dram["bo"].rearrange("(a n) -> a n", a=1).partition_broadcast(P)
                          ).then_inc(w_in, 16)
            act.dma_start(b1_rows[:], dram["b1"].rearrange("e (f p) -> (e f) p", p=P)).then_inc(w_in, 16)
            act.wait_ge(b1_turned, 1)
            nc.scalar.copy(keep["b1"][:], ps_t[:, 0, 0:E * FF]).then_inc(bias_ready, 1)
            act.wait_ge(pool_step, 6)
            act.sem_inc(a_kept, 1)
            act.wait_ge(bias_ready, 1)
            act.sem_inc(h_kept, 1)
            act.sem_inc(xs_kept, 16)
            act.sem_inc(xs_ready, CB)
            act.wait_ge(dve_step, 1)
            nc.scalar.activation(std[:, 0:1], eps[:], ACT.Sqrt).then_inc(std_ready, 1)

            def keep_turned(c):
                act.wait_ge(m_turned, c + 3)
                act.wait_ge(projected, c + 1)
                nc.scalar.copy(aT[:], ps_a[:]).then_inc(a_kept, 1)

            def normalise(c):
                act.wait_ge(var_ready, c + 1)
                nc.scalar.activation(std[:], mean_var[:, :, 1], ACT.Sqrt, bias=eps[:, 0:1]).then_inc(std_ready, 1)
                act.wait_ge(norm_ready, c + 1)
                act.wait_ge(xs_kept, c * 16 + 16)
                for j in range(CB):
                    nc.scalar.activation(xs[:, j, :], mixed[:, bass.ds(c * CB + j, 1), :].rearrange("p a d -> p (a d)"),
                                         ACT.Identity, scale=rstd[:, j:j + 1],
                                         bias=shift[:, j:j + 1]).then_inc(xs_ready, 1)
                act.wait_ge(xs_ready, c * CB + 2 * CB)
                act.dma_start(rows[:, bass.ds(c * CB, CB), :], xs[:]).then_inc(xs_kept, 16)
                act.wait_ge(x_turned, c + 1)
                act.wait_ge(scored, c + 1)
                for k in range(KD):
                    ins = nc.scalar.activation(hT[:, k, :], ps_t[:, k, :], ACT.Identity,
                                               scale=mod_cols[:, 6 + k:7 + k], bias=mod_cols[:, 4 + k:5 + k])
                ins.then_inc(h_kept, 1)

            keep_turned(0)
            with act.Fori(0, NC - 1) as c:
                keep_turned(c + 1)
                normalise(c)
            normalise(NC - 1)
            act.wait_ge(tops_ready, 1)
            nc.scalar.activation(ex[:], least[:], ACT.Exp).then_inc(ex_ready, 1)
            act.wait_ge(h_kept, NC + 1)

        @block.vector
        def _(dve):
            step = Tally(dve_step)
            step.inc(nc.vector.memset(eps[:], EPS))
            dve.sem_inc(sum_ready, 2)
            dve.sem_inc(o_read, 1)
            dve.sem_inc(score_kept, 1)
            dve.wait_ge(w_in, 16 * 5)
            STEPS = 2
            first = step.n

            def sum_chunk(c, u):
                step = Tally(dve_step, c * STEPS + first)
                dve.wait_ge(projected, c + 2)
                nc.vector.tensor_tensor(gated[:], ps_o[:], gates[:, 0, :].unsqueeze(1).to_broadcast([P, CB, D]),
                                        ALU.mult).then_inc(o_read, 1)
                dve.wait_ge(o_read, c + 2)
                dve.wait_ge(x_biased, c + 1)
                chunk = mixed[:, bass.ds(c * CB, CB), :]
                nc.vector.tensor_tensor(chunk, gated[:], x_now[:, u], ALU.add).then_inc(sum_ready, 1)
                dve.wait_ge(sum_ready, c + 3)
                dve.sem_inc(sum_seen, 1)
                for j in range(CB):
                    ins = nc.vector.bn_stats(stats[:, j, :],
                                             mixed[:, bass.ds(c * CB + j, 1), :].rearrange("p a d -> p (a d)"))
                step.inc(ins)
                step.wait(dve)
                dve.wait_ge(xs_ready, c * CB + CB)
                dve.sem_inc(stats_seen, 1)
                for j in range(CB):
                    ins = nc.vector.bn_aggr(mean_var[:, j, :], stats[:, j, :])
                ins.then_inc(var_ready, 1)
                dve.wait_ge(std_ready, c + 2)
                step.inc(nc.vector.reciprocal(rstd[:], std[:]))
                step.wait(dve)
                nc.vector.scalar_tensor_tensor(out=shift[:], in0=mean_var[:, :, 0], scalar=-1.0, in1=rstd[:],
                                               op0=ALU.mult, op1=ALU.mult).then_inc(norm_ready, 1)
                assert step.n == STEPS

            def keep_scores(c):
                dve.wait_ge(scored, c + 2)
                nc.vector.tensor_tensor(score[:, bass.ds(c * CB, CB), :],
                                        ps_g[:, 0:CB * E].rearrange("p (j e) -> p j e", e=E),
                                        gate_b[:].unsqueeze(1).to_broadcast([P, CB, E]),
                                        ALU.add).then_inc(score_kept, 1)

            def chunk_steps(c, u, it):
                sum_chunk(c, u)
                keep_scores(c - 1)

            sum_chunk(0, 0)
            chunk_steps(1, 1, 0)
            pairs(dve, chunk_steps, 1, PAIRS)
            keep_scores(NC - 1)
            dve.wait_ge(score_kept, NC + 1)
            dve.wait_ge(pool_step, 6)
            step = Tally(dve_step, first + NC * STEPS)

            def wide(ap):
                return ap.unsqueeze(2).to_broadcast([P, NT, E])

            experts = order[:].unsqueeze(1).to_broadcast([P, NT, E])
            values = score
            for i in range(2):
                step.inc(nc.vector.tensor_reduce(top[i][:], values[:], AX.X, ALU.max))
                step.wait(dve)
                step.inc(nc.vector.tensor_tensor(equal, values[:], wide(top[i][:]), ALU.is_equal))
                step.wait(dve)
                step.inc(nc.vector.tensor_tensor(equal, equal, experts, ALU.mult))
                step.wait(dve)
                step.inc(nc.vector.tensor_reduce(least[:], equal, AX.X, ALU.min))
                step.wait(dve)
                step.inc(nc.vector.tensor_tensor(pick[i][:], experts, wide(least[:]), ALU.is_equal))
                step.wait(dve)
                if i == 0:
                    step.inc(nc.vector.scalar_tensor_tensor(out=masked, in0=pick[0][:], scalar=MASKED,
                                                            in1=score[:], op0=ALU.mult, op1=ALU.add))
                    step.wait(dve)
                    values = masked
            nc.vector.tensor_tensor(both[:], pick[0][:], pick[1][:], ALU.add).then_inc(both_ready, 1)
            nc.vector.tensor_tensor(least[:], top[1][:], top[0][:], ALU.subtract).then_inc(tops_ready, 1)
            dve.wait_ge(ex_ready, 1)
            step.inc(nc.vector.tensor_scalar_add(den[:], ex[:], 1.0))
            step.wait(dve)
            step.inc(nc.vector.reciprocal(keep["share"][:, 0, :], den[:]))
            step.wait(dve)
            step.inc(nc.vector.tensor_tensor(keep["share"][:, 1, :], ex[:], keep["share"][:, 0, :], ALU.mult))
            dve.wait_ge(counted, 1)
            step.inc(nc.vector.tensor_copy(total[:], ps_r[:, 1, :].rearrange("p (t e) -> p t e", e=E)))
            step.wait(dve)
            have, n, reach = total, 0, 1
            while reach < NT:
                to = scan[n % 2]
                step.inc(nc.vector.tensor_copy(to[:, 0:reach], have[:, 0:reach]))
                step.inc(nc.vector.tensor_tensor(to[:, reach:], have[:, reach:], have[:, 0:NT - reach], ALU.add))
                step.wait(dve)
                have, n, reach = to, n + 1, reach * 2
            count = have[:, NT - 1, :]
            step.inc(nc.vector.tensor_tensor(filled[:], count.unsqueeze(2).to_broadcast([P, E, NT]),
                                             starts_at[:].unsqueeze(1).to_broadcast([P, E, NT]), ALU.is_gt))
            step.wait(dve)
            step.inc(nc.vector.tensor_reduce(tiles[:], filled[:], AX.X, ALU.add))
            step.wait(dve)
            sums, n, reach = tiles, 0, 1
            while reach < E:
                to = run[n % 2]
                step.inc(nc.vector.tensor_copy(to[:, 0:reach], sums[:, 0:reach]))
                step.inc(nc.vector.tensor_tensor(to[:, reach:], sums[:, reach:], sums[:, 0:E - reach], ALU.add))
                step.wait(dve)
                sums, n, reach = to, n + 1, reach * 2
            step.inc(nc.vector.tensor_tensor(start[:], sums[:], tiles[:], ALU.subtract))
            step.inc(nc.vector.tensor_tensor(slot[:], have[:], total[:], ALU.subtract))
            step.wait(dve)
            step.inc(nc.vector.tensor_tensor(slot[:], slot[:], ps_r[:, 0, :].rearrange("p (t e) -> p t e", e=E),
                                             ALU.add))
            step.wait(dve)
            step.inc(nc.vector.scalar_tensor_tensor(out=slot[:], in0=start[:].unsqueeze(1).to_broadcast([P, NT, E]),
                                                    scalar=float(P), in1=slot[:], op0=ALU.mult, op1=ALU.add))
            step.wait(dve)
            for i in range(2):
                step.inc(nc.vector.tensor_tensor(pick[i][:], pick[i][:], slot[:], ALU.mult))
                step.wait(dve)
                step.inc(nc.vector.tensor_reduce(slot_of[:, :, i], pick[i][:], AX.X, ALU.add))
            step.wait(dve)
            nc.vector.tensor_copy(keep["slots"][:], slot_of[:].rearrange("p t i -> p (t i)")).then_inc(slots_ready, 1)
            step.inc(nc.vector.tensor_tensor(begun[:], tile_no[:].unsqueeze(2).to_broadcast([1, TILES, E]),
                                             start[0:1, :].unsqueeze(1).to_broadcast([1, TILES, E]), ALU.is_ge))
            step.wait(dve)
            step.inc(nc.vector.tensor_reduce(owner[:], begun[:], AX.X, ALU.add))
            step.wait(dve)
            step.inc(nc.vector.tensor_scalar_add(owner[:], owner[:], -1.0))
            step.wait(dve)
            step.inc(nc.vector.tensor_copy(keep["owner"][:], owner[:]))
            step.wait(dve)


def experts(nc, dram, keep):
    with ExitStack() as ctx:
        def sb(name, shape, dt):
            return ctx.enter_context(nc.sbuf_tensor(name, shape, dt))

        def psum(name, shape, dt):
            return ctx.enter_context(nc.psum_tensor(name, shape, dt))

        def sem(name):
            return ctx.enter_context(nc.semaphore(name))

        ident, mod_cols, w1, w2, b1, b2, owner = (
            keep[n] for n in ("ident", "mod_cols", "w1", "w2", "b1", "b2", "owner"))
        HALVES = FF * P // C
        x_tile = sb("ex_x_tile", [P, 2, D], F32)
        xT = sb("ex_xT", [P, KD, P], F32)
        h = sb("ex_h", [P, FF * P], F32)
        hT = sb("ex_hT", [P, FF, P], F32)
        y = sb("ex_y", [P, 2, D], F32)

        ps_x = psum("ex_ps_x", [P, C], F32)
        ps_h = [psum(f"ex_ps_h_{i}", [P, C], F32) for i in range(HALVES)]
        ps_hT = psum("ex_ps_hT", [P, FF, P], F32)
        ps_y = [psum(f"ex_ps_y_{u}", [P, C], F32) for u in range(2)]

        x_in = [sem(f"ex_x_in_{u}") for u in range(2)]
        w2_in = sem("ex_w2_in")
        x_turned = sem("ex_x_turned")
        xT_ready = sem("ex_xT_ready")
        hidden = [sem(f"ex_hidden_{i}") for i in range(HALVES)]
        h_copied = [sem(f"ex_h_copied_{i}") for i in range(HALVES)]
        h_turned = sem("ex_h_turned")
        rectified = sem("ex_rectified")
        out_done = sem("ex_out_done")
        y_ready = sem("ex_y_ready")
        y_stored = [sem(f"ex_y_stored_{u}") for u in range(2)]
        block = ctx.enter_context(nc.Block())

        def over_queue(eng, body, done=0):
            with eng.Fori(done, (TILES - 1) // 2) as it:
                for u in range(2):
                    body(it * 2 + (u + 1), (u + 1) % 2, it)

        @block.sync
        def _(sp):
            for e in range(E // 2 - 2, E):
                sp.dma_start(w2[:, e], dram["W2"][e].rearrange("(f p) d -> p f d", p=P)).then_inc(w2_in, 16)
            sp.sem_inc(x_turned, 2)

            def load(tile, u):
                sp.wait_ge(x_turned, tile + 1)
                sp.dma_start(x_tile[:, u, :], dram["queue"][bass.ds(tile * P, P), :]).then_inc(x_in[u], 16)

            load(0, 0)
            over_queue(sp, lambda tile, u, it: load(tile, u))
            load(TILES, TILES % 2)
            sp.wait_ge(x_in[TILES % 2], 16 * ((TILES + 1) // 2))

        @block.gpsimd
        def _(pool):
            def store(tile, u):
                pool.wait_ge(y_ready, tile + 3)
                pool.dma_start(dram["answers"][bass.ds(tile * P, P), :], y[:, u, :]).then_inc(y_stored[u], 16)

            store(0, 0)
            over_queue(pool, lambda tile, u, it: store(tile, u))
            for u in range(2):
                pool.wait_ge(y_stored[u], 16 * ((TILES + 1 - u) // 2))

        @block.tensor
        def _(pe):
            def turn_rows(tile, u, loads):
                pe.wait_ge(x_in[u], loads * 16)
                pe.wait_ge(xT_ready, tile + 1)
                for k in range(KD):
                    ins = nc.tensor.transpose(ps_x[:, k * P:(k + 1) * P], x_tile[:, u, k * P:(k + 1) * P], ident[:])
                ins.then_inc(x_turned, 1)

            def first_layer(tile):
                e = pe.value_load(owner[0:1, bass.ds(tile, 1)], min_val=0, max_val=E - 1)
                pe.wait_ge(xT_ready, tile + 2)
                for i in range(HALVES):
                    pe.wait_ge(h_copied[i], tile + 1)
                    for k in range(KD):
                        ins = nc.tensor.matmul(ps_h[i][:], xT[:, k, :],
                                               w1[:, bass.ds(e, 1), k, i * C:(i + 1) * C].rearrange(
                                                   "p a f -> p (a f)"), start=k == 0, stop=k == KD - 1)
                    ins.then_inc(hidden[i], 1)
                return e

            def turn_hidden(tile):
                for i in range(HALVES):
                    pe.wait_ge(h_copied[i], tile + 2)
                pe.wait_ge(rectified, tile * FF + FF)
                for f in range(FF):
                    ins = nc.tensor.transpose(ps_hT[:, f, :], h[:, f * P:(f + 1) * P], ident[:])
                ins.then_inc(h_turned, 1)

            def second_layer(tile, u):
                e = pe.value_load(owner[0:1, bass.ds(tile, 1)], min_val=0, max_val=E - 1)
                pe.wait_ge(rectified, tile * FF + 2 * FF)
                pe.wait_ge(y_ready, tile + 1)
                for f in range(FF):
                    ins = nc.tensor.matmul(ps_y[u][:, 0:D], hT[:, f, :],
                                           w2[:, bass.ds(e, 1), f, :].rearrange("p a d -> p (a d)"),
                                           start=f == 0, stop=f == FF - 1)
                ins.then_inc(out_done, 1)

            pe.wait_ge(keep["weights_in"], 16 * (1 + E + E // 2 - 2))
            turn_rows(0, 0, 1)
            first_layer(0)
            pe.wait_ge(w2_in, 16 * (E // 2 + 2))
            turn_rows(1, 1, 1)
            turn_hidden(0)

            def tile_steps(tile, u, it):
                first_layer(tile)
                second_layer(tile - 1, 1 - u)
                turn_rows(tile + 1, 1 - u, it + (2 if u == 1 else 2))
                turn_hidden(tile)

            over_queue(pe, tile_steps)
            second_layer(TILES - 1, (TILES - 1) % 2)

        @block.scalar
        def _(act):
            act.sem_inc(h_copied[0], 1)
            act.sem_inc(rectified, FF)

            def tile_steps(tile):
                e = act.value_load(owner[0:1, bass.ds(tile, 1)], min_val=0, max_val=E - 1)
                act.wait_ge(hidden[0], tile + 1)
                nc.scalar.copy(h[:, 0:C], ps_h[0][:]).then_inc(h_copied[0], 1)
                act.wait_ge(h_turned, tile + 1)
                for f in range(FF):
                    nc.scalar.activation(hT[:, f, :], ps_hT[:, f, :], ACT.Relu,
                                         bias=b1[:, bass.ds(e * FF + f, 1)]).then_inc(rectified, 1)

            tile_steps(0)
            over_queue(act, lambda tile, u, it: tile_steps(tile))

        @block.vector
        def _(dve):
            dve.sem_inc(h_copied[1], 1)
            dve.sem_inc(xT_ready, 1)
            dve.sem_inc(y_ready, 2)

            def modulate(tile):
                dve.wait_ge(x_turned, tile + 3)
                for k in range(KD):
                    ins = nc.vector.tensor_scalar(xT[:, k, :], ps_x[:, k * P:(k + 1) * P], mod_cols[:, 6 + k:7 + k],
                                                  mod_cols[:, 4 + k:5 + k], ALU.mult, ALU.add)
                ins.then_inc(xT_ready, 1)

            def copy_hidden(tile):
                dve.wait_ge(hidden[1], tile + 1)
                nc.vector.tensor_copy(h[:, C:2 * C], ps_h[1][:]).then_inc(h_copied[1], 1)

            def answer(tile, u, stores):
                e = dve.value_load(owner[0:1, bass.ds(tile, 1)], min_val=0, max_val=E - 1)
                dve.wait_ge(out_done, tile + 1)
                if not isinstance(stores, int) or stores > 0:
                    dve.wait_ge(y_stored[u], stores * 16)
                nc.vector.tensor_tensor(y[:, u, :], ps_y[u][:, 0:D],
                                        b2[:, bass.ds(e, 1), :].rearrange("p a d -> p (a d)"),
                                        ALU.add).then_inc(y_ready, 1)

            modulate(0)
            copy_hidden(0)
            modulate(1)

            def tile_steps(tile, u, it):
                copy_hidden(tile)
                answer(tile - 1, 1 - u, it)
                modulate(tile + 1)

            for tile in (1, 2):
                tile_steps(tile, tile % 2, 0)
            over_queue(dve, tile_steps, done=1)
            answer(TILES - 1, (TILES - 1) % 2, (TILES - 1) // 2)


def combine(nc, dram, keep):
    with ExitStack() as ctx:
        def sb(name, shape, dt):
            return ctx.enter_context(nc.sbuf_tensor(name, shape, dt))

        def sem(name):
            return ctx.enter_context(nc.semaphore(name))

        RING = 4
        share, gates, mixed = keep["share"], keep["gates"], keep["mixed"]
        answer = [sb(f"co_answer_{i}", [P, RING, D], F32) for i in range(2)]
        fetched = [sem(f"co_fetched_{r}") for r in range(RING)]
        stored = [sem(f"co_stored_{r}") for r in range(RING)]
        dve_step = sem("co_dve_step")
        summed = sem("co_summed")
        out_v = dram["out"].rearrange("a (t p) d -> p (a t) d", p=P)
        block = ctx.enter_context(nc.Block())

        @block.gpsimd
        def _(pool):
            for t in range(NT):
                if t >= RING:
                    pool.wait_ge(stored[t % RING], 16 * (t // RING))
                for i in range(2):
                    pool.indirect_dma_start(answer[i][:, t % RING, :], None, dram["answers"],
                                            bass.IndirectOffsetOnAxis(ap=keep["slots"][:, 2 * t + i:2 * t + i + 1],
                                                                      axis=0)).then_inc(fetched[t % RING], 16)

        @block.sync
        def _(sp):
            with sp.Fori(0, NT // RING) as it:
                for r in range(RING):
                    sp.wait_ge(summed, it * RING + (r + 1))
                    sp.dma_start(out_v[:, bass.ds(it * RING + r, 1), :], answer[1][:, r:r + 1, :]
                                 ).then_inc(stored[r], 16)
            for r in range(RING):
                sp.wait_ge(stored[r], 16 * (NT // RING))

        @block.vector
        def _(dve):
            STEPS = 3
            with dve.Fori(0, NT // RING) as it:
                for r in range(RING):
                    t = it * RING + r
                    step = Tally(dve_step, t * STEPS)
                    dve.wait_ge(fetched[r], it * 32 + 32)
                    first, second = answer[0][:, r, :], answer[1][:, r, :]
                    step.inc(nc.vector.tensor_scalar(first, first, share[:, 0, bass.ds(t, 1)], None, ALU.mult))
                    step.wait(dve)
                    step.inc(nc.vector.scalar_tensor_tensor(out=second, in0=second,
                                                            scalar=share[:, 1, bass.ds(t, 1)], in1=first,
                                                            op0=ALU.mult, op1=ALU.add))
                    step.wait(dve)
                    step.inc(nc.vector.tensor_tensor(second, second, gates[:, 1, :], ALU.mult))
                    step.wait(dve)
                    nc.vector.tensor_tensor(second, second,
                                            mixed[:, bass.ds(t, 1), :].rearrange("p a d -> p (a d)"),
                                            ALU.add).then_inc(summed, 1)
                    assert step.n == STEPS


def adaln_attention_experts(nc, dram):
    for name in ("k_stack", "q_stack"):
        dram[name] = nc.dram_tensor(name, (STACK, H, S), BF16).ap()
    for name, tiles in (("queue", TILES + 1), ("answers", TILES)):
        dram[name] = nc.dram_tensor(name, (tiles * P, D), F32).ap()
    with ExitStack() as outer:
        def kept(ctx, name, shape, dt):
            keep[name] = ctx.enter_context(nc.sbuf_tensor("kept_" + name, shape, dt))

        keep = {"weights_in": outer.enter_context(nc.semaphore("weights_in"))}
        kept(outer, "ident", [P, P], F32)
        kept(outer, "gates", [P, 2, D], F32)
        kept(outer, "mod_cols", [P, 8], F32)
        kept(outer, "mixed", [P, NT, D], F32)
        with ExitStack() as inner:
            kept(inner, "ident_bf", [P, P], BF16)
            kept(inner, "mask_kq", [P, P], BF16)
            kept(inner, "mask_qk", [P, P], BF16)
            keep["k_in"] = inner.enter_context(nc.semaphore("k_in"))
            kept(inner, "too_wide", [1, 1], I32)
            kept(inner, "v", [P, NT, D], F32)
            attention_inputs(nc, dram, keep)
            kept(inner, "k_rows", [STACK, 2 * GH * S], BF16)
            score_shifts(nc, dram, keep)
            row_maxima(nc, dram, keep)
            attention(nc, dram, keep)
        kept(outer, "w1", [P, E, KD, FF * P], F32)
        kept(outer, "w2", [P, E, FF, D], F32)
        kept(outer, "b1", [P, E * FF], F32)
        kept(outer, "b2", [P, E, D], F32)
        kept(outer, "slots", [P, 2 * NT], U32)
        kept(outer, "share", [P, 2, NT], F32)
        kept(outer, "owner", [1, TILES], I32)
        route(nc, dram, keep)
        experts(nc, dram, keep)
        combine(nc, dram, keep)


INPUTS = {
    "x": "L0_attn_x", "Wq": "L0_attn_Wq", "bq": "L0_attn_bq", "Wk": "L0_attn_Wk", "bk": "L0_attn_bk",
    "Wv": "L0_attn_Wv", "bv": "L0_attn_bv", "Wo": "L0_attn_Wo", "bo": "L0_attn_bo",
    "gate_w": "L0_ffn_gate_w", "gate_b": "L0_ffn_gate_b", "W1": "L0_ffn_W1", "b1": "L0_ffn_b1",
    "W2": "L0_ffn_W2", "b2": "L0_ffn_b2", "c": "L0_c", "wmod": "L0_wmod",
}


def kernel(**inputs):
    import numpy as _np
    import concourse.bacc as _bacc
    from concourse.bass_utils import run_bass_kernel_spmd as _run

    nc = _bacc.Bacc("TRN2", target_bir_lowering=False, num_devices=1)
    arrays, dram = {}, {}
    for name, given in INPUTS.items():
        a = _np.ascontiguousarray(inputs[given])
        arrays[f"in_{name}"] = a
        dram[name] = nc.dram_tensor(f"in_{name}", a.shape, mybir.dt.from_np(a.dtype), kind="ExternalInput").ap()
    dram["out"] = nc.dram_tensor("out", (1, S, D), F32, kind="ExternalOutput").ap()
    adaln_attention_experts(nc, dram)
    return _run(nc, [arrays], core_ids=[0]).results[0]["out"]
```

```python
from contextlib import ExitStack

import concourse.bass as bass
from concourse import mybir

ALU = mybir.AluOpType
ACT = mybir.ActivationFunctionType
AX = mybir.AxisListType
F32 = mybir.dt.float32
BF16 = mybir.dt.bfloat16
U32 = mybir.dt.uint32
I32 = mybir.dt.int32

P = 128
S = 4096
D = 256
KD = D // P
H = 16
HD = D // H
GH = 4
G = H // GH
NT = S // P
C = 512
NC = S // C
CB = C // P
TERMS = 6
ROWS = TERMS * HD
STACK = ROWS + 3
PARTS = 3 * HD
E = 8
FF = 1024 // P
TILES = (2 * S + E * (P - 1)) // P
QROWS = S + P
MASKED = -3.0e38
EPS = 1e-5
FIRST_KEYS = 32
ROOM_UP = 70.0
ROOM_DOWN = 60.0
SLACK = 1.0 + 2.0 ** -6
LOADS = 4
K_TERM = [0, 0, 0, 1, 1, 2]
Q_TERM = [0, 1, 2, 0, 1, 0]


def stack_runs(order, rows=STACK):
    runs = []
    for term, part in enumerate(order + ([3] if rows == STACK else [])):
        n = HD if part < 3 else STACK - ROWS
        if runs and runs[-1][1] + runs[-1][2] == part * HD:
            runs[-1][2] += n
        else:
            runs.append([term * HD, part * HD, n])
    return runs


def load_stack(eng, to, parts, order, heads, tokens, done, rows=STACK):
    for row, of, n in stack_runs(order, rows):
        eng.dma_start(to[row:row + n], parts[of:of + n, heads, tokens]).then_inc(done, 16)


class Tally:

    def __init__(self, sem, base=0):
        self.sem, self.base, self.n = sem, base, 0

    def inc(self, ins):
        self.n += 1
        return ins.then_inc(self.sem, 1)

    def wait(self, eng):
        eng.wait_ge(self.sem, self.base + self.n)


def attention_inputs(nc, dram, keep):
    with ExitStack() as ctx:
        def sb(name, shape, dt):
            return ctx.enter_context(nc.sbuf_tensor(name, shape, dt))

        def psum(name, shape, dt):
            return ctx.enter_context(nc.psum_tensor(name, shape, dt))

        def sem(name):
            return ctx.enter_context(nc.semaphore(name))

        ident, gates, v, mod_cols = keep["ident"], keep["gates"], keep["v"], keep["mod_cols"]
        x = sb("x_rows", [P, NT, D], F32)
        xn = sb("xn", [P, 2, CB, D], F32)
        ccol = sb("ccol", [P, KD], F32)
        silu = sb("silu", [P, 4, KD], F32)
        silu_rows = sb("silu_rows", [P, KD, P], F32)
        wmod = sb("wmod", [P, KD, 6 * D], F32)
        wq = sb("wq", [P, KD, D], F32)
        wk = sb("wk", [P, KD, D], F32)
        wv = sb("wv", [P, KD, D], F32)
        wk_turned = sb("wk_turned", [P, KD, D], F32)
        wq_turned = sb("wq_turned", [P, KD, D], F32)
        bk = sb("bk", [P, KD], F32)
        bq = sb("bq", [P, KD], F32)
        bq_scaled = sb("bq_scaled", [P, KD], F32)
        bv_rows = sb("bv_rows", [P, D], F32)
        mod_raw = sb("mod_raw", [P, 8], F32)
        gate_raw = sb("gate_raw", [P, 2, D], F32)
        gate_sign = sb("gate_sign", [P, 2, D], F32)
        gate_abs = sb("gate_abs", [P, 2, D], F32)
        gate_size = sb("gate_size", [P, 2, D], F32)
        stats = sb("stats", [P, NT, 6], F32)
        mean2 = sb("mean2", [P, NT], F32)
        dev = sb("dev", [P, NT], F32)
        dev2 = sb("dev2", [P, NT], F32)
        m2 = sb("m2", [P, NT], F32)
        m2d = sb("m2d", [P, NT], F32)
        var = sb("var", [P, NT], F32)
        shift = sb("shift", [P, NT], F32)
        eps = sb("eps", [P, 1], F32)
        std = sb("std", [P, NT], F32)
        rstd = sb("rstd", [P, NT], F32)
        hT = sb("hT", [P, 2, KD, C], F32)
        kf = sb("kf", [P, KD, C], F32)
        qf = sb("qf", [P, KD, C], F32)
        kparts = sb("kparts", [P, 2, 3, KD, C], BF16)
        qparts = sb("qparts", [P, 2, 3, KD, C], BF16)
        ones = sb("ones", [P, P], F32)
        ones_rows = sb("ones_rows", [3 * H, S], BF16)

        ps_turn = psum("ps_turn", [P, KD, C], F32)
        ps_k = psum("ps_k", [P, KD, C], F32)
        ps_q = psum("ps_q", [P, KD, C], F32)
        ps_v = psum("ps_v", [P, CB, D], F32)

        x_in = [sem(f"x_in_{n}") for n in range(LOADS)]
        mod_in = sem("mod_in")
        w_in = sem("w_in")
        dve_step = sem("dve_step")
        act_step = sem("act_step")
        pool_step = sem("pool_step")
        c_exp = sem("c_exp")
        silu_ready = sem("silu_ready")
        rows_ready = sem("rows_ready")
        mod_ready = sem("mod_ready")
        cols_ready = sem("cols_ready")
        var_ready = sem("var_ready")
        std_ready = sem("std_ready")
        xn_ready = sem("xn_ready")
        turned = sem("turned")
        h_ready = sem("h_ready")
        k_ready = sem("k_ready")
        v_ready = sem("v_ready")
        kq_kept = sem("kq_kept")
        parts_ready = sem("parts_ready")
        v_kept = sem("v_kept")
        stats_ready = sem("stats_ready")
        norm_ready = sem("norm_ready")
        ones_stored = sem("ones_stored")
        k_stored = [sem(f"k_stored_{u}") for u in range(2)]
        q_stored = [sem(f"q_stored_{u}") for u in range(2)]

        x_v = dram["x"].rearrange("a (t p) d -> p (a t) d", p=P)
        block = ctx.enter_context(nc.Block())

        @block.sync
        def _(sp):
            sp.dma_start(ccol[:], dram["c"].rearrange("a (k p) -> p (a k)", p=P),
                         allow_slow_non_contiguous=True).then_inc(mod_in, 16)
            for n in range(LOADS):
                part = slice(n * NT // LOADS, (n + 1) * NT // LOADS)
                sp.dma_start(x[:, part, :], x_v[:, part, :]).then_inc(x_in[n], 16)
            sp.wait_ge(pool_step, 2)
            sp.dma_start(dram["k_parts"][PARTS:PARTS + 3].rearrange("r h s -> (r h) s"),
                         ones_rows[:]).then_inc(ones_stored, 16)
            with sp.Fori(0, NC // 2) as it:
                for u in range(2):
                    for n, (parts, name, kept) in enumerate(
                            ((kparts, "k_parts", k_stored), (qparts, "q_parts", q_stored))):
                        sp.wait_ge(parts_ready, it * 4 + (2 * u + n + 3))
                        to = dram[name][0:PARTS, :, bass.ds(it * 2 * C + u * C, C)]
                        sp.dma_start(to.rearrange("(a d) h s -> (d h) a s", a=3 * KD),
                                     parts[:, u].rearrange("p a m s -> p (a m) s")).then_inc(kept[u], 16)
            sp.wait_ge(ones_stored, 16)
            for u in range(2):
                sp.wait_ge(k_stored[u], 16 * (NC // 2 + 1))
                sp.wait_ge(q_stored[u], 16 * (NC // 2 + 1))

        @block.gpsimd
        def _(pool):
            nc.gpsimd.memset(ones_rows[:], 1.0).then_inc(pool_step, 1)
            nc.gpsimd.memset(ones[:], 1.0).then_inc(pool_step, 1)
            pool.wait_ge(pool_step, 2)
            nc.gpsimd.affine_select(out=keep["ident"][:], in_=ones[:], compare_op=ALU.is_equal, fill=0.0,
                                    base=0, pattern=[[-1, P]], channel_multiplier=1).then_inc(pool_step, 1)
            nc.gpsimd.affine_select(out=keep["ident_bf"][:], in_=ones[:], compare_op=ALU.is_equal, fill=0.0,
                                    base=0, pattern=[[-1, P]], channel_multiplier=1).then_inc(pool_step, 1)
            nc.gpsimd.memset(keep["mask_kq"][:], 0.0).then_inc(pool_step, 1)
            nc.gpsimd.memset(keep["mask_qk"][:], 0.0).then_inc(pool_step, 1)
            pool.wait_ge(pool_step, 6)
            nc.gpsimd.affine_select(out=keep["mask_kq"][:], in_=keep["mask_kq"][:], compare_op=ALU.is_ge, fill=MASKED,
                                    base=0, pattern=[[1, P]], channel_multiplier=-1).then_inc(pool_step, 1)
            nc.gpsimd.affine_select(out=keep["mask_qk"][:], in_=keep["mask_qk"][:], compare_op=ALU.is_ge, fill=MASKED,
                                    base=0, pattern=[[-1, P]], channel_multiplier=1).then_inc(pool_step, 1)
            pool.wait_ge(w_in, 16 * 6)
            for w, turned_w in ((wk, wk_turned), (wq, wq_turned)):
                for k in range(KD):
                    nc.gpsimd.tensor_copy(turned_w[:, k].rearrange("p (d h) -> p d h", h=H),
                                          w[:, k].rearrange("p (h d) -> p d h", h=H)).then_inc(pool_step, 1)
            pool.wait_ge(pool_step, 8 + 2 * KD)

        @block.scalar
        def _(act):
            act.dma_start(wmod[:], dram["wmod"].rearrange("(k p) n -> p k n", p=P),
                         allow_slow_non_contiguous=True).then_inc(mod_in, 16)
            for to, name in ((wk, "Wk"), (wq, "Wq"), (wv, "Wv")):
                act.dma_start(to[:], dram[name].rearrange("(k p) n -> p k n", p=P)).then_inc(w_in, 16)
            for to, name in ((bk, "bk"), (bq, "bq")):
                of = dram[name].rearrange("(h m d) -> d h m", h=H, m=KD)
                act.dma_start(to[:], of, allow_slow_non_contiguous=True).then_inc(w_in, 16)
            act.dma_start(bv_rows[:], dram["bv"].rearrange("(a n) -> a n", a=1).partition_broadcast(P)
                          ).then_inc(w_in, 16)
            act.wait_ge(mod_in, 32)
            nc.scalar.activation(silu[:, 0, :], ccol[:], ACT.Exp, scale=-1.0).then_inc(c_exp, 1)
            act.wait_ge(w_in, 16 * 6)
            nc.scalar.mul(bq_scaled[:], bq[:], HD ** -0.5).then_inc(act_step, 1)
            act.wait_ge(mod_ready, 2)
            nc.scalar.copy(mod_raw[:], ps_turn[:, 0, 0:8]).then_inc(act_step, 1)
            nc.scalar.copy(gate_raw[:], ps_k[:, 0, :].rearrange("p (a d) -> p a d", a=2)).then_inc(act_step, 1)
            act.wait_ge(var_ready, 1)
            nc.scalar.activation(std[:], var[:], ACT.Sqrt, bias=eps[:, 0:1]).then_inc(std_ready, 1)
            act.wait_ge(norm_ready, 1)
            act.wait_ge(cols_ready, 1)
            act.wait_ge(act_step, 3)
            act.sem_inc(h_ready, KD)
            act.sem_inc(kq_kept, 2 * KD)
            with act.Fori(0, NC // 2) as it:
                for u in range(2):
                    c = it * 2 + u
                    act.wait_ge(turned, c + 1)
                    for j in range(CB):
                        t = it * (2 * CB) + u * CB + j
                        nc.scalar.activation(xn[:, u, j, :], x[:, bass.ds(t, 1), :].rearrange("p a d -> p (a d)"),
                                             ACT.Identity, scale=rstd[:, bass.ds(t, 1)],
                                             bias=shift[:, bass.ds(t, 1)]).then_inc(xn_ready, 1)
                    act.wait_ge(v_ready, c + 1)
                    act.wait_ge(turned, c + 3)
                    for k in range(KD):
                        nc.scalar.activation(hT[:, u, k, :], ps_turn[:, k, :], ACT.Identity,
                                             scale=mod_cols[:, 2 + k:3 + k],
                                             bias=mod_cols[:, k:k + 1]).then_inc(h_ready, 1)
                    act.wait_ge(k_ready, c * 2 + 1)
                    act.wait_ge(parts_ready, c * 2 + 1)
                    for m in range(KD):
                        nc.scalar.activation(kf[:, m, :], ps_k[:, m, :], ACT.Identity,
                                             bias=bk[:, m:m + 1]).then_inc(kq_kept, 1)
                    act.wait_ge(k_ready, c * 2 + 2)
                    act.wait_ge(parts_ready, c * 2 + 2)
                    for m in range(KD):
                        nc.scalar.activation(qf[:, m, :], ps_q[:, m, :], ACT.Identity, scale=HD ** -0.5,
                                             bias=bq_scaled[:, m:m + 1]).then_inc(kq_kept, 1)

        @block.tensor
        def _(pe):
            pe.wait_ge(mod_in, 32)
            pe.wait_ge(silu_ready, 1)
            for n, start in enumerate((0, P, D, D + P, 3 * D, 3 * D + P, 4 * D, 4 * D + P)):
                for k in range(KD):
                    last = nc.tensor.matmul(ps_turn[:, 0, n:n + 1], wmod[:, k, start:start + P],
                                            silu[:, 3, k:k + 1], start=k == 0, stop=k == KD - 1)
            last.then_inc(mod_ready, 1)
            pe.wait_ge(rows_ready, KD)
            for n, start in enumerate((2 * D, 5 * D)):
                for k in range(KD):
                    last = nc.tensor.matmul(ps_k[:, 0, n * D:(n + 1) * D], silu_rows[:, k, :],
                                            wmod[:, k, start:start + D], start=k == 0, stop=k == KD - 1)
            last.then_inc(mod_ready, 1)
            pe.wait_ge(act_step, 3)
            pe.wait_ge(pool_step, 8 + 2 * KD)
            pe.wait_ge(w_in, 16 * 6)
            pe.sem_inc(turned, 2)
            pe.sem_inc(v_ready, 2)
            with pe.Fori(0, NC // 2) as it:
                for u in range(2):
                    c = it * 2 + u
                    pe.wait_ge(xn_ready, c * CB + CB)
                    pe.wait_ge(h_ready, c * KD + KD)
                    for k in range(KD):
                        for j in range(CB):
                            last = nc.tensor.transpose(ps_turn[:, k, j * P:(j + 1) * P],
                                                       xn[:, u, j, k * P:(k + 1) * P], ident[:])
                    last.then_inc(turned, 1)
                    pe.wait_ge(h_ready, c * KD + 2 * KD)
                    for n, (w, ps) in enumerate(((wk_turned, ps_k), (wq_turned, ps_q))):
                        pe.wait_ge(kq_kept, c * (2 * KD) + (n + 1) * KD)
                        for m in range(KD):
                            for k in range(KD):
                                last = nc.tensor.matmul(ps[:, m, :], w[:, k, m * P:(m + 1) * P], hT[:, u, k, :],
                                                        start=k == 0, stop=k == KD - 1)
                        last.then_inc(k_ready, 1)
                    pe.wait_ge(v_kept, c + 1)
                    for j in range(CB):
                        for k in range(KD):
                            last = nc.tensor.matmul(ps_v[:, j, :], hT[:, u, k, j * P:(j + 1) * P], wv[:, k, :],
                                                    start=k == 0, stop=k == KD - 1)
                    last.then_inc(v_ready, 1)

        @block.vector
        def _(dve):
            step = Tally(dve_step)
            step.inc(nc.vector.memset(eps[:], EPS))
            dve.wait_ge(c_exp, 1)
            step.inc(nc.vector.tensor_scalar_add(silu[:, 1, :], silu[:, 0, :], 1.0))
            step.wait(dve)
            step.inc(nc.vector.reciprocal(silu[:, 2, :], silu[:, 1, :]))
            step.wait(dve)
            nc.vector.tensor_tensor(silu[:, 3, :], silu[:, 2, :], ccol[:], ALU.mult).then_inc(silu_ready, 1)
            dve.wait_ge(silu_ready, 1)
            dve.wait_ge(pool_step, 2)
            for k in range(KD):
                nc.vector.tensor_scalar(silu_rows[:, k, :], ones[:], silu[:, 3, k:k + 1], None,
                                        ALU.mult).then_inc(rows_ready, 1)
            for n in range(LOADS):
                dve.wait_ge(x_in[n], 16)
                with dve.Fori(n * NT // LOADS, (n + 1) * NT // LOADS) as t:
                    nc.vector.bn_stats(stats[:, bass.ds(t, 1), :].rearrange("p a s -> p (a s)"),
                                       x[:, bass.ds(t, 1), :].rearrange("p a d -> p (a d)")).then_inc(stats_ready, 1)
            dve.wait_ge(stats_ready, NT)
            step.inc(nc.vector.tensor_tensor(mean2[:], stats[:, :, 1], stats[:, :, 4], ALU.add))
            step.inc(nc.vector.tensor_tensor(dev[:], stats[:, :, 1], stats[:, :, 4], ALU.subtract))
            step.inc(nc.vector.tensor_tensor(m2[:], stats[:, :, 2], stats[:, :, 5], ALU.add))
            step.wait(dve)
            step.inc(nc.vector.tensor_tensor(dev2[:], dev[:], dev[:], ALU.mult))
            step.inc(nc.vector.tensor_scalar(m2d[:], m2[:], 1.0 / D, None, ALU.mult))
            step.wait(dve)
            nc.vector.scalar_tensor_tensor(out=var[:], in0=dev2[:], scalar=0.25, in1=m2d[:], op0=ALU.mult,
                                           op1=ALU.add).then_inc(var_ready, 1)
            dve.wait_ge(std_ready, 1)
            step.inc(nc.vector.reciprocal(rstd[:], std[:]))
            step.wait(dve)
            nc.vector.scalar_tensor_tensor(out=shift[:], in0=mean2[:], scalar=-0.5, in1=rstd[:], op0=ALU.mult,
                                           op1=ALU.mult).then_inc(norm_ready, 1)
            dve.wait_ge(act_step, 3)
            step.inc(nc.vector.tensor_copy(mod_cols[:], mod_raw[:]))
            step.wait(dve)
            for n in (2, 6):
                step.inc(nc.vector.tensor_scalar_add(mod_cols[:, n:n + 2], mod_raw[:, n:n + 2], 1.0))
            step.wait(dve)
            step.inc(nc.vector.tensor_scalar(gate_sign[:], gate_raw[:], 0.0, 2.0, ALU.is_ge, ALU.mult))
            step.inc(nc.vector.scalar_tensor_tensor(out=gate_abs[:], in0=gate_raw[:], scalar=-1.0, in1=gate_raw[:],
                                                    op0=ALU.mult, op1=ALU.max))
            step.wait(dve)
            step.inc(nc.vector.tensor_scalar(gate_size[:], gate_abs[:], 0.25, None, ALU.max))
            step.wait(dve)
            nc.vector.scalar_tensor_tensor(out=gates[:], in0=gate_sign[:], scalar=-1.0, in1=gate_size[:],
                                           op0=ALU.add, op1=ALU.mult).then_inc(cols_ready, 1)
            dve.wait_ge(w_in, 16 * 6)
            dve.sem_inc(parts_ready, 2)
            dve.sem_inc(v_kept, 1)
            for u in range(2):
                dve.sem_inc(k_stored[u], 16)
                dve.sem_inc(q_stored[u], 16)
            first = step.n
            per_chunk = 6
            with dve.Fori(0, NC // 2) as it:
                for u in range(2):
                    c = it * 2 + u
                    step = Tally(dve_step, c * per_chunk + first)
                    for n, (full, parts, kept) in enumerate(((kf, kparts, k_stored), (qf, qparts, q_stored))):
                        dve.wait_ge(kq_kept, c * (2 * KD) + (2 * KD + (n + 1) * KD))
                        dve.wait_ge(kept[u], it * (16) + 16)
                        step.inc(nc.vector.tensor_copy(parts[:, u, 0], full[:]))
                        step.wait(dve)
                        step.inc(nc.vector.tensor_tensor(full[:], full[:], parts[:, u, 0], ALU.subtract))
                        step.wait(dve)
                        step.inc(nc.vector.tensor_copy(parts[:, u, 1], full[:]))
                        step.wait(dve)
                        nc.vector.tensor_tensor(parts[:, u, 2], full[:], parts[:, u, 1],
                                                ALU.subtract).then_inc(parts_ready, 1)
                    assert step.n == per_chunk
                    dve.wait_ge(v_ready, c + 3)
                    nc.vector.tensor_tensor(v[:, bass.ds(it * (2 * CB) + u * CB, CB), :], ps_v[:],
                                            bv_rows[:].unsqueeze(1).to_broadcast([P, CB, D]),
                                            ALU.add).then_inc(v_kept, 1)
            dve.wait_ge(v_kept, NC + 1)

def over_tiles(eng, body):
    body(0, False)
    with eng.Fori(1, NC - 1) as tile:
        body(tile, False)
    body(NC - 1, True)


def score_shifts(nc, dram, keep):
    with ExitStack() as ctx:
        def sb(name, shape, dt):
            return ctx.enter_context(nc.sbuf_tensor(name, shape, dt))

        def psum(name, shape, dt):
            return ctx.enter_context(nc.psum_tensor(name, shape, dt))

        def sem(name):
            return ctx.enter_context(nc.semaphore(name))

        ident = keep["ident"]
        BLOCKS = 8
        TOKEN_PARTS = NT // BLOCKS
        W = BLOCKS * P
        HH = H // KD
        RING = 4
        SETS = H * NT // P
        high = [sb(f"sh_high_{n}", [P, KD, S], BF16) for n in "kq"]
        square = [sb(f"sh_square_{n}", [P, 2, KD, W], BF16) for n in "kq"]
        ones = sb("sh_ones", [P, P], F32)
        own = sb("sh_own", [P, HH], BF16)
        first_keys = sb("sh_first_keys", [P, KD, HH, FIRST_KEYS], BF16)
        low = sb("sh_low", [P, H, NT], F32)
        bound2 = sb("sh_bound2", [P, H, NT], F32)
        bound = sb("sh_bound", [P, H, NT], F32)
        width = sb("sh_width", [P, H, NT], F32)
        shift = sb("sh_shift", [P, H, NT], F32)
        longest = sb("sh_longest", [P, H], F32)
        longest_all = sb("sh_longest_all", [H, 1], F32)
        longest_diag = sb("sh_longest_diag", [H, H], F32)
        widest = sb("sh_widest", [P, 1], F32)
        widest_all = sb("sh_widest_all", [1, 1], F32)
        too_wide = sb("sh_too_wide", [1, 1], F32)
        rest = sb("sh_rest", [P, SETS, P], F32)
        parts = sb("sh_parts", [P, 3, SETS, P], BF16)

        ps_low = psum("sh_ps_low", [P, RING, H, FIRST_KEYS], F32)
        ps_norm = [psum(f"sh_ps_norm_{n}", [P, H, NT], F32) for n in "kq"]
        ps_small = psum("sh_ps_small", [P, C], F32)
        ps_turn = psum("sh_ps_turn", [P, SETS, P], F32)

        high_in = [[sem(f"sh_{n}_in_{m}") for m in range(TOKEN_PARTS)] for n in "kq"]
        pool_step = sem("sh_pool_step")
        keys_ready = sem("sh_keys_ready")
        squared = sem("sh_squared")
        low_scored = sem("sh_low_scored")
        low_kept = sem("sh_low_kept")
        norms_ready = sem("sh_norms_ready")
        dve_step = sem("sh_dve_step")
        small_ready = sem("sh_small_ready")
        bound2_ready = sem("sh_bound2_ready")
        bound_ready = sem("sh_bound_ready")
        shift_ready = sem("sh_shift_ready")
        turned = sem("sh_turned")
        parts_ready = sem("sh_parts_ready")
        stored = sem("sh_stored")
        block = ctx.enter_context(nc.Block())

        def load(eng, n, name):
            for part in range(TOKEN_PARTS):
                for m in range(KD):
                    of = dram[name][0:HD, m * HH:(m + 1) * HH, part * W:(part + 1) * W]
                    eng.dma_start(high[n][:, m, part * W:(part + 1) * W], of.rearrange("d h s -> h d s")
                                  ).then_inc(high_in[n][part], 16)

        @block.sync
        def _(sp):
            load(sp, 1, "q_parts")
            load_stack(sp, keep["k_rows"][:, 0:GH * S].rearrange("r (h s) -> r h s", h=GH), dram["k_parts"], K_TERM,
                       slice(0, GH), slice(0, S), keep["k_in"])
            for part in range(3):
                sp.wait_ge(parts_ready, part + 1)
                to = dram["q_parts"][PARTS + part].rearrange("h (t s) -> (h t) s", s=P)
                sp.dma_start(to.rearrange("(n p) s -> p n s", p=P), parts[:, part]).then_inc(stored, 16)
            sp.wait_ge(stored, 16 * 3)

        @block.gpsimd
        def _(pool):
            nc.gpsimd.memset(own[:], 1.0).then_inc(pool_step, 1)
            nc.gpsimd.memset(ones[:], 1.0).then_inc(pool_step, 1)
            pool.wait_ge(pool_step, 1)
            nc.gpsimd.affine_select(out=own[:], in_=own[:], compare_op=ALU.is_ge, fill=0.0, base=0,
                                    pattern=[[-HD, HH]], channel_multiplier=1).then_inc(pool_step, 1)
            pool.wait_ge(pool_step, 3)
            nc.gpsimd.affine_select(out=own[:], in_=own[:], compare_op=ALU.is_ge, fill=0.0, base=HD - 1,
                                    pattern=[[HD, HH]], channel_multiplier=-1).then_inc(pool_step, 1)

        @block.scalar
        def _(act):
            load(act, 0, "k_parts")
            for part in range(TOKEN_PARTS):
                for n in range(2):
                    act.wait_ge(high_in[n][part], 16 * KD)
                    if part >= 2:
                        act.wait_ge(norms_ready, part - 1)
                    nc.scalar.activation(square[n][:, part % 2], high[n][:, :, part * W:(part + 1) * W],
                                         ACT.Square).then_inc(squared, 1)
            act.wait_ge(bound2_ready, 1)
            nc.scalar.activation(bound[:], bound2[:], ACT.Sqrt).then_inc(bound_ready, 1)

        @block.tensor
        def _(pe):
            pe.wait_ge(keys_ready, KD)
            for t in range(NT):
                part = t // BLOCKS
                if t % BLOCKS == 0:
                    pe.wait_ge(high_in[1][part], 16 * KD)
                if t >= RING:
                    pe.wait_ge(low_kept, t - RING + 1)
                for m in range(KD):
                    ins = nc.tensor.matmul(ps_low[:, t % RING, m * HH:(m + 1) * HH, :], high[1][:, m, t * P:(t + 1) * P],
                                           first_keys[:, m], start=True, stop=True)
                ins.then_inc(low_scored, 1)
                if t % BLOCKS == 0:
                    pe.wait_ge(squared, 2 * part + 2)
                for n in range(2):
                    for m in range(KD):
                        ins = nc.tensor.matmul(ps_norm[n][:, m * HH:(m + 1) * HH, t],
                                               square[n][:, part % 2, m, t % BLOCKS * P:(t % BLOCKS + 1) * P],
                                               own[:], start=True, stop=True)
                if t % BLOCKS == BLOCKS - 1:
                    ins.then_inc(norms_ready, 1)
            pe.wait_ge(dve_step, 1)
            nc.tensor.transpose(ps_small[0:H, 0:P], longest[:], ident[:]).then_inc(small_ready, 1)
            pe.wait_ge(dve_step, 3)
            nc.tensor.matmul(ps_small[:, P:P + H], ones[0:H, :], longest_diag[:], start=True,
                             stop=True).then_inc(small_ready, 1)
            pe.wait_ge(shift_ready, 1)
            flat = shift[:].rearrange("p h t -> p (h t)")
            for n in range(SETS):
                ins = nc.tensor.transpose(ps_turn[:, n, :], flat[:, n * P:(n + 1) * P], ident[:])
            ins.then_inc(turned, 1)
            pe.wait_ge(shift_ready, 2)
            nc.tensor.transpose(ps_small[0:1, 2 * P:3 * P], widest[:], ident[:]).then_inc(small_ready, 1)

        @block.vector
        def _(dve):
            dve.wait_ge(high_in[0][0], 16 * KD)
            dve.wait_ge(pool_step, 4)
            for m in range(KD):
                nc.vector.tensor_tensor(first_keys[:, m],
                                        high[0][:, m, 0:FIRST_KEYS].unsqueeze(1).to_broadcast([P, HH, FIRST_KEYS]),
                                        own[:].unsqueeze(2).to_broadcast([P, HH, FIRST_KEYS]),
                                        ALU.mult).then_inc(keys_ready, 1)
            for t in range(NT):
                dve.wait_ge(low_scored, t + 1)
                nc.vector.tensor_reduce(low[:, :, t], ps_low[:, t % RING], AX.X, ALU.max).then_inc(low_kept, 1)
            dve.wait_ge(norms_ready, TOKEN_PARTS)
            step = Tally(dve_step)
            step.inc(nc.vector.tensor_reduce(longest[:], ps_norm[0][:], AX.X, ALU.max))
            dve.wait_ge(small_ready, 1)
            step.inc(nc.vector.tensor_reduce(longest_all[:], ps_small[0:H, 0:P], AX.X, ALU.max))
            step.wait(dve)
            step.inc(nc.vector.tensor_scalar(longest_diag[:], ident[0:H, 0:H], longest_all[:, 0:1], None, ALU.mult))
            dve.wait_ge(small_ready, 2)
            step.inc(nc.vector.tensor_copy(longest[:], ps_small[:, P:P + H]))
            step.wait(dve)
            nc.vector.scalar_tensor_tensor(out=bound2[:], in0=ps_norm[1][:], scalar=SLACK * SLACK,
                                           in1=longest[:].unsqueeze(2).to_broadcast([P, H, NT]),
                                           op0=ALU.mult, op1=ALU.mult).then_inc(bound2_ready, 1)
            dve.wait_ge(low_kept, NT)
            dve.wait_ge(bound_ready, 1)
            step.inc(nc.vector.scalar_tensor_tensor(out=width[:], in0=bound[:], scalar=-ROOM_UP, in1=low[:],
                                                    op0=ALU.add, op1=ALU.max))
            step.wait(dve)
            nc.vector.tensor_scalar(shift[:], width[:], -1.0, None, ALU.mult).then_inc(shift_ready, 1)
            dve.wait_ge(shift_ready, 1)
            step.inc(nc.vector.tensor_tensor(width[:], bound[:], low[:], ALU.subtract))
            step.wait(dve)
            nc.vector.tensor_reduce(widest[:], width[:].rearrange("p h t -> p (h t)"), AX.X,
                                    ALU.max).then_inc(shift_ready, 1)
            dve.wait_ge(turned, 1)
            nc.vector.tensor_copy(parts[:, 0], ps_turn[:]).then_inc(parts_ready, 1)
            dve.wait_ge(parts_ready, 1)
            step.inc(nc.vector.tensor_tensor(rest[:], ps_turn[:], parts[:, 0], ALU.subtract))
            step.wait(dve)
            nc.vector.tensor_copy(parts[:, 1], rest[:]).then_inc(parts_ready, 1)
            dve.wait_ge(parts_ready, 2)
            nc.vector.tensor_tensor(parts[:, 2], rest[:], parts[:, 1], ALU.subtract).then_inc(parts_ready, 1)
            dve.wait_ge(small_ready, 3)
            step.inc(nc.vector.tensor_reduce(widest_all[:], ps_small[0:1, 2 * P:3 * P], AX.X, ALU.max))
            step.wait(dve)
            step.inc(nc.vector.tensor_scalar(too_wide[:], widest_all[:], ROOM_UP + ROOM_DOWN, None,
                                             ALU.is_gt))
            step.wait(dve)
            step.inc(nc.vector.tensor_copy(keep["too_wide"][:], too_wide[:]))
            step.wait(dve)


def row_maxima(nc, dram, keep):
    with ExitStack() as ctx:
        def sb(name, shape, dt):
            return ctx.enter_context(nc.sbuf_tensor(name, shape, dt))

        def psum(name, shape, dt):
            return ctx.enter_context(nc.psum_tensor(name, shape, dt))

        def sem(name):
            return ctx.enter_context(nc.semaphore(name))

        ident, ident_bf, mask = keep["ident"], keep["ident_bf"], keep["mask_qk"]
        U = GH * CB
        BANKS = 4
        K_IN = 16 * len(stack_runs(K_TERM, ROWS))
        Q_IN = 16 * len(stack_runs(Q_TERM, ROWS))
        CUT = 5
        k_rows = sb("mx_k_rows", [ROWS, GH, S], BF16)
        q_rows = sb("mx_q_rows", [ROWS, GH, C], BF16)
        best = sb("mx_best", [P, U], F32)
        edge = sb("mx_edge", [P, GH], F32)
        chunk = sb("mx_chunk", [P, U], F32)
        neg = sb("mx_neg", [U, P], F32)
        parts = sb("mx_parts", [U, 3, P], BF16)
        ps = psum("mx_ps", [P, BANKS, C], F32)
        ps_turn = psum("mx_turn", [U, C], F32)

        k_in = sem("mx_k_in")
        q_in = sem("mx_q_in")
        scored = sem("mx_scored")
        reduced = sem("mx_reduced")
        joined = sem("mx_joined")
        turned = sem("mx_turned")
        cut = sem("mx_cut")
        stored = sem("mx_stored")
        written = sem("mx_written")

        def units_before(tile):
            return tile * (U // 2 + GH) + tile * tile * (U // 2)

        GROUP_UNITS = units_before(NC) - GH

        def joins_before(tile):
            return (tile * tile + tile)

        GROUP_JOINS = joins_before(NC) - 2

        block = ctx.enter_context(nc.Block())

        @block.sync
        def _(sp):
            sp.sem_inc(stored, 16)
            needed = sp.value_load(keep["too_wide"][0:1, 0:1], min_val=0, max_val=1)
            with sp.If(needed > 0):
                with sp.Fori(0, G) as g:
                    with sp.Fori(0, NC) as tile:
                        r = g * NC + tile
                        sp.wait_ge(turned, r + 1)
                        load_stack(sp, q_rows[:], dram["q_parts"], Q_TERM, bass.ds(g * GH, GH),
                                   bass.ds(tile * C, C), q_in, rows=ROWS)
                        load_stack(sp, k_rows[:], dram["k_parts"], K_TERM, bass.ds(g * GH, GH),
                                   slice(0, S), k_in, rows=ROWS)
                        sp.wait_ge(cut, r * CUT + CUT + 1)
                        for part in range(3):
                            to = dram["q_parts"][PARTS + part, bass.ds(g * GH, GH), bass.ds(tile * C, C)]
                            sp.dma_start(to.rearrange("h (j q) -> h j q", q=P), parts[:, part, :]).then_inc(stored, 16)
                        sp.wait_ge(stored, r * 48 + 64)
                        sp.sem_inc(written, 1)

        @block.tensor
        def _(pe):
            pe.sem_inc(turned, 1)
            needed = pe.value_load(keep["too_wide"][0:1, 0:1], min_val=0, max_val=1)
            with pe.If(needed > 0):
                with pe.Fori(0, G) as g:
                    def tile_scores(tile, last):
                        base = pe.snap(g * GROUP_UNITS + units_before(tile))
                        r = g * NC + tile
                        pe.wait_ge(q_in, r * Q_IN + Q_IN)
                        pe.wait_ge(k_in, r * K_IN + K_IN)
                        unit = 0
                        for h in range(GH):
                            for j in range(CB):
                                pe.wait_ge(reduced, base + (unit + 1))
                                out = ps[:, unit % BANKS, :]
                                width = min(j + 2, CB) * P
                                masked = j + 1 < CB
                                ins = nc.tensor.matmul(out[:, 0:width], q_rows[:, h, j * P:(j + 1) * P],
                                                       k_rows[:, h, bass.ds(tile * C, width)],
                                                       start=True, stop=not masked)
                                if masked:
                                    ins = nc.tensor.matmul(out[:, width - P:width], ident_bf[:], mask[:],
                                                           start=False, stop=True)
                                ins.then_inc(scored, 1)
                                unit += 1
                        if not last:
                            for h in range(GH):
                                pe.wait_ge(reduced, base + (unit + 1))
                                out = ps[:, unit % BANKS, 0:P]
                                nc.tensor.matmul(out, q_rows[:, h, C - P:C],
                                                 k_rows[:, h, bass.ds(tile * C + C, P)], start=True, stop=False)
                                nc.tensor.matmul(out, ident_bf[:], mask[:], start=False, stop=True).then_inc(scored, 1)
                                unit += 1
                        if not isinstance(tile, int) or tile > 0:
                            with pe.Fori(0, tile) as kc:
                                for u in range(U):
                                    pe.wait_ge(reduced, base + kc * U + (unit + u + 1))
                                    h, j = u // CB, u % CB
                                    nc.tensor.matmul(ps[:, (unit + u) % BANKS, :], q_rows[:, h, j * P:(j + 1) * P],
                                                     k_rows[:, h, bass.ds(kc * C, C)], start=True,
                                                     stop=True).then_inc(scored, 1)
                        pe.wait_ge(joined, g * GROUP_JOINS + joins_before(tile) + tile * 2 + (0 if last else 2))
                        pe.wait_ge(cut, r * CUT + 1)
                        nc.tensor.transpose(ps_turn[:, 0:P], best[:], ident[:]).then_inc(turned, 1)

                    over_tiles(pe, tile_scores)

        @block.vector
        def _(dve):
            dve.sem_inc(reduced, BANKS)
            dve.sem_inc(cut, 1)
            needed = dve.value_load(keep["too_wide"][0:1, 0:1], min_val=0, max_val=1)
            with dve.If(needed > 0):
                with dve.Fori(0, G) as g:
                    def tile_maxima(tile, last):
                        base = dve.snap(g * GROUP_UNITS + units_before(tile))
                        joins = dve.snap(g * GROUP_JOINS + joins_before(tile))
                        r = g * NC + tile
                        dve.wait_ge(turned, r + 1)
                        unit = 0
                        for h in range(GH):
                            for j in range(CB):
                                dve.wait_ge(scored, base + (unit + 1))
                                width = min(j + 2, CB) * P
                                nc.vector.tensor_reduce(best[:, unit:unit + 1], ps[:, unit % BANKS, 0:width], AX.X,
                                                        ALU.max).then_inc(reduced, 1)
                                unit += 1
                        if not last:
                            for h in range(GH):
                                dve.wait_ge(scored, base + (unit + 1))
                                nc.vector.tensor_reduce(edge[:, h:h + 1], ps[:, unit % BANKS, 0:P], AX.X,
                                                        ALU.max).then_inc(reduced, 1)
                                unit += 1
                            dve.wait_ge(reduced, base + (unit + BANKS))
                            bottom = best[:].rearrange("p (h j) -> p h j", h=GH)[:, :, CB - 1]
                            nc.vector.tensor_tensor(bottom, bottom, edge[:], ALU.max).then_inc(joined, 2)
                        if not isinstance(tile, int) or tile > 0:
                            with dve.Fori(0, tile) as kc:
                                dve.wait_ge(joined, joins + kc * 2 + (0 if last else 2))
                                for u in range(U):
                                    dve.wait_ge(scored, base + kc * U + (unit + u + 1))
                                    nc.vector.tensor_reduce(chunk[:, u:u + 1], ps[:, (unit + u) % BANKS, :], AX.X,
                                                            ALU.max).then_inc(reduced, 1)
                                dve.wait_ge(reduced, base + kc * U + (unit + U + BANKS))
                                nc.vector.tensor_tensor(best[:], best[:], chunk[:], ALU.max).then_inc(joined, 2)
                        dve.wait_ge(turned, r + 2)
                        dve.wait_ge(stored, r * 48 + 16)
                        step = Tally(cut, r * CUT + 1)
                        step.inc(nc.vector.tensor_scalar(neg[:], ps_turn[:, 0:P], -1.0, None, ALU.mult))
                        step.wait(dve)
                        step.inc(nc.vector.tensor_copy(parts[:, 0], neg[:]))
                        step.wait(dve)
                        step.inc(nc.vector.tensor_tensor(neg[:], neg[:], parts[:, 0], ALU.subtract))
                        step.wait(dve)
                        step.inc(nc.vector.tensor_copy(parts[:, 1], neg[:]))
                        step.wait(dve)
                        step.inc(nc.vector.tensor_tensor(parts[:, 2], neg[:], parts[:, 1], ALU.subtract))
                        assert step.n == CUT

                    over_tiles(dve, tile_maxima)


def attention(nc, dram, keep):
    with ExitStack() as ctx:
        def sb(name, shape, dt):
            return ctx.enter_context(nc.sbuf_tensor(name, shape, dt))

        def psum(name, shape, dt):
            return ctx.enter_context(nc.psum_tensor(name, shape, dt))

        def sem(name):
            return ctx.enter_context(nc.semaphore(name))

        ident, ident_bf, mask, v, mixed = (keep[n] for n in ("ident", "ident_bf", "mask_kq", "v", "mixed"))
        CT = 32
        RING = CB
        FAR = RING
        HALF = GH // 2
        K_IN = 16 * len(stack_runs(K_TERM))
        Q_IN = 16 * len(stack_runs(Q_TERM))
        LAG = 2

        k_rows = keep["k_rows"]
        q_rows = sb("at_q_rows", [STACK, 2 * GH * C], BF16)
        probs = sb("at_probs", [P, RING + 1, GH, C], F32)
        v_now = sb("at_v_now", [P, RING + 1, GH, CT], F32)
        out_T = sb("at_out_T", [P, C], F32)
        inv = sb("at_inv", [P, CB, GH], F32)
        warm = sb("at_warm", [P, 1], F32)

        ps_s = psum("at_scores", [P, 2, HALF, C], F32)
        ps_o = psum("at_out", [P, C], F32)
        ps_t = psum("at_turn", [P, CB, P], F32)

        k_in = keep["k_in"]
        q_in = sem("at_q_in")
        v_zeroed = sem("at_v_zeroed")
        ready = sem("at_ready")
        scored = sem("at_scored")
        exped = sem("at_exped")
        slot_free = sem("at_slot_free")
        q_there = sem("at_q_there")
        v_copied = sem("at_v_copied")
        pv_done = sem("at_pv_done")
        out_read = sem("at_out_read")
        turned = sem("at_turned")
        inverted = sem("at_inverted")
        normed = sem("at_normed")

        def steps_before(tile):
            return tile * tile * (CB // 2) + tile * (CB // 2 + 1)

        GROUP_STEPS = steps_before(NC) - 1

        def first_steps(last):
            steps = [(j, (j - 1) * P, (CB - j) if j < CB else FAR) for j in range(CB, 0, -1)]
            return steps[1 if last else 0:] + [(0, 0, 0)]

        block = ctx.enter_context(nc.Block())

        @block.sync
        def _(sp):
            def load_keys(g, half):
                load_stack(sp, k_rows[:, bass.ds(half * (GH * S), GH * S)].rearrange("r (h s) -> r h s", h=GH),
                           dram["k_parts"], K_TERM, bass.ds(g * GH, GH), slice(0, S), k_in)

            def load_queries(g, tile, half):
                sp.wait_ge(turned, g * NC + tile + 1)
                load_stack(sp, q_rows[:, bass.ds(half * (GH * C), GH * C)].rearrange("r (h s) -> r h s", h=GH),
                           dram["q_parts"], Q_TERM, bass.ds(g * GH, GH), bass.ds(tile * C, C), q_in)
                sp.wait_ge(q_in, g * (NC * Q_IN) + tile * Q_IN + Q_IN)
                sp.sem_inc(q_there, 1)

            def group(g, last):
                for tile in range(4):
                    load_queries(g, tile, tile % 2)
                if not last:
                    sp.wait_ge(k_in, g * K_IN + K_IN)
                    load_keys(g + 1, (g + 1) % 2)
                with sp.Fori(2, NC // 2) as pair:
                    for u in range(2):
                        load_queries(g, pair * 2 + u, u)

            with sp.Fori(0, G - 1) as g:
                group(g, False)
            group(G - 1, True)
            sp.wait_ge(k_in, G * K_IN)

        @block.gpsimd
        def _(pool):
            nc.gpsimd.memset(v_now[:], 0.0).then_inc(v_zeroed, 1)
            nc.gpsimd.memset(probs[:, 0], 0.0).then_inc(ready, 1)
            pool.wait_ge(v_zeroed, 1)
            nc.gpsimd.memset(v_now[:, :, :, HD:HD + 1], 1.0).then_inc(ready, 1)
            pool.wait_ge(ready, 3)
            pool.sem_inc(v_copied, LAG)
            with pool.Fori(0, G) as g:
                def copy(n, kb, slot):
                    pool.wait_ge(pv_done, n + 1)
                    pool.sem_inc(slot_free, 1)
                    nc.gpsimd.tensor_copy(v_now[:, slot, :, 0:HD],
                                          v[:, bass.ds(kb, 1), bass.ds(g * (GH * HD), GH * HD)].rearrange(
                                              "p a (h d) -> p (a h) d", h=GH)).then_inc(v_copied, 1)

                def tile_values(tile, last):
                    n = pool.snap(g * GROUP_STEPS + steps_before(tile))
                    steps = first_steps(last)
                    for i, (j, _, slot) in enumerate(steps):
                        copy(n + i, tile * CB + j if j else 0, slot)
                    if not isinstance(tile, int) or tile > 0:
                        with pool.Fori(0, tile) as it:
                            for u in range(CB):
                                copy(n + it * CB + (len(steps) + u), it * CB + (u + 1), (u + 1) % RING)

                over_tiles(pool, tile_values)

        @block.tensor
        def _(pe):
            def scores(n, half, kb, first, place, edge):
                k_at, q_at = place
                pe.wait_ge(exped, n * 2 + (half + 3))
                for i in range(HALF):
                    h = half * HALF + i
                    ins = nc.tensor.matmul(ps_s[:, half, i, first:C],
                                           k_rows[:, bass.ds(k_at + kb * P + h * S, P)],
                                           q_rows[:, bass.ds(q_at + (h * C + first), C - first)],
                                           start=True, stop=not edge)
                    if edge:
                        ins = nc.tensor.matmul(ps_s[:, half, i, first:first + P], ident_bf[:], mask[:],
                                               start=False, stop=True)
                ins.then_inc(scored, 1)

            def product(n, first, slot, start):
                pe.wait_ge(v_copied, n + 1)
                pe.wait_ge(exped, n * 2 + 2)
                for h in range(GH):
                    ins = nc.tensor.matmul(ps_o[h * CT:(h + 1) * CT, first:C], v_now[:, slot, h, :],
                                           probs[:, slot, h, first:C], start=start, stop=False,
                                           skip_group_check=True)
                ins.then_inc(pv_done, 1)

            def transposes(r):
                pe.wait_ge(out_read, r + 1)
                pe.wait_ge(normed, r + 1)
                for j in range(CB):
                    ins = nc.tensor.transpose(ps_t[:, j, :], out_T[:, j * P:(j + 1) * P], ident[:])
                ins.then_inc(turned, 1)

            pe.wait_ge(ready, 3)
            pe.sem_inc(turned, 1)
            pe.sem_inc(pv_done, LAG)
            for h in range(GH):
                nc.tensor.matmul(ps_o[h * CT:(h + 1) * CT, :], v_now[:, 0, h, :], probs[:, 0, h, :], start=True,
                                 stop=False, skip_group_check=True)
            with pe.Fori(0, G) as g:
                def tile_steps(tile, last):
                    n = pe.snap(g * GROUP_STEPS + steps_before(tile))
                    r = g * NC + tile
                    place = (pe.snap((g % 2) * (GH * S)),
                             (tile % 2) * (GH * C) if isinstance(tile, int) else pe.snap((tile % 2) * (GH * C)))
                    pe.wait_ge(k_in, g * K_IN + K_IN)
                    pe.wait_ge(q_in, r * Q_IN + Q_IN)
                    steps = first_steps(last)
                    waiting = [(0, RING - 1, False), (0, 0, False)]
                    for i, (j, first, slot) in enumerate(steps):
                        kb = tile * CB + j if j else 0
                        scores(n + i, 0, kb, first, place, j > 0)
                        if i == LAG:
                            pe.wait_ge(out_read, r + 1)
                        product(n + i, *waiting.pop(0))
                        scores(n + i, 1, kb, first, place, j > 0)
                        if i == LAG + 1:
                            transposes(r)
                        waiting.append((first, slot, i == 0))
                    if not isinstance(tile, int) or tile > 0:
                        with pe.Fori(0, tile) as it:
                            for u in range(CB):
                                m = n + it * CB + (len(steps) + u)
                                scores(m, 0, it * CB + (u + 1), 0, place, False)
                                product(m, 0, (u + 1 - LAG) % RING, False)
                                scores(m, 1, it * CB + (u + 1), 0, place, False)

                over_tiles(pe, tile_steps)
            product(G * GROUP_STEPS, 0, RING - 1, False)
            product(G * GROUP_STEPS + 1, 0, 0, False)
            transposes(G * NC)

        @block.scalar
        def _(act):
            nc.scalar.activation(warm[:], ident[:, 0:1], ACT.Exp).then_inc(exped, 1)
            act.sem_inc(exped, 3)
            with act.Fori(0, G) as g:
                def exponentials(n, first, slot):
                    for half in range(2):
                        act.wait_ge(scored, n * 2 + (half + 1))
                        if half == 0:
                            act.wait_ge(pv_done, n + 1)
                        heads = slice(half * HALF, (half + 1) * HALF)
                        nc.scalar.activation(probs[:, slot, heads, first:C], ps_s[:, half, :, first:C],
                                             ACT.Exp).then_inc(exped, 1)

                def tile_exponentials(tile, last):
                    n = act.snap(g * GROUP_STEPS + steps_before(tile))
                    steps = first_steps(last)
                    for i, (_, first, slot) in enumerate(steps):
                        exponentials(n + i, first, slot)
                    if not isinstance(tile, int) or tile > 0:
                        with act.Fori(0, tile) as it:
                            for u in range(CB):
                                exponentials(n + it * CB + (len(steps) + u), 0, (u + 1) % RING)

                over_tiles(act, tile_exponentials)

        @block.vector
        def _(dve):
            nc.vector.memset(probs[:, RING - 1], 0.0).then_inc(ready, 1)
            nc.vector.memset(out_T[:], 0.0).then_inc(out_read, 1)
            dve.sem_inc(normed, 2)
            with dve.Fori(0, G) as g:
                def tile_out(tile, last):
                    n = dve.snap(g * GROUP_STEPS + steps_before(tile))
                    r = g * NC + tile
                    dve.wait_ge(pv_done, n + tile * CB + (len(first_steps(last)) + 2 * LAG))
                    dve.wait_ge(turned, r + 2)
                    nc.vector.tensor_copy(out_T[:], ps_o[:]).then_inc(out_read, 1)
                    dve.wait_ge(turned, r + 3)
                    heads = ps_t[:].rearrange("p j (h c) -> p j h c", h=GH)
                    nc.vector.reciprocal(inv[:], heads[:, :, :, HD]).then_inc(inverted, 1)
                    dve.wait_ge(inverted, r + 1)
                    to = mixed[:, bass.ds(tile * CB, CB), bass.ds(g * (GH * HD), GH * HD)]
                    nc.vector.tensor_tensor(to.rearrange("p j (h d) -> p j h d", h=GH), heads[:, :, :, 0:HD],
                                            inv[:].unsqueeze(3).to_broadcast([P, CB, GH, HD]),
                                            ALU.mult).then_inc(normed, 1)

                over_tiles(dve, tile_out)


def route(nc, dram, keep):
    with ExitStack() as ctx:
        def sb(name, shape, dt):
            return ctx.enter_context(nc.sbuf_tensor(name, shape, dt))

        def psum(name, shape, dt):
            return ctx.enter_context(nc.psum_tensor(name, shape, dt))

        def sem(name):
            return ctx.enter_context(nc.semaphore(name))

        ident, gates, mod_cols, mixed = (keep[n] for n in ("ident", "gates", "mod_cols", "mixed"))
        xs = keep["w2"][:, E - 3].rearrange("p (u j) d -> p u j d", u=2)
        m_now = keep["w2"][:, E - 2].rearrange("p (u j) d -> p u j d", u=2)
        spare = keep["w2"][:, E - 1]
        wo = sb("rt_wo", [P, KD, D], F32)
        gate_w = sb("rt_gate_w", [P, KD, E], F32)
        gate_b = sb("rt_gate_b", [P, E], F32)
        bo_gated = sb("rt_bo_gated", [P, D], F32)
        b1_rows = sb("rt_b1_rows", [E * FF, P], F32)
        x_now = sb("rt_x_now", [P, 2, CB, D], F32)
        aT = sb("rt_aT", [P, KD, C], F32)
        hT = sb("rt_hT", [P, KD, C], F32)
        gated = sb("rt_gated", [P, CB, D], F32)
        stats = sb("rt_stats", [P, CB, 6], F32)
        mean_var = sb("rt_mean_var", [P, CB, 2], F32)
        eps = sb("rt_eps", [P, 1], F32)
        std = sb("rt_std", [P, CB], F32)
        rstd = sb("rt_rstd", [P, CB], F32)
        shift = sb("rt_shift", [P, CB], F32)
        score = sb("rt_score", [P, CB, E], F32)
        masked = sb("rt_masked", [P, CB, E], F32)
        equal = sb("rt_equal", [P, CB, E], F32)
        top = [sb(f"rt_top_{i}", [P, CB], F32) for i in range(2)]
        least = sb("rt_least", [P, CB], F32)
        order = sb("rt_order", [P, E], F32)
        both = sb("rt_both", [P, CB, E], BF16)
        rank = sb("rt_rank", [P, CB, E], F32)
        row_now = sb("rt_row_now", [P, CB, 2], F32)
        row_int = sb("rt_row_int", [P, 2, CB, 2], U32)
        *pick, moved = (spare[:, i].rearrange("p (t e) -> p t e", e=E) for i in range(3))
        filled = spare[:, 3].rearrange("p (e t) -> p e t", e=E)
        row_of = sb("rt_row_of", [P, NT, 2], F32)
        apart = sb("rt_apart", [P, NT], F32)
        before_bf = sb("rt_before", [P, P], BF16)
        ones_bf = sb("rt_ones", [P, P], BF16)
        ex = sb("rt_ex", [P, NT], F32)
        den = sb("rt_den", [P, NT], F32)
        queue_start = sb("rt_queue_start", [P, E], F32)
        queue_end = sb("rt_queue_end", [P, E], F32)
        end_int = sb("rt_end_int", [1, E], I32)
        zeros = sb("rt_zeros", [P, D], F32)
        starts_at = sb("rt_starts_at", [P, NT], F32)
        count = sb("rt_count", [P, E], F32)
        tiles = sb("rt_tiles", [P, E], F32)
        run = [sb(f"rt_run_{i}", [P, E], F32) for i in range(2)]
        start = sb("rt_start", [P, E], F32)
        offset = sb("rt_offset", [P, E], F32)
        offset_step = sb("rt_offset_step", [1, E], F32)
        shift_by = sb("rt_shift_by", [P, NT], F32)
        tile_no = sb("rt_tile_no", [1, TILES + 1], F32)
        begun = sb("rt_begun", [1, TILES + 1, E], F32)
        owner = sb("rt_owner", [1, TILES + 1], F32)
        row = sb("rt_row", [1, TILES + 1], F32)

        ps_a = psum("rt_ps_a", [P, KD, C], F32)
        ps_o = psum("rt_ps_o", [P, CB, D], F32)
        ps_t = psum("rt_ps_t", [P, KD, C], F32)
        ps_g = psum("rt_ps_g", [P, C], F32)
        ps_r = psum("rt_ps_r", [P, C], F32)

        w_in = sem("rt_w_in")
        x_in = [sem(f"rt_x_in_{u}") for u in range(2)]
        pool_step = sem("rt_pool_step")
        dve_step = sem("rt_dve_step")
        m_in = [sem(f"rt_m_in_{u}") for u in range(2)]
        sum_seen = sem("rt_sum_seen")
        stats_seen = sem("rt_stats_seen")
        x_biased = sem("rt_x_biased")
        m_turned = sem("rt_m_turned")
        a_kept = sem("rt_a_kept")
        projected = sem("rt_projected")
        o_read = sem("rt_o_read")
        sum_ready = sem("rt_sum_ready")
        var_ready = sem("rt_var_ready")
        std_ready = sem("rt_std_ready")
        norm_ready = sem("rt_norm_ready")
        xs_ready = sem("rt_xs_ready")
        x_turned = sem("rt_x_turned")
        h_kept = sem("rt_h_kept")
        scored = sem("rt_scored")
        score_kept = sem("rt_score_kept")
        b1_turned = sem("rt_b1_turned")
        tops_ready = sem("rt_tops_ready")
        ex_ready = sem("rt_ex_ready")
        both_ready = sem("rt_both_ready")
        counted = sem("rt_counted")
        count_read = sem("rt_count_read")
        pick_step = sem("rt_pick_step")
        rows_placed = sem("rt_rows_placed")
        may_scatter = sem("rt_may_scatter")
        scattered = [sem(f"rt_scattered_{u}") for u in range(2)]
        ends_ready = sem("rt_ends_ready")
        ends_cleared = sem("rt_ends_cleared")
        bias_ready = sem("rt_bias_ready")

        x_v = dram["x"].rearrange("a (t p) d -> p (a t) d", p=P)
        block = ctx.enter_context(nc.Block())

        def pairs(eng, body, begin, end):
            with eng.Fori(begin, end) as it:
                for u in range(2):
                    body(it * 2 + u, u, it)

        PAIRS = NC // 2
        W1_SHARE = E // NC
        SCATTERS = CB * 2 * 16

        @block.sync
        def _(sp):
            def load(c, u, it):
                chunk = bass.ds(c * CB, CB)
                sp.wait_ge(m_turned, c + 1)
                sp.dma_start(m_now[:, u], mixed[:, chunk, :]).then_inc(m_in[u], 16)
                sp.wait_ge(sum_ready, c + 1)
                sp.dma_start(x_now[:, u], x_v[:, chunk, :]).then_inc(x_in[u], 16)
                share = bass.ds(c * W1_SHARE, W1_SHARE)
                sp.dma_start(keep["w1"][:, share].rearrange("p e k f -> p (e k) f"),
                             dram["W1"][share].rearrange("e (k p) f -> p (e k) f", p=P)
                             ).then_inc(keep["weights_in"], 16)

            def load_w2(e):
                e = bass.ds(e, 1)
                sp.dma_start(keep["w2"][:, e].rearrange("p e f d -> p (e f) d"),
                             dram["W2"][e].rearrange("e (f p) d -> p (e f) d", p=P)
                             ).then_inc(keep["weights_in"], 16)

            def load_more(c, u, it):
                load(c, u, it)
                load_w2(c)

            pairs(sp, load_more, 0, PAIRS // 2)
            pairs(sp, load, PAIRS // 2, PAIRS)
            sp.dma_start(keep["b2"][:], dram["b2"].rearrange("(a e) d -> a e d", a=1).partition_broadcast(P)
                         ).then_inc(keep["weights_in"], 16)
            for e in range(NC // 2, E - 3):
                load_w2(e)
            sp.wait_ge(ends_ready, 1)
            for e in range(E):
                end = sp.value_load(end_int[0:1, e:e + 1], min_val=e * QROWS, max_val=e * QROWS + S)
                sp.dma_start(dram["queue"][bass.ds(end, P), :], zeros[:]).then_inc(ends_cleared, 16)
            sp.wait_ge(ends_cleared, 16 * E)

        @block.gpsimd
        def _(pool):
            nc.gpsimd.iota(order[:], pattern=[[1, E]], base=-E, channel_multiplier=0,
                           allow_small_or_imprecise_dtypes=True).then_inc(pool_step, 1)
            nc.gpsimd.iota(starts_at[:], pattern=[[P, NT]], base=0, channel_multiplier=0,
                           allow_small_or_imprecise_dtypes=True).then_inc(pool_step, 1)
            nc.gpsimd.iota(queue_start[:], pattern=[[QROWS, E]], base=0, channel_multiplier=0,
                           allow_small_or_imprecise_dtypes=True).then_inc(pool_step, 1)
            nc.gpsimd.iota(queue_end[:], pattern=[[QROWS, E]], base=0, channel_multiplier=0,
                           allow_small_or_imprecise_dtypes=True).then_inc(pool_step, 1)
            nc.gpsimd.memset(zeros[:], 0.0).then_inc(pool_step, 1)
            nc.gpsimd.iota(tile_no[:], pattern=[[1, TILES + 1]], base=0, channel_multiplier=0,
                           allow_small_or_imprecise_dtypes=True).then_inc(pool_step, 1)
            nc.gpsimd.memset(ones_bf[:], 1.0).then_inc(pool_step, 1)
            pool.wait_ge(pool_step, 7)
            nc.gpsimd.affine_select(out=before_bf[:], in_=ones_bf[:], compare_op=ALU.is_gt, fill=0.0, base=0,
                                    pattern=[[1, P]], channel_multiplier=-1).then_inc(pool_step, 1)
            pool.wait_ge(w_in, 16 * 5)
            nc.gpsimd.tensor_tensor(bo_gated[:], bo_gated[:], gates[:, 0, :], ALU.mult).then_inc(pool_step, 1)
            pool.wait_ge(pool_step, 9)

            def add_bias(c, u, it):
                pool.wait_ge(x_in[u], it * 16 + 16)
                nc.gpsimd.tensor_tensor(x_now[:, u], x_now[:, u],
                                        bo_gated[:].unsqueeze(1).to_broadcast([P, CB, D]),
                                        ALU.add).then_inc(x_biased, 1)

            def scatter(c, u):
                pool.wait_ge(rows_placed, c + 1)
                pool.sem_inc(may_scatter, 1)
                for j in range(CB):
                    for i in range(2):
                        pool.indirect_dma_start(
                            dram["queue"], bass.IndirectOffsetOnAxis(ap=row_int[:, u, j, i:i + 1], axis=0),
                            xs[:, u, j, :], None).then_inc(scattered[u], 16)

            for u in range(2):
                add_bias(u, u, 0)

            def chunk_steps(c, u, it):
                add_bias(c + 2, u, it + 1)
                scatter(c, u)

            pairs(pool, chunk_steps, 0, PAIRS - 1)
            for u in range(2):
                scatter(NC - 2 + u, u)
            for u in range(2):
                pool.wait_ge(scattered[u], PAIRS * SCATTERS)

        @block.tensor
        def _(pe):
            pe.wait_ge(w_in, 16 * 5)
            nc.tensor.transpose(ps_t[:, 0, 0:E * FF], b1_rows[:], ident[0:E * FF, 0:E * FF]).then_inc(b1_turned, 1)
            pe.wait_ge(bias_ready, 1)
            pe.sem_inc(m_turned, 2)
            pe.sem_inc(projected, 1)
            pe.sem_inc(scored, 1)
            pe.wait_ge(pool_step, 9)

            def project(c, u, it):
                pe.wait_ge(m_in[u], it * 16 + 16)
                pe.wait_ge(a_kept, c + 1)
                for k in range(KD):
                    for j in range(CB):
                        ins = nc.tensor.transpose(ps_a[:, k, j * P:(j + 1) * P],
                                                  m_now[:, u, j, k * P:(k + 1) * P], ident[:])
                ins.then_inc(m_turned, 1)
                pe.wait_ge(a_kept, c + 2)
                pe.wait_ge(o_read, c + 1)
                for j in range(CB):
                    for k in range(KD):
                        ins = nc.tensor.matmul(ps_o[:, j, :], aT[:, k, j * P:(j + 1) * P], wo[:, k, :],
                                               start=k == 0, stop=k == KD - 1)
                ins.then_inc(projected, 1)

            def score_chunk(c, u):
                pe.wait_ge(xs_ready, c * CB + 2 * CB)
                pe.wait_ge(h_kept, c + 1)
                for k in range(KD):
                    for j in range(CB):
                        ins = nc.tensor.transpose(ps_t[:, k, j * P:(j + 1) * P],
                                                  xs[:, u, j, k * P:(k + 1) * P], ident[:])
                ins.then_inc(x_turned, 1)
                pe.wait_ge(h_kept, c + 2)
                pe.wait_ge(score_kept, c + 1)
                for j in range(CB):
                    for k in range(KD):
                        ins = nc.tensor.matmul(ps_g[:, j * E:(j + 1) * E], hT[:, k, j * P:(j + 1) * P],
                                               gate_w[:, k, :], start=k == 0, stop=k == KD - 1)
                ins.then_inc(scored, 1)

            def count_chunk(c):
                pe.wait_ge(both_ready, c + 1)
                pe.wait_ge(count_read, c + 1)
                for j in range(CB):
                    for i in range(j + 1):
                        nc.tensor.matmul(ps_r[:, j * E:(j + 1) * E], (before_bf if i == j else ones_bf)[:],
                                         both[:, i, :], start=i == 0, stop=i == j)
                for i in range(CB):
                    ins = nc.tensor.matmul(ps_r[:, CB * E:(CB + 1) * E], ones_bf[:], both[:, i, :],
                                           start=i == 0, stop=i == CB - 1)
                ins.then_inc(counted, 1)

            project(0, 0, 0)
            project(1, 1, 0)
            score_chunk(0, 0)
            with pe.Fori(0, PAIRS - 1) as it:
                for u in (1, 0):
                    c = it * 2 + (2 - u)
                    project(c + 1, 1 - u, it + 1)
                    count_chunk(c - 1)
                    score_chunk(c, u)
            count_chunk(NC - 2)
            score_chunk(NC - 1, 1)
            count_chunk(NC - 1)

        @block.scalar
        def _(act):
            act.dma_start(wo[:], dram["Wo"].rearrange("(k p) n -> p k n", p=P)).then_inc(w_in, 16)
            act.dma_start(gate_w[:], dram["gate_w"].rearrange("(k p) n -> p k n", p=P)).then_inc(w_in, 16)
            act.dma_start(gate_b[:], dram["gate_b"].rearrange("(a n) -> a n", a=1).partition_broadcast(P)
                          ).then_inc(w_in, 16)
            act.dma_start(bo_gated[:], dram["bo"].rearrange("(a n) -> a n", a=1).partition_broadcast(P)
                          ).then_inc(w_in, 16)
            act.dma_start(b1_rows[:], dram["b1"].rearrange("e (f p) -> (e f) p", p=P)).then_inc(w_in, 16)
            act.wait_ge(b1_turned, 1)
            nc.scalar.copy(keep["b1"][:], ps_t[:, 0, 0:E * FF]).then_inc(bias_ready, 1)
            act.wait_ge(pool_step, 9)
            act.sem_inc(a_kept, 1)
            act.wait_ge(bias_ready, 1)
            act.sem_inc(h_kept, 1)
            act.sem_inc(xs_ready, CB)
            act.wait_ge(dve_step, 1)
            nc.scalar.activation(std[:, 0:1], eps[:], ACT.Sqrt).then_inc(std_ready, 1)

            def keep_turned(c):
                act.wait_ge(m_turned, c + 3)
                act.wait_ge(projected, c + 1)
                nc.scalar.copy(aT[:], ps_a[:]).then_inc(a_kept, 1)

            def normalise(c, u, it):
                act.wait_ge(var_ready, c + 1)
                nc.scalar.activation(std[:], mean_var[:, :, 1], ACT.Sqrt, bias=eps[:, 0:1]).then_inc(std_ready, 1)
                act.wait_ge(norm_ready, c + 1)
                if not isinstance(it, int) or it > 0:
                    act.wait_ge(scattered[u], it * SCATTERS)
                for j in range(CB):
                    nc.scalar.activation(xs[:, u, j, :], mixed[:, bass.ds(c * CB + j, 1), :].rearrange("p a d -> p (a d)"),
                                         ACT.Identity, scale=rstd[:, j:j + 1],
                                         bias=shift[:, j:j + 1]).then_inc(xs_ready, 1)
                act.wait_ge(x_turned, c + 1)
                act.wait_ge(scored, c + 1)
                for k in range(KD):
                    ins = nc.scalar.activation(hT[:, k, :], ps_t[:, k, :], ACT.Identity,
                                               scale=mod_cols[:, 6 + k:7 + k], bias=mod_cols[:, 4 + k:5 + k])
                ins.then_inc(h_kept, 1)

            def chunk_steps(c, u, it):
                keep_turned(c + 1)
                normalise(c, u, it)

            keep_turned(0)
            for u in range(2):
                chunk_steps(u, u, 0)
            pairs(act, chunk_steps, 1, PAIRS - 1)
            chunk_steps(NC - 2, 0, PAIRS - 1)
            normalise(NC - 1, 1, PAIRS - 1)
            act.wait_ge(tops_ready, 1)
            nc.scalar.activation(ex[:], apart[:], ACT.Exp).then_inc(ex_ready, 1)
            act.wait_ge(h_kept, NC + 1)

        @block.vector
        def _(dve):
            step = Tally(dve_step)
            step.inc(nc.vector.memset(eps[:], EPS))
            dve.sem_inc(sum_ready, 2)
            dve.sem_inc(o_read, 1)
            dve.sem_inc(score_kept, 1)
            dve.wait_ge(w_in, 16 * 5)
            STEPS = 2
            first = step.n

            def sum_chunk(c, u):
                step = Tally(dve_step, c * STEPS + first)
                dve.wait_ge(projected, c + 2)
                nc.vector.tensor_tensor(gated[:], ps_o[:], gates[:, 0, :].unsqueeze(1).to_broadcast([P, CB, D]),
                                        ALU.mult).then_inc(o_read, 1)
                dve.wait_ge(o_read, c + 2)
                dve.wait_ge(x_biased, c + 1)
                chunk = mixed[:, bass.ds(c * CB, CB), :]
                nc.vector.tensor_tensor(chunk, gated[:], x_now[:, u], ALU.add).then_inc(sum_ready, 1)
                dve.wait_ge(sum_ready, c + 3)
                dve.sem_inc(sum_seen, 1)
                for j in range(CB):
                    ins = nc.vector.bn_stats(stats[:, j, :],
                                             mixed[:, bass.ds(c * CB + j, 1), :].rearrange("p a d -> p (a d)"))
                step.inc(ins)
                step.wait(dve)
                dve.wait_ge(xs_ready, c * CB + CB)
                dve.sem_inc(stats_seen, 1)
                for j in range(CB):
                    ins = nc.vector.bn_aggr(mean_var[:, j, :], stats[:, j, :])
                ins.then_inc(var_ready, 1)
                dve.wait_ge(std_ready, c + 2)
                step.inc(nc.vector.reciprocal(rstd[:], std[:]))
                step.wait(dve)
                nc.vector.scalar_tensor_tensor(out=shift[:], in0=mean_var[:, :, 0], scalar=-1.0, in1=rstd[:],
                                               op0=ALU.mult, op1=ALU.mult).then_inc(norm_ready, 1)
                assert step.n == STEPS

            def route_chunk(c, u):
                step = Tally(pick_step, c * PICK_STEPS)
                blocks = bass.ds(c * CB, CB)

                def wide(ap):
                    return ap.unsqueeze(2).to_broadcast([P, CB, E])

                experts = order[:].unsqueeze(1).to_broadcast([P, CB, E])
                dve.wait_ge(scored, c + 2)
                nc.vector.tensor_tensor(score[:], ps_g[:, 0:CB * E].rearrange("p (j e) -> p j e", e=E),
                                        gate_b[:].unsqueeze(1).to_broadcast([P, CB, E]),
                                        ALU.add).then_inc(score_kept, 1)
                dve.wait_ge(score_kept, c + 2)
                values = score
                for i in range(2):
                    step.inc(nc.vector.tensor_reduce(top[i][:], values[:], AX.X, ALU.max))
                    step.wait(dve)
                    step.inc(nc.vector.tensor_tensor(equal[:], values[:], wide(top[i][:]), ALU.is_equal))
                    step.wait(dve)
                    step.inc(nc.vector.tensor_tensor(equal[:], equal[:], experts, ALU.mult))
                    step.wait(dve)
                    step.inc(nc.vector.tensor_reduce(least[:], equal[:], AX.X, ALU.min))
                    step.wait(dve)
                    step.inc(nc.vector.tensor_tensor(pick[i][:, blocks], experts, wide(least[:]), ALU.is_equal))
                    step.wait(dve)
                    if i == 0:
                        step.inc(nc.vector.scalar_tensor_tensor(out=masked[:], in0=pick[0][:, blocks], scalar=MASKED,
                                                                in1=score[:], op0=ALU.mult, op1=ALU.add))
                        step.wait(dve)
                        values = masked
                nc.vector.tensor_tensor(both[:], pick[0][:, blocks], pick[1][:, blocks], ALU.add
                                        ).then_inc(both_ready, 1)
                step.inc(nc.vector.tensor_tensor(apart[:, blocks], top[1][:], top[0][:], ALU.subtract))
                dve.wait_ge(counted, c + 1)
                step.inc(nc.vector.tensor_tensor(rank[:], ps_r[:, 0:CB * E].rearrange("p (j e) -> p j e", e=E),
                                                 queue_end[:].unsqueeze(1).to_broadcast([P, CB, E]), ALU.add))
                step.wait(dve)
                nc.vector.tensor_tensor(queue_end[:], queue_end[:], ps_r[:, CB * E:(CB + 1) * E], ALU.add
                                        ).then_inc(count_read, 1)
                for i in range(2):
                    step.inc(nc.vector.tensor_tensor(equal[:], rank[:], pick[i][:, blocks], ALU.mult))
                    step.wait(dve)
                    step.inc(nc.vector.tensor_reduce(row_now[:, :, i], equal[:], AX.X, ALU.add))
                    step.wait(dve)
                nc.vector.tensor_copy(row_int[:, u], row_now[:]).then_inc(rows_placed, 1)
                step.inc(nc.vector.tensor_scalar(row_of[:, blocks, :], row_now[:], 1.0, None, ALU.mult))
                step.wait(dve)
                dve.wait_ge(rows_placed, c + 1)
                dve.wait_ge(count_read, c + 2)
                assert step.n == PICK_STEPS

            def chunk_steps(c, u, it):
                sum_chunk(c, u)
                route_chunk(c - 1, 1 - u)

            PICK_STEPS = 18
            dve.sem_inc(count_read, 1)
            dve.wait_ge(pool_step, 9)
            sum_chunk(0, 0)
            chunk_steps(1, 1, 0)
            pairs(dve, chunk_steps, 1, PAIRS)
            route_chunk(NC - 1, 1)
            step = Tally(dve_step, first + NC * STEPS)
            nc.vector.tensor_copy(end_int[:], queue_end[0:1, :]).then_inc(ends_ready, 1)
            dve.sem_inc(tops_ready, 1)
            step.inc(nc.vector.tensor_tensor(count[:], queue_end[:], queue_start[:], ALU.subtract))
            step.wait(dve)
            step.inc(nc.vector.tensor_tensor(filled, count[:].unsqueeze(2).to_broadcast([P, E, NT]),
                                             starts_at[:].unsqueeze(1).to_broadcast([P, E, NT]), ALU.is_gt))
            step.wait(dve)
            step.inc(nc.vector.tensor_reduce(tiles[:], filled, AX.X, ALU.add))
            step.wait(dve)
            sums, n, reach = tiles, 0, 1
            while reach < E:
                to = run[n % 2]
                step.inc(nc.vector.tensor_copy(to[:, 0:reach], sums[:, 0:reach]))
                step.inc(nc.vector.tensor_tensor(to[:, reach:], sums[:, reach:], sums[:, 0:E - reach], ALU.add))
                step.wait(dve)
                sums, n, reach = to, n + 1, reach * 2
            step.inc(nc.vector.tensor_tensor(start[:], sums[:], tiles[:], ALU.subtract))
            step.wait(dve)
            step.inc(nc.vector.scalar_tensor_tensor(out=offset[:], in0=start[:], scalar=float(P), in1=queue_start[:],
                                                    op0=ALU.mult, op1=ALU.subtract))
            step.inc(nc.vector.tensor_tensor(begun[:], tile_no[:].unsqueeze(2).to_broadcast([1, TILES + 1, E]),
                                             start[0:1, :].unsqueeze(1).to_broadcast([1, TILES + 1, E]), ALU.is_ge))
            step.wait(dve)
            step.inc(nc.vector.tensor_reduce(owner[:], begun[:], AX.X, ALU.add))
            step.inc(nc.vector.tensor_copy(offset_step[:, 0:1], offset[0:1, 0:1]))
            step.inc(nc.vector.tensor_tensor(offset_step[:, 1:], offset[0:1, 1:], offset[0:1, 0:E - 1], ALU.subtract))
            step.wait(dve)
            step.inc(nc.vector.tensor_scalar(keep["owner"][:], owner[:], -1.0, None, ALU.add))
            step.inc(nc.vector.tensor_tensor(begun[:], begun[:],
                                             offset_step[:].unsqueeze(1).to_broadcast([1, TILES + 1, E]), ALU.mult))
            step.wait(dve)
            step.inc(nc.vector.tensor_reduce(row[:], begun[:], AX.X, ALU.add))
            step.wait(dve)
            step.inc(nc.vector.scalar_tensor_tensor(out=row[:], in0=tile_no[:], scalar=float(P), in1=row[:],
                                                    op0=ALU.mult, op1=ALU.subtract))
            step.wait(dve)
            step.inc(nc.vector.tensor_scalar(keep["row_of_tile"][:], row[:], queue_end[0:1, E - 1:E], None, ALU.min))
            for i in range(2):
                step.inc(nc.vector.tensor_tensor(moved, pick[i], offset[:].unsqueeze(1).to_broadcast([P, NT, E]),
                                                 ALU.mult))
                step.wait(dve)
                step.inc(nc.vector.tensor_reduce(shift_by[:], moved, AX.X, ALU.add))
                step.wait(dve)
                step.inc(nc.vector.tensor_tensor(row_of[:, :, i], row_of[:, :, i], shift_by[:], ALU.add))
                step.wait(dve)
            step.inc(nc.vector.tensor_copy(keep["slots"][:], row_of[:].rearrange("p t i -> p (t i)")))
            dve.wait_ge(ex_ready, 1)
            step.inc(nc.vector.tensor_scalar_add(den[:], ex[:], 1.0))
            step.wait(dve)
            step.inc(nc.vector.reciprocal(keep["share"][:, 0, :], den[:]))
            step.wait(dve)
            step.inc(nc.vector.tensor_tensor(keep["share"][:, 1, :], ex[:], keep["share"][:, 0, :], ALU.mult))
            step.wait(dve)


def experts(nc, dram, keep):
    with ExitStack() as ctx:
        def sb(name, shape, dt):
            return ctx.enter_context(nc.sbuf_tensor(name, shape, dt))

        def psum(name, shape, dt):
            return ctx.enter_context(nc.psum_tensor(name, shape, dt))

        def sem(name):
            return ctx.enter_context(nc.semaphore(name))

        ident, mod_cols, w1, w2, b1, b2, owner = (
            keep[n] for n in ("ident", "mod_cols", "w1", "w2", "b1", "b2", "owner"))
        HALVES = FF * P // C
        x_tile = sb("ex_x_tile", [P, 2, D], F32)
        xT = sb("ex_xT", [P, KD, P], F32)
        h = sb("ex_h", [P, FF * P], F32)
        hT = sb("ex_hT", [P, FF, P], F32)
        y = sb("ex_y", [P, 2, D], F32)

        ps_x = psum("ex_ps_x", [P, C], F32)
        ps_h = [psum(f"ex_ps_h_{i}", [P, C], F32) for i in range(HALVES)]
        ps_hT = psum("ex_ps_hT", [P, FF, P], F32)
        ps_y = [psum(f"ex_ps_y_{u}", [P, C], F32) for u in range(2)]

        x_in = [sem(f"ex_x_in_{u}") for u in range(2)]
        w2_in = sem("ex_w2_in")
        x_turned = sem("ex_x_turned")
        xT_ready = sem("ex_xT_ready")
        hidden = [sem(f"ex_hidden_{i}") for i in range(HALVES)]
        h_copied = [sem(f"ex_h_copied_{i}") for i in range(HALVES)]
        h_turned = sem("ex_h_turned")
        rectified = sem("ex_rectified")
        out_done = sem("ex_out_done")
        y_ready = sem("ex_y_ready")
        y_stored = [sem(f"ex_y_stored_{u}") for u in range(2)]
        block = ctx.enter_context(nc.Block())

        def over_queue(eng, body, done=0):
            with eng.Fori(done, (TILES - 1) // 2) as it:
                for u in range(2):
                    body(it * 2 + (u + 1), (u + 1) % 2, it)

        @block.sync
        def _(sp):
            sp.sem_inc(x_turned, 2)

            def load(tile, u):
                sp.wait_ge(x_turned, tile + 1)
                row = sp.value_load(keep["row_of_tile"][0:1, bass.ds(tile, 1)], min_val=0, max_val=E * QROWS - P)
                sp.dma_start(x_tile[:, u, :], dram["queue"][bass.ds(row, P), :]).then_inc(x_in[u], 16)

            load(0, 0)
            load(1, 1)
            for e in range(E - 3, E):
                sp.dma_start(w2[:, e], dram["W2"][e].rearrange("(f p) d -> p f d", p=P)).then_inc(w2_in, 16)
            load(2, 0)
            over_queue(sp, lambda tile, u, it: load(tile, u), done=1)
            load(TILES, TILES % 2)
            sp.wait_ge(x_in[TILES % 2], 16 * ((TILES + 1) // 2))

        @block.gpsimd
        def _(pool):
            def store(tile, u):
                pool.wait_ge(y_ready, tile + 3)
                pool.dma_start(dram["answers"][bass.ds(tile * P, P), :], y[:, u, :]).then_inc(y_stored[u], 16)

            store(0, 0)
            over_queue(pool, lambda tile, u, it: store(tile, u))
            for u in range(2):
                pool.wait_ge(y_stored[u], 16 * ((TILES + 1 - u) // 2))

        @block.tensor
        def _(pe):
            def turn_rows(tile, u, loads):
                pe.wait_ge(x_in[u], loads * 16)
                pe.wait_ge(xT_ready, tile + 1)
                for k in range(KD):
                    ins = nc.tensor.transpose(ps_x[:, k * P:(k + 1) * P], x_tile[:, u, k * P:(k + 1) * P], ident[:])
                ins.then_inc(x_turned, 1)

            def first_layer(tile):
                e = pe.value_load(owner[0:1, bass.ds(tile, 1)], min_val=0, max_val=E - 1)
                pe.wait_ge(xT_ready, tile + 2)
                for i in range(HALVES):
                    pe.wait_ge(h_copied[i], tile + 1)
                    for k in range(KD):
                        ins = nc.tensor.matmul(ps_h[i][:], xT[:, k, :],
                                               w1[:, bass.ds(e, 1), k, i * C:(i + 1) * C].rearrange(
                                                   "p a f -> p (a f)"), start=k == 0, stop=k == KD - 1)
                    ins.then_inc(hidden[i], 1)
                return e

            def turn_hidden(tile):
                for i in range(HALVES):
                    pe.wait_ge(h_copied[i], tile + 2)
                pe.wait_ge(rectified, tile * FF + FF)
                for f in range(FF):
                    ins = nc.tensor.transpose(ps_hT[:, f, :], h[:, f * P:(f + 1) * P], ident[:])
                ins.then_inc(h_turned, 1)

            def second_layer(tile, u):
                e = pe.value_load(owner[0:1, bass.ds(tile, 1)], min_val=0, max_val=E - 1)
                pe.wait_ge(rectified, tile * FF + 2 * FF)
                pe.wait_ge(y_ready, tile + 1)
                for f in range(FF):
                    ins = nc.tensor.matmul(ps_y[u][:, 0:D], hT[:, f, :],
                                           w2[:, bass.ds(e, 1), f, :].rearrange("p a d -> p (a d)"),
                                           start=f == 0, stop=f == FF - 1)
                ins.then_inc(out_done, 1)

            pe.wait_ge(keep["weights_in"], 16 * (1 + NC + E - 3))
            turn_rows(0, 0, 1)
            first_layer(0)
            pe.wait_ge(w2_in, 16 * 3)
            turn_rows(1, 1, 1)
            turn_hidden(0)

            def tile_steps(tile, u, it):
                first_layer(tile)
                second_layer(tile - 1, 1 - u)
                turn_rows(tile + 1, 1 - u, it + 2)
                turn_hidden(tile)

            over_queue(pe, tile_steps)
            second_layer(TILES - 1, (TILES - 1) % 2)

        @block.scalar
        def _(act):
            act.sem_inc(h_copied[0], 1)
            act.sem_inc(rectified, FF)

            def tile_steps(tile):
                e = act.value_load(owner[0:1, bass.ds(tile, 1)], min_val=0, max_val=E - 1)
                act.wait_ge(hidden[0], tile + 1)
                nc.scalar.copy(h[:, 0:C], ps_h[0][:]).then_inc(h_copied[0], 1)
                act.wait_ge(h_turned, tile + 1)
                for f in range(FF):
                    nc.scalar.activation(hT[:, f, :], ps_hT[:, f, :], ACT.Relu,
                                         bias=b1[:, bass.ds(e * FF + f, 1)]).then_inc(rectified, 1)

            tile_steps(0)
            over_queue(act, lambda tile, u, it: tile_steps(tile))

        @block.vector
        def _(dve):
            dve.sem_inc(h_copied[1], 1)
            dve.sem_inc(xT_ready, 1)
            dve.sem_inc(y_ready, 2)

            def modulate(tile):
                dve.wait_ge(x_turned, tile + 3)
                for k in range(KD):
                    ins = nc.vector.tensor_scalar(xT[:, k, :], ps_x[:, k * P:(k + 1) * P], mod_cols[:, 6 + k:7 + k],
                                                  mod_cols[:, 4 + k:5 + k], ALU.mult, ALU.add)
                ins.then_inc(xT_ready, 1)

            def copy_hidden(tile):
                dve.wait_ge(hidden[1], tile + 1)
                nc.vector.tensor_copy(h[:, C:2 * C], ps_h[1][:]).then_inc(h_copied[1], 1)

            def answer(tile, u, stores):
                e = dve.value_load(owner[0:1, bass.ds(tile, 1)], min_val=0, max_val=E - 1)
                dve.wait_ge(out_done, tile + 1)
                if not isinstance(stores, int) or stores > 0:
                    dve.wait_ge(y_stored[u], stores * 16)
                nc.vector.tensor_tensor(y[:, u, :], ps_y[u][:, 0:D],
                                        b2[:, bass.ds(e, 1), :].rearrange("p a d -> p (a d)"),
                                        ALU.add).then_inc(y_ready, 1)

            modulate(0)
            copy_hidden(0)
            modulate(1)

            def tile_steps(tile, u, it):
                copy_hidden(tile)
                answer(tile - 1, 1 - u, it)
                modulate(tile + 1)

            for tile in (1, 2):
                tile_steps(tile, tile % 2, 0)
            over_queue(dve, tile_steps, done=1)
            answer(TILES - 1, (TILES - 1) % 2, (TILES - 1) // 2)


def combine(nc, dram, keep):
    with ExitStack() as ctx:
        def sb(name, shape, dt):
            return ctx.enter_context(nc.sbuf_tensor(name, shape, dt))

        def sem(name):
            return ctx.enter_context(nc.semaphore(name))

        RING = 8
        share, gates, mixed = keep["share"], keep["gates"], keep["mixed"]
        answer = [sb(f"co_answer_{i}", [P, RING, D], F32) for i in range(2)]
        fetched = [sem(f"co_fetched_{r}") for r in range(RING)]
        stored = [sem(f"co_stored_{r}") for r in range(RING)]
        dve_step = sem("co_dve_step")
        summed = sem("co_summed")
        out_v = dram["out"].rearrange("a (t p) d -> p (a t) d", p=P)
        block = ctx.enter_context(nc.Block())

        @block.gpsimd
        def _(pool):
            for t in range(NT):
                if t >= RING:
                    pool.wait_ge(stored[t % RING], 16 * (t // RING))
                for i in range(2):
                    pool.indirect_dma_start(answer[i][:, t % RING, :], None, dram["answers"],
                                            bass.IndirectOffsetOnAxis(ap=keep["slots"][:, 2 * t + i:2 * t + i + 1],
                                                                      axis=0)).then_inc(fetched[t % RING], 16)

        @block.sync
        def _(sp):
            with sp.Fori(0, NT // RING) as it:
                for r in range(RING):
                    sp.wait_ge(summed, it * RING + (r + 1))
                    sp.dma_start(out_v[:, bass.ds(it * RING + r, 1), :], answer[1][:, r:r + 1, :]
                                 ).then_inc(stored[r], 16)
            for r in range(RING):
                sp.wait_ge(stored[r], 16 * (NT // RING))

        @block.vector
        def _(dve):
            STEPS = 3
            with dve.Fori(0, NT // RING) as it:
                for r in range(RING):
                    t = it * RING + r
                    step = Tally(dve_step, t * STEPS)
                    dve.wait_ge(fetched[r], it * 32 + 32)
                    first, second = answer[0][:, r, :], answer[1][:, r, :]
                    step.inc(nc.vector.tensor_scalar(first, first, share[:, 0, bass.ds(t, 1)], None, ALU.mult))
                    step.wait(dve)
                    step.inc(nc.vector.scalar_tensor_tensor(out=second, in0=second,
                                                            scalar=share[:, 1, bass.ds(t, 1)], in1=first,
                                                            op0=ALU.mult, op1=ALU.add))
                    step.wait(dve)
                    step.inc(nc.vector.tensor_tensor(second, second, gates[:, 1, :], ALU.mult))
                    step.wait(dve)
                    nc.vector.tensor_tensor(second, second,
                                            mixed[:, bass.ds(t, 1), :].rearrange("p a d -> p (a d)"),
                                            ALU.add).then_inc(summed, 1)
                    assert step.n == STEPS


def adaln_attention_experts(nc, dram):
    for name in ("k_parts", "q_parts"):
        dram[name] = nc.dram_tensor(name, (PARTS + STACK - ROWS, H, S), BF16).ap()
    for name, rows in (("queue", E * QROWS), ("answers", TILES * P)):
        dram[name] = nc.dram_tensor(name, (rows, D), F32).ap()
    with ExitStack() as outer:
        def kept(ctx, name, shape, dt):
            keep[name] = ctx.enter_context(nc.sbuf_tensor("kept_" + name, shape, dt))

        keep = {"weights_in": outer.enter_context(nc.semaphore("weights_in"))}
        kept(outer, "ident", [P, P], F32)
        kept(outer, "gates", [P, 2, D], F32)
        kept(outer, "mod_cols", [P, 8], F32)
        kept(outer, "mixed", [P, NT, D], F32)
        with ExitStack() as inner:
            kept(inner, "ident_bf", [P, P], BF16)
            kept(inner, "mask_kq", [P, P], BF16)
            kept(inner, "mask_qk", [P, P], BF16)
            keep["k_in"] = inner.enter_context(nc.semaphore("k_in"))
            kept(inner, "too_wide", [1, 1], I32)
            kept(inner, "v", [P, NT, D], F32)
            attention_inputs(nc, dram, keep)
            kept(inner, "k_rows", [STACK, 2 * GH * S], BF16)
            score_shifts(nc, dram, keep)
            row_maxima(nc, dram, keep)
            attention(nc, dram, keep)
        kept(outer, "w1", [P, E, KD, FF * P], F32)
        kept(outer, "w2", [P, E, FF, D], F32)
        kept(outer, "b1", [P, E * FF], F32)
        kept(outer, "b2", [P, E, D], F32)
        kept(outer, "slots", [P, 2 * NT], U32)
        kept(outer, "share", [P, 2, NT], F32)
        kept(outer, "owner", [1, TILES + 1], I32)
        kept(outer, "row_of_tile", [1, TILES + 1], I32)
        route(nc, dram, keep)
        experts(nc, dram, keep)
        combine(nc, dram, keep)


INPUTS = {
    "x": "L0_attn_x", "Wq": "L0_attn_Wq", "bq": "L0_attn_bq", "Wk": "L0_attn_Wk", "bk": "L0_attn_bk",
    "Wv": "L0_attn_Wv", "bv": "L0_attn_bv", "Wo": "L0_attn_Wo", "bo": "L0_attn_bo",
    "gate_w": "L0_ffn_gate_w", "gate_b": "L0_ffn_gate_b", "W1": "L0_ffn_W1", "b1": "L0_ffn_b1",
    "W2": "L0_ffn_W2", "b2": "L0_ffn_b2", "c": "L0_c", "wmod": "L0_wmod",
}


def kernel(**inputs):
    import numpy as _np
    import concourse.bacc as _bacc
    from concourse.bass_utils import run_bass_kernel_spmd as _run

    nc = _bacc.Bacc("TRN2", target_bir_lowering=False, num_devices=1)
    arrays, dram = {}, {}
    for name, given in INPUTS.items():
        a = _np.ascontiguousarray(inputs[given])
        arrays[f"in_{name}"] = a
        dram[name] = nc.dram_tensor(f"in_{name}", a.shape, mybir.dt.from_np(a.dtype), kind="ExternalInput").ap()
    dram["out"] = nc.dram_tensor("out", (1, S, D), F32, kind="ExternalOutput").ap()
    adaln_attention_experts(nc, dram)
    return _run(nc, [arrays], core_ids=[0]).results[0]["out"]
```
